# Optimizing a Trainium2 kernel written in Bass

```python
import numpy as np
import jax
import jax.numpy as jnp

def _softmax(x, axis=-1):
    return jax.nn.softmax(x, axis=axis)

def _gelu(x):
    return jax.nn.gelu(x, approximate=True)

def _silu(x):
    return jax.nn.silu(x)

def _sigmoid(x):
    return jax.nn.sigmoid(x)

def _layernorm(x, axis=-1, eps=1e-05):
    m = jnp.mean(x, axis=axis, keepdims=True)
    v = jnp.var(x, axis=axis, keepdims=True)
    return (x - m) / jnp.sqrt(v + eps)

def _scatter_add(tgt, idx, src, axis=0):
    return tgt.at[idx].add(src)

def _segment_sum(src, seg, n):
    return jax.ops.segment_sum(src, seg, n)
kernel_name = 'mk_metaformer_d4_conv_nchw256_r4_b543c5'

def setup_inputs(seed: int=0):
    np.random.seed(seed)
    _w = jnp.asarray

    def _rec_inputs():
        import jax
        import jax.numpy as jnp
        _gk = jax.random.key(seed)
        x = -0.000125 + 0.9999 * jax.random.normal(jax.random.fold_in(_gk, 1), (8, 64, 32, 32), jnp.float32)
        return x
    x = _rec_inputs()

    def _L0_conv_setup():
        import jax, jax.numpy as jnp
        import numpy as np
        B, C, H, W = (8, 64, 32, 32)
        KC, VC, HEADS = (64, 64, 2)
        HK, HV = (KC // HEADS, VC // HEADS)
        EPS = 1e-05
        key = jax.random.key(seed)
        ks = jax.random.split(key, 10)
        s = 0.02
        return {'x': jax.random.normal(ks[0], (B, C, H, W), jnp.float32), 'bn_gamma': jnp.ones((C,), jnp.float32), 'bn_beta': jnp.zeros((C,), jnp.float32), 'wk': jax.random.normal(ks[1], (KC, C), jnp.float32) * s, 'bk': jnp.zeros((KC,), jnp.float32), 'wq': jax.random.normal(ks[2], (KC, C), jnp.float32) * s, 'bq': jnp.zeros((KC,), jnp.float32), 'wv': jax.random.normal(ks[3], (VC, C), jnp.float32) * s, 'bv': jnp.zeros((VC,), jnp.float32), 'w_fc1': jax.random.normal(ks[4], (HEADS, HEADS), jnp.float32) * 0.5, 'b_fc1': jnp.zeros((HEADS,), jnp.float32), 'w_fc2': jax.random.normal(ks[5], (HEADS, HEADS), jnp.float32) * 0.5, 'b_fc2': jnp.zeros((HEADS,), jnp.float32), 'w_se': jax.random.normal(ks[6], (HEADS,), jnp.float32) * 0.5, 'b_se': jnp.zeros((), jnp.float32), 'w_rep': jax.random.normal(ks[7], (C, C), jnp.float32) * s, 'b_rep': jnp.zeros((C,), jnp.float32)}
    _L0_conv_all = _L0_conv_setup()
    _L0_conv_in = {k: v for k, v in _L0_conv_all.items() if k in ('bn_gamma', 'bn_beta', 'wk', 'bk', 'wq', 'bq', 'wv', 'bv', 'w_fc1', 'b_fc1', 'w_fc2', 'b_fc2', 'w_se', 'b_se', 'w_rep', 'b_rep')}
    del _L0_conv_all

    def _L0_ffn_setup():
        import jax, jax.numpy as jnp
        import numpy as np
        D_MODEL = 64
        N_EXPERTS = 16
        HIDDEN = 128
        SCALE = 0.02
        key = jax.random.key(seed)
        ks = jax.random.split(key, 5)
        x = jax.random.normal(ks[0], (4, 2048, D_MODEL), dtype=jnp.float32)
        gate_w = jax.random.normal(ks[1], (D_MODEL, N_EXPERTS), dtype=jnp.float32) * SCALE
        gate_b = jnp.zeros((N_EXPERTS,), dtype=jnp.float32)
        w1 = jax.random.normal(ks[2], (N_EXPERTS, D_MODEL, HIDDEN), dtype=jnp.float32) * SCALE
        w2 = jax.random.normal(ks[3], (N_EXPERTS, D_MODEL, HIDDEN), dtype=jnp.float32) * SCALE
        w3 = jax.random.normal(ks[4], (N_EXPERTS, HIDDEN, D_MODEL), dtype=jnp.float32) * SCALE
        return {'x': x, 'gate_w': gate_w, 'gate_b': gate_b, 'w1': w1, 'w2': w2, 'w3': w3}
    _L0_ffn_all = _L0_ffn_setup()
    _L0_ffn_in = {k: v for k, v in _L0_ffn_all.items() if k in ('gate_w', 'gate_b', 'w1', 'w2', 'w3')}
    del _L0_ffn_all

    def _L1_conv_setup():
        import jax, jax.numpy as jnp
        import numpy as np
        B, C_IN, C_OUT, H, W = (16, 64, 64, 16, 16)
        K_EXP, KS, RED, POOL = (8, 3, 16, 4)
        STRIDE, PAD = (1, 1)

        def _routing(x, w1, w2, w_exp):
            b, c, h, w = x.shape
            gap = x.mean((2, 3))
            cw = jnp.maximum(gap @ w1.T, 0.0) @ w2.T
            pooled = x.reshape(b, c, POOL, h // POOL, POOL, w // POOL).mean((3, 5))
            cp = pooled.mean(1).reshape(b, POOL * POOL)
            ew = cp @ w_exp.T
            return jax.nn.sigmoid(cw[:, :, None] * ew[:, None, :])
        key = jax.random.key(seed)
        ks = jax.random.split(key, 5)
        red_ch = max(C_IN // RED, RED)
        s = 0.05
        return {'x': jax.random.normal(ks[0], (B, C_IN, H, W), jnp.float32), 'w1': jax.random.normal(ks[1], (red_ch, C_IN), jnp.float32) * s, 'w2': jax.random.normal(ks[2], (C_IN, red_ch), jnp.float32) * s, 'w_exp': jax.random.normal(ks[3], (K_EXP, POOL * POOL), jnp.float32) * s, 'weight': jax.random.normal(ks[4], (K_EXP, C_OUT, C_IN, KS, KS), jnp.float32) * s}
    _L1_conv_all = _L1_conv_setup()
    _L1_conv_in = {k: v for k, v in _L1_conv_all.items() if k in ('w1', 'w2', 'w_exp', 'weight')}
    del _L1_conv_all

    def _L1_ffn_setup():
        import jax, jax.numpy as jnp
        import numpy as np
        TOP_K = 2
        key = jax.random.key(seed)
        ks = jax.random.split(key, 4)
        B, L, D, H, E = (8, 1024, 64, 256, 8)
        s = 0.02
        return {'x': jax.random.normal(ks[0], (B, L, D), jnp.float32), 'Wg': jax.random.normal(ks[1], (D, E), jnp.float32) * s, 'bg': jnp.zeros((E,), jnp.float32), 'W1': jax.random.normal(ks[2], (E, D, H), jnp.float32) * s, 'b1': jnp.zeros((E, H), jnp.float32), 'W2': jax.random.normal(ks[3], (E, H, D), jnp.float32) * s, 'b2': jnp.zeros((E, D), jnp.float32)}
    _L1_ffn_all = _L1_ffn_setup()
    _L1_ffn_in = {k: v for k, v in _L1_ffn_all.items() if k in ('Wg', 'bg', 'W1', 'b1', 'W2', 'b2')}
    del _L1_ffn_all

    def _L2_conv_setup():
        import jax, jax.numpy as jnp
        import numpy as np
        K = 5
        C = 64
        M = 4
        CM = C // M
        PLANES = 64

        def _depthwise_per_sample(f, w, b, dilation, pad):
            N, Cm, H, W = f.shape
            x = f.reshape(1, N * Cm, H, W)
            wk = w.reshape(N * Cm, 1, w.shape[2], w.shape[3])
            out = jax.lax.conv_general_dilated(x, wk, window_strides=(1, 1), padding=[(pad, pad), (pad, pad)], rhs_dilation=(dilation, dilation), feature_group_count=N * Cm, dimension_numbers=('NCHW', 'OIHW', 'NCHW'))
            return out.reshape(N, Cm, H, W) + b[None, :, None, None]
        key = jax.random.key(seed)
        ks = jax.random.split(key, 16)
        N, H, W = (16, 24, 24)
        s = 0.05
        return {'x': jax.random.normal(ks[0], (N, C, H, W), jnp.float32), 'conv_w': jax.random.normal(ks[1], (CM, C)) * s, 'conv_b': jax.random.normal(ks[2], (CM,)) * s, 'conv_k_w': jax.random.normal(ks[3], ()) * s + 1.0, 'conv_k_b': jax.random.normal(ks[4], ()) * s, 'conv_k2_w': jax.random.normal(ks[5], ()) * s + 1.0, 'conv_k2_b': jax.random.normal(ks[6], ()) * s, 'conv_kernel_w': jax.random.normal(ks[7], (K * K,)) * s, 'conv_kernel_b': jax.random.normal(ks[8], (K * K,)) * s, 'conv_kernel2_w': jax.random.normal(ks[9], (9,)) * s, 'conv_kernel2_b': jax.random.normal(ks[10], (9,)) * s, 'fuse_w': jax.random.normal(ks[11], (PLANES // 2, CM)) * s, 'fuse_b': jax.random.normal(ks[12], (PLANES // 2,)) * s, 'adap_b': jax.random.normal(ks[13], (CM,)) * s, 'atrous_b': jax.random.normal(ks[14], (CM,)) * s}
    _L2_conv_all = _L2_conv_setup()
    _L2_conv_in = {k: v for k, v in _L2_conv_all.items() if k in ('conv_w', 'conv_b', 'conv_k_w', 'conv_k_b', 'conv_k2_w', 'conv_k2_b', 'conv_kernel_w', 'conv_kernel_b', 'conv_kernel2_w', 'conv_kernel2_b', 'fuse_w', 'fuse_b', 'adap_b', 'atrous_b')}
    del _L2_conv_all

    def _L2_ffn_setup():
        import jax, jax.numpy as jnp
        import numpy as np
        TOP_K = 2
        key = jax.random.key(seed)
        ks = jax.random.split(key, 4)
        B, L, D, H, E = (8, 1024, 64, 256, 8)
        s = 0.02
        return {'x': jax.random.normal(ks[0], (B, L, D), jnp.float32), 'Wg': jax.random.normal(ks[1], (D, E), jnp.float32) * s, 'bg': jnp.zeros((E,), jnp.float32), 'W1': jax.random.normal(ks[2], (E, D, H), jnp.float32) * s, 'b1': jnp.zeros((E, H), jnp.float32), 'W2': jax.random.normal(ks[3], (E, H, D), jnp.float32) * s, 'b2': jnp.zeros((E, D), jnp.float32)}
    _L2_ffn_all = _L2_ffn_setup()
    _L2_ffn_in = {k: v for k, v in _L2_ffn_all.items() if k in ('Wg', 'bg', 'W1', 'b1', 'W2', 'b2')}
    del _L2_ffn_all

    def _L3_conv_setup():
        import jax, jax.numpy as jnp
        import numpy as np
        from jax import lax
        B, CIN, COUT, H, W = (4, 64, 64, 16, 16)
        KH = KW = 3
        K = KH * KW
        GN_GROUPS = 32
        EPS = 1e-05

        def _deform_conv(x, offset, weight):
            b, c, h, w = x.shape
            off = offset.reshape(b, K, 2, h, w)
            ky, kx = jnp.meshgrid(jnp.arange(KH), jnp.arange(KW), indexing='ij')
            base_y = (jnp.arange(h, dtype=jnp.float32) - 1.0)[None, :, None] + ky.reshape(K).astype(jnp.float32)[:, None, None]
            base_x = (jnp.arange(w, dtype=jnp.float32) - 1.0)[None, None, :] + kx.reshape(K).astype(jnp.float32)[:, None, None]
            py = base_y[None] + off[:, :, 0]
            px = base_x[None] + off[:, :, 1]
            y0 = jnp.floor(py)
            x0 = jnp.floor(px)
            ty = py - y0
            tx = px - x0
            y0 = y0.astype(jnp.int32)
            x0 = x0.astype(jnp.int32)
            x_hw = x.transpose(0, 2, 3, 1).reshape(b, h * w, c)

            def corner(yi, xi, wgt):
                valid = (yi >= 0) & (yi < h) & (xi >= 0) & (xi < w)
                yc = jnp.clip(yi, 0, h - 1)
                xc = jnp.clip(xi, 0, w - 1)
                idx = (yc * w + xc).reshape(b, K * h * w)
                v = jnp.take_along_axis(x_hw, idx[..., None], axis=1)
                return v * (wgt * valid.astype(wgt.dtype)).reshape(b, K * h * w, 1)
            samp = corner(y0, x0, (1 - ty) * (1 - tx)) + corner(y0, x0 + 1, (1 - ty) * tx) + corner(y0 + 1, x0, ty * (1 - tx)) + corner(y0 + 1, x0 + 1, ty * tx)
            samp = samp.reshape(b, K, h, w, c)
            return jnp.einsum('bkhwc,ock->bohw', samp, weight.reshape(weight.shape[0], c, K))
        key = jax.random.key(seed)
        ks = jax.random.split(key, 6)
        x = jax.random.normal(ks[0], (B, CIN, H, W), jnp.float32)
        offset_w = jax.random.normal(ks[1], (2 * K, CIN, KH, KW), jnp.float32) * 0.01
        offset_b = jax.random.normal(ks[2], (2 * K,), jnp.float32) * 0.01
        deform_w = jax.random.normal(ks[3], (COUT, CIN, KH, KW), jnp.float32) * (1.0 / np.sqrt(CIN * K))
        gn_gamma = jnp.ones((COUT,), jnp.float32)
        gn_beta = jnp.zeros((COUT,), jnp.float32)
        return {'x': x, 'offset_w': offset_w, 'offset_b': offset_b, 'deform_w': deform_w, 'gn_gamma': gn_gamma, 'gn_beta': gn_beta}
    _L3_conv_all = _L3_conv_setup()
    _L3_conv_in = {k: v for k, v in _L3_conv_all.items() if k in ('offset_w', 'offset_b', 'deform_w', 'gn_gamma', 'gn_beta')}
    del _L3_conv_all

    def _L3_ffn_setup():
        import jax, jax.numpy as jnp
        import numpy as np
        D_MODEL = 64
        N_EXPERTS = 16
        HIDDEN = 128
        SCALE = 0.02
        key = jax.random.key(seed)
        ks = jax.random.split(key, 5)
        x = jax.random.normal(ks[0], (4, 2048, D_MODEL), dtype=jnp.float32)
        gate_w = jax.random.normal(ks[1], (D_MODEL, N_EXPERTS), dtype=jnp.float32) * SCALE
        gate_b = jnp.zeros((N_EXPERTS,), dtype=jnp.float32)
        w1 = jax.random.normal(ks[2], (N_EXPERTS, D_MODEL, HIDDEN), dtype=jnp.float32) * SCALE
        w2 = jax.random.normal(ks[3], (N_EXPERTS, D_MODEL, HIDDEN), dtype=jnp.float32) * SCALE
        w3 = jax.random.normal(ks[4], (N_EXPERTS, HIDDEN, D_MODEL), dtype=jnp.float32) * SCALE
        return {'x': x, 'gate_w': gate_w, 'gate_b': gate_b, 'w1': w1, 'w2': w2, 'w3': w3}
    _L3_ffn_all = _L3_ffn_setup()
    _L3_ffn_in = {k: v for k, v in _L3_ffn_all.items() if k in ('gate_w', 'gate_b', 'w1', 'w2', 'w3')}
    del _L3_ffn_all
    return {'x': x, 'L0_conv_bn_gamma': _L0_conv_in['bn_gamma'], 'L0_conv_bn_beta': _L0_conv_in['bn_beta'], 'L0_conv_wk': _L0_conv_in['wk'], 'L0_conv_bk': _L0_conv_in['bk'], 'L0_conv_wq': _L0_conv_in['wq'], 'L0_conv_bq': _L0_conv_in['bq'], 'L0_conv_wv': _L0_conv_in['wv'], 'L0_conv_bv': _L0_conv_in['bv'], 'L0_conv_w_fc1': _L0_conv_in['w_fc1'], 'L0_conv_b_fc1': _L0_conv_in['b_fc1'], 'L0_conv_w_fc2': _L0_conv_in['w_fc2'], 'L0_conv_b_fc2': _L0_conv_in['b_fc2'], 'L0_conv_w_se': _L0_conv_in['w_se'], 'L0_conv_b_se': _L0_conv_in['b_se'], 'L0_conv_w_rep': _L0_conv_in['w_rep'], 'L0_conv_b_rep': _L0_conv_in['b_rep'], 'L0_ffn_gate_w': _L0_ffn_in['gate_w'], 'L0_ffn_gate_b': _L0_ffn_in['gate_b'], 'L0_ffn_w1': _L0_ffn_in['w1'], 'L0_ffn_w2': _L0_ffn_in['w2'], 'L0_ffn_w3': _L0_ffn_in['w3'], 'L1_conv_w1': _L1_conv_in['w1'], 'L1_conv_w2': _L1_conv_in['w2'], 'L1_conv_w_exp': _L1_conv_in['w_exp'], 'L1_conv_weight': _L1_conv_in['weight'], 'L1_ffn_Wg': _L1_ffn_in['Wg'], 'L1_ffn_bg': _L1_ffn_in['bg'], 'L1_ffn_W1': _L1_ffn_in['W1'], 'L1_ffn_b1': _L1_ffn_in['b1'], 'L1_ffn_W2': _L1_ffn_in['W2'], 'L1_ffn_b2': _L1_ffn_in['b2'], 'L2_conv_conv_w': _L2_conv_in['conv_w'], 'L2_conv_conv_b': _L2_conv_in['conv_b'], 'L2_conv_conv_k_w': _L2_conv_in['conv_k_w'], 'L2_conv_conv_k_b': _L2_conv_in['conv_k_b'], 'L2_conv_conv_k2_w': _L2_conv_in['conv_k2_w'], 'L2_conv_conv_k2_b': _L2_conv_in['conv_k2_b'], 'L2_conv_conv_kernel_w': _L2_conv_in['conv_kernel_w'], 'L2_conv_conv_kernel_b': _L2_conv_in['conv_kernel_b'], 'L2_conv_conv_kernel2_w': _L2_conv_in['conv_kernel2_w'], 'L2_conv_conv_kernel2_b': _L2_conv_in['conv_kernel2_b'], 'L2_conv_fuse_w': _L2_conv_in['fuse_w'], 'L2_conv_fuse_b': _L2_conv_in['fuse_b'], 'L2_conv_adap_b': _L2_conv_in['adap_b'], 'L2_conv_atrous_b': _L2_conv_in['atrous_b'], 'L2_ffn_Wg': _L2_ffn_in['Wg'], 'L2_ffn_bg': _L2_ffn_in['bg'], 'L2_ffn_W1': _L2_ffn_in['W1'], 'L2_ffn_b1': _L2_ffn_in['b1'], 'L2_ffn_W2': _L2_ffn_in['W2'], 'L2_ffn_b2': _L2_ffn_in['b2'], 'L3_conv_offset_w': _L3_conv_in['offset_w'], 'L3_conv_offset_b': _L3_conv_in['offset_b'], 'L3_conv_deform_w': _L3_conv_in['deform_w'], 'L3_conv_gn_gamma': _L3_conv_in['gn_gamma'], 'L3_conv_gn_beta': _L3_conv_in['gn_beta'], 'L3_ffn_gate_w': _L3_ffn_in['gate_w'], 'L3_ffn_gate_b': _L3_ffn_in['gate_b'], 'L3_ffn_w1': _L3_ffn_in['w1'], 'L3_ffn_w2': _L3_ffn_in['w2'], 'L3_ffn_w3': _L3_ffn_in['w3']}

def reference(x, L0_conv_bn_gamma, L0_conv_bn_beta, L0_conv_wk, L0_conv_bk, L0_conv_wq, L0_conv_bq, L0_conv_wv, L0_conv_bv, L0_conv_w_fc1, L0_conv_b_fc1, L0_conv_w_fc2, L0_conv_b_fc2, L0_conv_w_se, L0_conv_b_se, L0_conv_w_rep, L0_conv_b_rep, L0_ffn_gate_w, L0_ffn_gate_b, L0_ffn_w1, L0_ffn_w2, L0_ffn_w3, L1_conv_w1, L1_conv_w2, L1_conv_w_exp, L1_conv_weight, L1_ffn_Wg, L1_ffn_bg, L1_ffn_W1, L1_ffn_b1, L1_ffn_W2, L1_ffn_b2, L2_conv_conv_w, L2_conv_conv_b, L2_conv_conv_k_w, L2_conv_conv_k_b, L2_conv_conv_k2_w, L2_conv_conv_k2_b, L2_conv_conv_kernel_w, L2_conv_conv_kernel_b, L2_conv_conv_kernel2_w, L2_conv_conv_kernel2_b, L2_conv_fuse_w, L2_conv_fuse_b, L2_conv_adap_b, L2_conv_atrous_b, L2_ffn_Wg, L2_ffn_bg, L2_ffn_W1, L2_ffn_b1, L2_ffn_W2, L2_ffn_b2, L3_conv_offset_w, L3_conv_offset_b, L3_conv_deform_w, L3_conv_gn_gamma, L3_conv_gn_beta, L3_ffn_gate_w, L3_ffn_gate_b, L3_ffn_w1, L3_ffn_w2, L3_ffn_w3):
    import jax
    import jax.numpy as jnp

    def _L0_conv_ref(x, bn_gamma, bn_beta, wk, bk, wq, bq, wv, bv, w_fc1, b_fc1, w_fc2, b_fc2, w_se, b_se, w_rep, b_rep):
        import jax, jax.numpy as jnp
        import numpy as np
        B, C, H, W = (8, 64, 32, 32)
        KC, VC, HEADS = (64, 64, 2)
        HK, HV = (KC // HEADS, VC // HEADS)
        EPS = 1e-05
        n, c, h, w = x.shape
        s = h * w
        mean = x.mean(axis=(0, 2, 3))
        var = x.var(axis=(0, 2, 3))
        xn = (x - mean[None, :, None, None]) * jax.lax.rsqrt(var + EPS)[None, :, None, None]
        xn = xn * bn_gamma[None, :, None, None] + bn_beta[None, :, None, None]
        xr = xn.reshape(n, c, s)
        k = jnp.einsum('oc,bcs->bos', wk, xr) + bk[None, :, None]
        q = jnp.einsum('oc,bcs->bos', wq, xr) + bq[None, :, None]
        v = jnp.einsum('oc,bcs->bos', wv, xr) + bv[None, :, None]
        k = jax.nn.softmax(k.reshape(n, HEADS, HK, s), axis=-1)
        q = jax.nn.softmax(q.reshape(n, HEADS, HK, s), axis=2)
        v = v.reshape(n, HEADS, HV, s)
        context = jnp.einsum('bnks,bnvs->bnkv', k, v)
        pooled = context.mean(axis=(2, 3))
        gate = jax.nn.sigmoid(jax.nn.relu(pooled @ w_fc1.T + b_fc1) @ w_fc2.T + b_fc2)
        gated = context * gate[:, :, None, None]
        ctx = jnp.einsum('n,bnkv->bkv', w_se, gated) + b_se
        out = jnp.einsum('bkv,bnks->bnvs', ctx, q).reshape(n, c, s)
        out = jnp.einsum('oc,bcs->bos', w_rep, out) + b_rep[None, :, None]
        return out.reshape(n, c, h, w)

    def _L0_ffn_ref(x, gate_w, gate_b, w1, w2, w3):
        import jax, jax.numpy as jnp
        import numpy as np
        D_MODEL = 64
        N_EXPERTS = 16
        HIDDEN = 128
        SCALE = 0.02
        n_experts = w1.shape[0]
        logits = jnp.einsum('bsd,de->bse', x, gate_w) + gate_b
        probs = jax.nn.softmax(logits, axis=-1)
        top_probs, top_idx = jax.lax.top_k(probs, 2)
        top_probs = top_probs / jnp.sum(top_probs, axis=-1, keepdims=True)
        dispatch = jnp.sum(jax.nn.one_hot(top_idx, n_experts, dtype=x.dtype) * top_probs[..., None], axis=-2)
        h1 = jnp.einsum('bsd,edh->bseh', x, w1)
        h2 = jnp.einsum('bsd,edh->bseh', x, w2)
        hidden = jax.nn.silu(h1) * h2
        expert_out = jnp.einsum('bseh,eho->bseo', hidden, w3)
        return jnp.einsum('bseo,bse->bso', expert_out, dispatch)

    def _L1_conv_ref(x, w1, w2, w_exp, weight):
        import jax, jax.numpy as jnp
        import numpy as np
        B, C_IN, C_OUT, H, W = (16, 64, 64, 16, 16)
        K_EXP, KS, RED, POOL = (8, 3, 16, 4)
        STRIDE, PAD = (1, 1)

        def _routing(x, w1, w2, w_exp):
            b, c, h, w = x.shape
            gap = x.mean((2, 3))
            cw = jnp.maximum(gap @ w1.T, 0.0) @ w2.T
            pooled = x.reshape(b, c, POOL, h // POOL, POOL, w // POOL).mean((3, 5))
            cp = pooled.mean(1).reshape(b, POOL * POOL)
            ew = cp @ w_exp.T
            return jax.nn.sigmoid(cw[:, :, None] * ew[:, None, :])
        routing = _routing(x, w1, w2, w_exp)
        combined = jnp.einsum('bik,koiuv->boiuv', routing, weight)

        def conv1(xi, wi):
            return jax.lax.conv_general_dilated(xi[None], wi, (STRIDE, STRIDE), [(PAD, PAD), (PAD, PAD)])[0]
        return jax.vmap(conv1)(x, combined)

    def _L1_ffn_ref(x, Wg, bg, W1, b1, W2, b2):
        import jax, jax.numpy as jnp
        import numpy as np
        TOP_K = 2
        B, L, D = x.shape
        E = W1.shape[0]
        xf = x.reshape(-1, D)
        gate_logits = xf @ Wg + bg
        top_w, top_i = jax.lax.top_k(gate_logits, TOP_K)
        top_w = jax.nn.softmax(top_w, axis=-1)
        w_dense = jnp.sum(jax.nn.one_hot(top_i, E, dtype=xf.dtype) * top_w[..., None], axis=1)
        out = jnp.zeros_like(xf)
        for e in range(E):
            h = jax.nn.gelu(xf @ W1[e] + b1[e], approximate=False)
            out = out + w_dense[:, e:e + 1] * (h @ W2[e] + b2[e])
        return out.reshape(B, L, D)

    def _L2_conv_ref(x, conv_w, conv_b, conv_k_w, conv_k_b, conv_k2_w, conv_k2_b, conv_kernel_w, conv_kernel_b, conv_kernel2_w, conv_kernel2_b, fuse_w, fuse_b, adap_b, atrous_b):
        import jax, jax.numpy as jnp
        import numpy as np
        K = 5
        C = 64
        M = 4
        CM = C // M
        PLANES = 64

        def _depthwise_per_sample(f, w, b, dilation, pad):
            N, Cm, H, W = f.shape
            x = f.reshape(1, N * Cm, H, W)
            wk = w.reshape(N * Cm, 1, w.shape[2], w.shape[3])
            out = jax.lax.conv_general_dilated(x, wk, window_strides=(1, 1), padding=[(pad, pad), (pad, pad)], rhs_dilation=(dilation, dilation), feature_group_count=N * Cm, dimension_numbers=('NCHW', 'OIHW', 'NCHW'))
            return out.reshape(N, Cm, H, W) + b[None, :, None, None]
        N = x.shape[0]
        f = jax.nn.relu(jnp.einsum('oc,nchw->nohw', conv_w, x) + conv_b[None, :, None, None])
        g = jax.nn.relu(x.mean(axis=(2, 3)) @ conv_w.T + conv_b)
        ker = conv_k_w * (g[:, :, None] * conv_kernel_w[None, None, :] + conv_kernel_b) + conv_k_b
        w_dyn = ker.reshape(N, CM, K, K)
        ker2 = conv_k2_w * (g[:, :, None] * conv_kernel2_w[None, None, :] + conv_kernel2_b) + conv_k2_b
        w_atr = ker2.reshape(N, CM, 3, 3)
        out = _depthwise_per_sample(f, w_dyn, adap_b, dilation=1, pad=(K - 1) // 2)
        out_atr = _depthwise_per_sample(f, w_atr, atrous_b, dilation=2, pad=2)
        y = jnp.einsum('oc,nchw->nohw', fuse_w, out) + fuse_b[None, :, None, None]
        y_atr = jnp.einsum('oc,nchw->nohw', fuse_w, out_atr) + fuse_b[None, :, None, None]
        return jnp.concatenate([y, y_atr], axis=1)

    def _L2_ffn_ref(x, Wg, bg, W1, b1, W2, b2):
        import jax, jax.numpy as jnp
        import numpy as np
        TOP_K = 2
        B, L, D = x.shape
        E = W1.shape[0]
        xf = x.reshape(-1, D)
        gate_logits = xf @ Wg + bg
        top_w, top_i = jax.lax.top_k(gate_logits, TOP_K)
        top_w = jax.nn.softmax(top_w, axis=-1)
        w_dense = jnp.sum(jax.nn.one_hot(top_i, E, dtype=xf.dtype) * top_w[..., None], axis=1)
        out = jnp.zeros_like(xf)
        for e in range(E):
            h = jax.nn.gelu(xf @ W1[e] + b1[e], approximate=False)
            out = out + w_dense[:, e:e + 1] * (h @ W2[e] + b2[e])
        return out.reshape(B, L, D)

    def _L3_conv_ref(x, offset_w, offset_b, deform_w, gn_gamma, gn_beta):
        import jax, jax.numpy as jnp
        import numpy as np
        from jax import lax
        B, CIN, COUT, H, W = (4, 64, 64, 16, 16)
        KH = KW = 3
        K = KH * KW
        GN_GROUPS = 32
        EPS = 1e-05

        def _deform_conv(x, offset, weight):
            b, c, h, w = x.shape
            off = offset.reshape(b, K, 2, h, w)
            ky, kx = jnp.meshgrid(jnp.arange(KH), jnp.arange(KW), indexing='ij')
            base_y = (jnp.arange(h, dtype=jnp.float32) - 1.0)[None, :, None] + ky.reshape(K).astype(jnp.float32)[:, None, None]
            base_x = (jnp.arange(w, dtype=jnp.float32) - 1.0)[None, None, :] + kx.reshape(K).astype(jnp.float32)[:, None, None]
            py = base_y[None] + off[:, :, 0]
            px = base_x[None] + off[:, :, 1]
            y0 = jnp.floor(py)
            x0 = jnp.floor(px)
            ty = py - y0
            tx = px - x0
            y0 = y0.astype(jnp.int32)
            x0 = x0.astype(jnp.int32)
            x_hw = x.transpose(0, 2, 3, 1).reshape(b, h * w, c)

            def corner(yi, xi, wgt):
                valid = (yi >= 0) & (yi < h) & (xi >= 0) & (xi < w)
                yc = jnp.clip(yi, 0, h - 1)
                xc = jnp.clip(xi, 0, w - 1)
                idx = (yc * w + xc).reshape(b, K * h * w)
                v = jnp.take_along_axis(x_hw, idx[..., None], axis=1)
                return v * (wgt * valid.astype(wgt.dtype)).reshape(b, K * h * w, 1)
            samp = corner(y0, x0, (1 - ty) * (1 - tx)) + corner(y0, x0 + 1, (1 - ty) * tx) + corner(y0 + 1, x0, ty * (1 - tx)) + corner(y0 + 1, x0 + 1, ty * tx)
            samp = samp.reshape(b, K, h, w, c)
            return jnp.einsum('bkhwc,ock->bohw', samp, weight.reshape(weight.shape[0], c, K))
        offset = lax.conv_general_dilated(x, offset_w, window_strides=(1, 1), padding=((1, 1), (1, 1)), dimension_numbers=('NCHW', 'OIHW', 'NCHW')) + offset_b[None, :, None, None]
        out = _deform_conv(x, offset, deform_w)
        b, c, h, w = out.shape
        g = out.reshape(b, GN_GROUPS, c // GN_GROUPS * h * w)
        mu = g.mean(axis=2, keepdims=True)
        var = g.var(axis=2, keepdims=True)
        g = (g - mu) * lax.rsqrt(var + EPS)
        out = g.reshape(b, c, h, w) * gn_gamma[None, :, None, None] + gn_beta[None, :, None, None]
        return jax.nn.relu(out)

    def _L3_ffn_ref(x, gate_w, gate_b, w1, w2, w3):
        import jax, jax.numpy as jnp
        import numpy as np
        D_MODEL = 64
        N_EXPERTS = 16
        HIDDEN = 128
        SCALE = 0.02
        n_experts = w1.shape[0]
        logits = jnp.einsum('bsd,de->bse', x, gate_w) + gate_b
        probs = jax.nn.softmax(logits, axis=-1)
        top_probs, top_idx = jax.lax.top_k(probs, 2)
        top_probs = top_probs / jnp.sum(top_probs, axis=-1, keepdims=True)
        dispatch = jnp.sum(jax.nn.one_hot(top_idx, n_experts, dtype=x.dtype) * top_probs[..., None], axis=-2)
        h1 = jnp.einsum('bsd,edh->bseh', x, w1)
        h2 = jnp.einsum('bsd,edh->bseh', x, w2)
        hidden = jax.nn.silu(h1) * h2
        expert_out = jnp.einsum('bseh,eho->bseo', hidden, w3)
        return jnp.einsum('bseo,bse->bso', expert_out, dispatch)

    def _gn(v, G=32, eps=1e-05):
        B_, C_, H_, W_ = v.shape
        g = v.reshape(B_, G, C_ // G, H_, W_)
        m = jnp.mean(g, axis=(2, 3, 4), keepdims=True)
        s = jnp.var(g, axis=(2, 3, 4), keepdims=True)
        return ((g - m) / jnp.sqrt(s + eps)).reshape(v.shape)

    def _ln_c(v, eps=1e-06):
        m = jnp.mean(v, axis=1, keepdims=True)
        s = jnp.var(v, axis=1, keepdims=True)
        return (v - m) / jnp.sqrt(s + eps)

    def _ln_t(v, eps=1e-05):
        m = jnp.mean(v, axis=-1, keepdims=True)
        s = jnp.var(v, axis=-1, keepdims=True)
        return (v - m) / jnp.sqrt(s + eps)

    def _to_tokens(v):
        B_, C_, H_, W_ = v.shape
        return v.reshape(B_, C_, H_ * W_).transpose(0, 2, 1)

    def _from_tokens(t, like):
        B_, C_, H_, W_ = like.shape
        return t.transpose(0, 2, 1).reshape(B_, C_, H_, W_)
    x = x + _L0_conv_ref(_ln_c(x), L0_conv_bn_gamma, L0_conv_bn_beta, L0_conv_wk, L0_conv_bk, L0_conv_wq, L0_conv_bq, L0_conv_wv, L0_conv_bv, L0_conv_w_fc1, L0_conv_b_fc1, L0_conv_w_fc2, L0_conv_b_fc2, L0_conv_w_se, L0_conv_b_se, L0_conv_w_rep, L0_conv_b_rep)
    t = _to_tokens(x)
    t = t + _L0_ffn_ref(_ln_t(t), L0_ffn_gate_w, L0_ffn_gate_b, L0_ffn_w1, L0_ffn_w2, L0_ffn_w3)
    x = _from_tokens(t, x)
    x = x + _L1_conv_ref(_ln_c(x), L1_conv_w1, L1_conv_w2, L1_conv_w_exp, L1_conv_weight)
    t = _to_tokens(x)
    t = t + _L1_ffn_ref(_ln_t(t), L1_ffn_Wg, L1_ffn_bg, L1_ffn_W1, L1_ffn_b1, L1_ffn_W2, L1_ffn_b2)
    x = _from_tokens(t, x)
    x = x + _L2_conv_ref(_ln_c(x), L2_conv_conv_w, L2_conv_conv_b, L2_conv_conv_k_w, L2_conv_conv_k_b, L2_conv_conv_k2_w, L2_conv_conv_k2_b, L2_conv_conv_kernel_w, L2_conv_conv_kernel_b, L2_conv_conv_kernel2_w, L2_conv_conv_kernel2_b, L2_conv_fuse_w, L2_conv_fuse_b, L2_conv_adap_b, L2_conv_atrous_b)
    t = _to_tokens(x)
    t = t + _L2_ffn_ref(_ln_t(t), L2_ffn_Wg, L2_ffn_bg, L2_ffn_W1, L2_ffn_b1, L2_ffn_W2, L2_ffn_b2)
    x = _from_tokens(t, x)
    x = x + _L3_conv_ref(_ln_c(x), L3_conv_offset_w, L3_conv_offset_b, L3_conv_deform_w, L3_conv_gn_gamma, L3_conv_gn_beta)
    t = _to_tokens(x)
    t = t + _L3_ffn_ref(_ln_t(t), L3_ffn_gate_w, L3_ffn_gate_b, L3_ffn_w1, L3_ffn_w2, L3_ffn_w3)
    x = _from_tokens(t, x)
    return x

_drawn_inputs = setup_inputs


def setup_inputs(seed=0):
    import zlib

    import numpy as np

    out = dict(_drawn_inputs(seed))
    spreads = {'L0_conv_bn_gamma': (1.0, 0.6),
     'L0_conv_bn_beta': (0.0, 0.8),
     'L0_conv_bk': (0.0, 2.0),
     'L0_conv_bq': (0.0, 0.8),
     'L0_conv_bv': (0.0, 0.8),
     'L0_conv_b_fc1': (0.0, 2.0),
     'L0_conv_b_fc2': (0.0, 2.0),
     'L0_conv_b_rep': (0.0, 0.384),
     'L0_ffn_gate_b': (0.0, 0.8),
     'L1_ffn_bg': (0.0, 0.1),
     'L1_ffn_b1': (0.0, 0.8),
     'L1_ffn_b2': (0.0, 0.776),
     'L2_ffn_bg': (0.0, 0.1),
     'L2_ffn_b1': (0.0, 0.8),
     'L2_ffn_b2': (0.0, 0.8),
     'L3_conv_gn_gamma': (1.0, 0.6),
     'L3_conv_gn_beta': (0.0, 0.8),
     'L3_ffn_gate_b': (0.0, 2.0)}
    factors = {'L0_conv_wk': 8.0,
     'L0_conv_wq': 8.0,
     'L0_conv_wv': 8.0,
     'L0_conv_w_fc1': 64.0,
     'L0_conv_w_fc2': 50.437,
     'L0_conv_w_se': 5.692,
     'L0_conv_w_rep': 7.21,
     'L0_ffn_gate_w': 8.0,
     'L0_ffn_w1': 8.0,
     'L0_ffn_w2': 8.0,
     'L0_ffn_w3': 8.0,
     'L1_ffn_W1': 5.47,
     'L1_ffn_W2': 4.642,
     'L2_conv_conv_w': 6.272,
     'L2_conv_conv_b': 22.229,
     'L2_conv_conv_kernel_w': 8.0,
     'L2_conv_conv_kernel_b': 28.892,
     'L2_conv_conv_kernel2_w': 8.0,
     'L2_conv_conv_kernel2_b': 32.03,
     'L2_conv_adap_b': 64.0,
     'L2_conv_atrous_b': 35.643,
     'L2_ffn_W1': 5.85,
     'L2_ffn_W2': 4.976,
     'L3_conv_offset_b': 55.383,
     'L3_ffn_gate_w': 8.0,
     'L3_ffn_w1': 8.0,
     'L3_ffn_w2': 8.0,
     'L3_ffn_w3': 8.0,
     'L2_conv_fuse_b': 8.0}
    for name, (base, spread) in spreads.items():
        noise = np.random.default_rng([zlib.crc32(name.encode()), seed]).standard_normal(out[name].shape)
        drawn = base * np.exp(spread * noise) if base else spread * noise
        out[name] = jnp.asarray(drawn.astype(out[name].dtype))
    for name, factor in factors.items():
        out[name] = (out[name] * factor).astype(out[name].dtype)
    return out
```

```python
from contextlib import ExitStack

import numpy as np

import concourse.bass as bass
from concourse import mybir

ALU = mybir.AluOpType
ACT = mybir.ActivationFunctionType
F32 = mybir.dt.float32
F32R = mybir.dt.float32r
AX = mybir.AxisListType

P = 128
B, C, H, W = 8, 64, 32, 32
HALVES = 2
IMAGES = B // HALVES
PIX = H * W
N = IMAGES * PIX
TILES = N // P
BANK = 512

HEADS = 2
HK = C // HEADS
CM = 16
class Mixture:
    def __init__(self, experts, hidden):
        self.experts, self.hidden = experts, hidden


SWIGLU = Mixture(experts=16, hidden=128)
GELU = Mixture(experts=8, hidden=256)
CHUNK = 256
CHUNKS = N // CHUNK
SLOTS = HALVES * CHUNK // P
LOWEST = -3.0e38
LN_TILES = 4


def spread(ap, axis, count):
    shape = list(ap.shape)
    shape.insert(axis, count)
    return ap.unsqueeze(axis).broadcast_to(shape)



def layer_norm(k, turn, eps):
    nc, x, xn = k.nc, k.x, k.xn
    WIDE = LN_TILES * P
    STEPS = N // WIDE
    ROWS = LN_TILES * HALVES
    t = turn * STEPS
    s = k.ln
    with ExitStack() as ctx:
        def sb(name, shape):
            return ctx.enter_context(nc.sbuf_tensor(f"ln{turn}_{name}", shape, F32))

        def ps(name, shape):
            return ctx.enter_context(nc.psum_tensor(f"ln{turn}_{name}", shape, F32))
        square = sb("square", [P, 2, WIDE])
        dev = sb("dev", [ROWS, 2, P])
        scale = sb("scale", [ROWS, 2, P])
        mean = ps("mean", [P, 2, WIDE])
        var = ps("var", [ROWS, 2, BANK])
        wide = ps("wide", [P, 2, WIDE])
        block = ctx.enter_context(nc.Block())

        def cols(i):
            return slice(i * WIDE, (i + 1) * WIDE)

        def staggered(*stages):
            for n in range(STEPS + len(stages) - 1):
                for behind, stage in enumerate(stages):
                    if 0 <= n - behind < STEPS:
                        stage(n - behind)

        @block.tensor
        def _(pe):
            def means(i):
                if i >= 2:
                    pe.wait_ge(s.centred, t + i - 1)
                pe.matmul(mean[:, i % 2, :], k.average[:], x[:, cols(i)],
                          start=True, stop=True).then_inc(s.mean, 1)

            def variances(i):
                pe.wait_ge(s.squared, t + i + 1)
                if i >= 2:
                    pe.wait_ge(s.dev, t + i - 1)
                for q in range(LN_TILES):
                    last = pe.matmul(var[:, i % 2, 0:P],
                                     k.shifted[:, ROWS - HALVES * (q + 1):2 * ROWS - HALVES * (q + 1)],
                                     square[:, i % 2, q * P:(q + 1) * P],
                                     start=(q == 0), stop=(q == LN_TILES - 1))
                last.then_inc(s.var, 1)

            def scales(i):
                pe.wait_ge(s.scale, t + i + 1)
                if i >= 2:
                    pe.wait_ge(s.normed, t + i - 1)
                for q in range(LN_TILES):
                    last = pe.matmul(wide[:, i % 2, q * P:(q + 1) * P], k.rows[:, q * P:(q + 1) * P],
                                     scale[:, i % 2, :], start=True, stop=True)
                last.then_inc(s.wide, 1)

            if turn == 0:
                pe.wait_ge(k.x_loaded, k.x_all)
            staggered(means, variances, scales)

        @block.scalar
        def _(act):
            def squares(i):
                act.wait_ge(s.centred, t + i + 1)
                if i >= 2:
                    act.wait_ge(s.var, t + i - 1)
                act.activation(square[:, i % 2, :], xn[:, cols(i)], ACT.Square).then_inc(s.squared, 1)

            def deviations(i):
                act.wait_ge(s.var, t + i + 1)
                if i >= 2:
                    act.wait_ge(s.scale, t + i - 1)
                act.activation(dev[:, i % 2, :], var[:, i % 2, 0:P], ACT.Sqrt,
                               bias=k.eps[eps][0:ROWS]).then_inc(s.dev, 1)

            staggered(squares, deviations)

        @block.vector
        def _(dve):
            def centre(i):
                dve.wait_ge(s.mean, t + i + 1)
                dve.tensor_tensor(xn[:, cols(i)], x[:, cols(i)], mean[:, i % 2, :],
                                  ALU.subtract).then_inc(s.centred, 1)

            def scales(i):
                dve.wait_ge(s.dev, t + i + 1)
                if i >= 2:
                    dve.wait_ge(s.wide, t + i - 1)
                dve.reciprocal(scale[:, i % 2, :], dev[:, i % 2, :]).then_inc(s.scale, 1)

            def norm(i):
                dve.wait_ge(s.wide, t + i + 1)
                dve.tensor_tensor(xn[:, cols(i)], xn[:, cols(i)], wide[:, i % 2, :],
                                  ALU.mult).then_inc(s.normed, 1)

            staggered(centre, scales, norm)



def gates(k, turn, m, w):
    nc, xn = k.nc, k.xn
    E = m.experts
    T = HALVES * TILES
    s = k.gt
    base = turn * 1
    WCOLS = w.first.shape[1]
    with ExitStack() as ctx:
        def sb(name, shape, dt=F32):
            return ctx.enter_context(nc.sbuf_tensor(f"gt{turn}_{name}", shape, dt))
        logits = sb("logits", [P, T, E])
        equal = sb("equal", [P, T, E])
        rank = sb("rank", [P, T, E])
        one_hot = [sb(f"one_hot{i}", [P, T, E]) for i in range(2)]
        best = [sb(f"best{i}", [P, T]) for i in range(2)]
        place = sb("place", [P, T])
        small = sb("small", [P, 4, T])
        raw = ctx.enter_context(nc.psum_tensor(f"gt{turn}_raw", [P, TILES, HALVES * E], F32))
        block = ctx.enter_context(nc.Block())
        gate = k.gate[:, 0:T * E].rearrange("p (t e) -> p t e", e=E)

        @block.tensor
        def _(pe):
            pe.wait_ge(w.loaded, w.all)
            for t in range(TILES):
                last = pe.matmul(raw[:, t, :], xn[:, t * P:(t + 1) * P], w.router[:],
                                 start=True, stop=True)
            last.then_inc(s.logits, 1)

        @block.scalar
        def _(act):
            act.wait_ge(w.loaded, w.all)
            for h in range(HALVES):
                act.copy(k.parts[h * C:(h + 1) * C, h, :], xn[h * C:(h + 1) * C, :]).then_inc(s.high, 1)
            act.copy(w.high[:, 0:WCOLS], w.first[:]).then_inc(s.w_high, 1)
            act.wait_ge(s.gap, base + 1)
            act.activation(small[:, 1, :], small[:, 0, :], ACT.Exp).then_inc(s.exp, 1)

        @block.gpsimd
        def _(pool):
            pool.wait_ge(s.w_high, base + 1)
            pool.tensor_tensor(w.low[:, 0:WCOLS], w.first[:], w.high[:, 0:WCOLS].bitcast(F32),
                               ALU.subtract)

        @block.vector
        def _(dve):
            step = [turn * 16]

            def done(ins):
                step[0] += 1
                ins.then_inc(s.step, 1)
                dve.wait_ge(s.step, step[0])

            dve.wait_ge(w.loaded, w.all)
            dve.wait_ge(s.logits, base + 1)
            done(dve.tensor_tensor(logits[:], raw[:].rearrange("p t (h e) -> p (t h) e", e=E),
                                   spread(w.router_bias[:], 1, T), ALU.add))
            for i in range(2):
                done(dve.tensor_reduce(best[i][:], logits[:], AX.X, ALU.max))
                done(dve.tensor_tensor(equal[:], logits[:], spread(best[i][:], 2, E), ALU.is_equal))
                done(dve.tensor_tensor(rank[:], equal[:], spread(k.countdown[:, 0:E], 1, T), ALU.mult))
                done(dve.tensor_reduce(place[:], rank[:], AX.X, ALU.max))
                done(dve.tensor_tensor(one_hot[i][:], rank[:], spread(place[:], 2, E), ALU.is_equal))
                if i == 0:
                    done(dve.scalar_tensor_tensor(out=logits[:], in0=one_hot[0][:], scalar=LOWEST,
                                                  in1=logits[:], op0=ALU.mult, op1=ALU.add))
            dve.tensor_tensor(small[:, 0, :], best[1][:], best[0][:], ALU.subtract).then_inc(s.gap, 1)
            for h in range(HALVES):
                dve.wait_ge(s.high, turn * HALVES + h + 1)
                dve.tensor_tensor(k.parts[(1 - h) * C:(2 - h) * C, h, :], xn[h * C:(h + 1) * C, :],
                                  k.parts[h * C:(h + 1) * C, h, :].bitcast(F32), ALU.subtract)
            dve.wait_ge(s.exp, base + 1)
            done(dve.tensor_scalar(small[:, 2, :], small[:, 1, :], 1.0, None, ALU.add))
            done(dve.reciprocal(small[:, 3, :], small[:, 2, :]))
            done(dve.tensor_tensor(small[:, 2, :], small[:, 1, :], small[:, 3, :], ALU.mult))
            dve.tensor_tensor(equal[:], one_hot[0][:], spread(small[:, 3, :], 2, E), ALU.mult)
            done(dve.tensor_tensor(rank[:], one_hot[1][:], spread(small[:, 2, :], 2, E), ALU.mult))
            dve.tensor_tensor(gate, equal[:], rank[:], ALU.add)
            assert step[0] == (turn + 1) * 16


def mixture(k, turn, m, w, swiglu):
    nc, x = k.nc, k.x
    E, HID = m.experts, m.hidden
    COLS = HALVES * CHUNK
    F = HID // P
    PAIRS = E // 2
    RING = 4
    s = k.mx
    eb, fb, hb, pb, cb = (k.mx_base[n] for n in ("expert", "first", "hidden", "pair", "chunk"))
    bb = k.mx_base["biased"]
    with ExitStack() as ctx:
        def sb(name, shape, dt=F32):
            return ctx.enter_context(nc.sbuf_tensor(f"mx{turn}_{name}", shape, dt))

        def ps(name, shape):
            return ctx.enter_context(nc.psum_tensor(f"mx{turn}_{name}", shape, F32))
        act_out = sb("act_out", [P, RING, F, COLS])
        hidden = sb("hidden", [P, RING, COLS]) if swiglu else act_out
        weighted = sb("weighted", [P, 2, 2, SLOTS, C])
        biased = None if swiglu else sb("biased", [P, 2, SLOTS, C])
        total = sb("total", [P, 2, SLOTS, C])
        summed = sb("summed", [P, SLOTS, C])
        first = ps("first", [P, 2, 2, COLS])
        second = ps("second", [P, 2, 2, SLOTS, C])
        back = ps("back", [P, CHUNK])
        gate = k.gate[:, 0:HALVES * TILES * E].rearrange("p (t e) -> p t e", e=E)
        block = ctx.enter_context(nc.Block())

        def hi(e, f):
            return w.high[:, (e * 2 + f) * P:(e * 2 + f + 1) * P]

        def lo(e, f):
            return w.low[:, (e * 2 + f) * P:(e * 2 + f + 1) * P]

        def w2(e, f):
            return w.second[:, (e * F + f) * C:(e * F + f + 1) * C]

        @block.tensor
        def _(pe):
            def first_layer(i, e):
                n = i * E + e
                tokens = k.parts[:, :, bass.ds(i * CHUNK, CHUNK)]
                for f in range(2):
                    if not (isinstance(n, int) and n < 2):
                        if f == 0 or not swiglu:
                            pe.wait_ge(s.act, fb + (n - 2) * (1 if swiglu else 2) + (1 if swiglu else f + 1))
                        else:
                            pe.wait_ge(s.hidden, hb + n - 1)
                    pe.matmul(first[:, e % 2, f, :], hi(e, f), tokens, start=True, stop=False)
                    pe.matmul(first[:, e % 2, f, :], lo(e, f), tokens,
                              start=False, stop=True).then_inc(s.first, 1)

            def second_layer(i, e):
                n = i * E + e
                if swiglu:
                    pe.wait_ge(s.hidden, hb + n + 1)
                else:
                    pe.wait_ge(s.act, fb + 2 * n + 2)
                pair = i * PAIRS + e // 2
                if e % 2 == 0 and not (isinstance(pair, int) and pair < 2):
                    pe.wait_ge(s.read if swiglu else s.biased, (pb if swiglu else bb) + pair - 1)
                for q in range(SLOTS):
                    h, t = q // (SLOTS // HALVES), q % (SLOTS // HALVES)
                    for f in range(F):
                        tile = hidden[:, e % RING, q * P:(q + 1) * P] if swiglu else \
                            hidden[:, e % RING, f, q * P:(q + 1) * P]
                        last = pe.matmul(second[:, (e // 2) % 2, e % 2, t * HALVES + h, :], tile,
                                         w2(e, f), start=(f == 0), stop=(f == F - 1))
                last.then_inc(s.second, 1)

            def turn_back(i):
                pe.wait_ge(s.summed, cb + i + 1)
                if not (isinstance(i, int) and i < 1):
                    pe.wait_ge(s.added, cb + i)
                for t in range(CHUNK // P):
                    last = pe.transpose(back[:, t * P:(t + 1) * P],
                                        summed[:, t * HALVES:(t + 1) * HALVES, :].rearrange("p h c -> p (h c)"),
                                        k.identity[:])
                last.then_inc(s.back, 1)

            def step(i, before):
                for e in range(E):
                    first_layer(i, e)
                    if e > 0:
                        second_layer(i, e - 1)
                    elif before is not None:
                        second_layer(before, E - 1)
                    if e == 3 and before is not None:
                        turn_back(before)

            step(0, None)
            with pe.Fori(1, CHUNKS, 1) as i:
                step(i, i - 1)
            second_layer(CHUNKS - 1, E - 1)
            turn_back(CHUNKS - 1)

        @block.scalar
        def _(act):
            def step(i, first_step):
                for e in range(E):
                    n = i * E + e
                    if swiglu:
                        act.wait_ge(s.first, eb + 2 * n + 1)
                        if not (first_step and e < RING):
                            act.wait_ge(s.hidden, hb + n - RING + 1)
                        act.activation(act_out[:, e % RING, 0, :], first[:, e % 2, 0, :],
                                       ACT.Silu).then_inc(s.act, 1)
                    else:
                        for f in range(F):
                            act.wait_ge(s.first, eb + 2 * n + f + 1)
                            if not (first_step and e < RING) and f == 0:
                                act.wait_ge(s.second, pb * 2 + n - RING + 1)
                            act.activation(act_out[:, e % RING, f, :], first[:, e % 2, f, :], ACT.Gelu,
                                           bias=w.bias1[:, e * F + f:e * F + f + 1]).then_inc(s.act, 1)

            step(0, True)
            with act.Fori(1, CHUNKS, 1) as i:
                step(i, False)

        @block.vector
        def _(dve):
            def product(i, e):
                n = i * E + e
                dve.wait_ge(s.act, fb + n + 1)
                dve.wait_ge(s.first, eb + 2 * n + 2)
                if not (isinstance(n, int) and n < RING):
                    dve.wait_ge(s.second, pb * 2 + n - RING + 1)
                dve.tensor_tensor(hidden[:, e % RING, :], first[:, e % 2, 1, :], act_out[:, e % RING, 0, :],
                                  ALU.mult).then_inc(s.hidden, 1)

            def weigh(i, p):
                n = i * PAIRS + p
                dve.wait_ge(s.second, pb * 2 + 2 * n + 2)
                sums = second[:, p % 2, :, :, :]
                if not swiglu:
                    if not (isinstance(n, int) and n < 1):
                        dve.wait_ge(s.read, pb + n)
                    dve.tensor_tensor(biased[:], sums, spread(w.bias2[:, 2 * p:2 * p + 2, :], 2, SLOTS),
                                      ALU.add).then_inc(s.biased, 1)
                    dve.wait_ge(s.biased, bb + n + 1)
                    sums = biased[:]
                out = total if p == 0 else weighted[:, p % 2, :, :, :]
                if p == 0:
                    if not (isinstance(i, int) and i < 1):
                        dve.wait_ge(s.summed, cb + i)
                elif not (isinstance(n, int) and n < 3):
                    dve.wait_ge(s.accumulated, k.mx_base["acc"] + i * (PAIRS - 1) + max(p - 2, 0))
                tiles = gate[:, bass.ds(i * SLOTS, SLOTS), 2 * p:2 * p + 2].rearrange("p t e -> p e t")
                dve.tensor_tensor(out[:] if p == 0 else out, sums, spread(tiles, 3, C),
                                  ALU.mult).then_inc(s.read, 1)

            def add(i):
                dve.wait_ge(s.back, cb + i + 1)
                place = x[:, bass.ds(i * CHUNK, CHUNK)]
                dve.tensor_tensor(place, place, back[:], ALU.add).then_inc(s.added, 1)

            def step(i, before):
                for e in range(E):
                    if swiglu:
                        product(i, e)
                    if e % 2 == 0:
                        if e > 0:
                            weigh(i, e // 2 - 1)
                        elif before is not None:
                            weigh(before, PAIRS - 1)
                    if e == 4 and before is not None:
                        add(before)

            step(0, None)
            with dve.Fori(1, CHUNKS, 1) as i:
                step(i, i - 1)
            weigh(CHUNKS - 1, PAIRS - 1)
            add(CHUNKS - 1)

        @block.gpsimd
        def _(pool):
            ab = k.mx_base["acc"]

            def step(i):
                for p in range(1, PAIRS):
                    pool.wait_ge(s.read, pb + i * PAIRS + p + 1)
                    if not (isinstance(i, int) and i == 0 and p == 1):
                        pool.wait_ge(s.accumulated, ab + i * (PAIRS - 1) + p - 1)
                    pool.tensor_tensor(total[:], total[:], weighted[:, p % 2, :, :, :],
                                       ALU.add).then_inc(s.accumulated, 1)
                pool.wait_ge(s.accumulated, ab + (i + 1) * (PAIRS - 1))
                if not (isinstance(i, int) and i < 1):
                    pool.wait_ge(s.back, cb + i)
                pool.tensor_tensor(summed[:], total[:, 0], total[:, 1], ALU.add).then_inc(s.summed, 1)

            step(0)
            with pool.Fori(1, CHUNKS, 1) as i:
                step(i)
    k.mx_base["expert"] += 2 * E * CHUNKS
    k.mx_base["first"] += E * CHUNKS * (1 if swiglu else 2)
    k.mx_base["hidden"] += E * CHUNKS if swiglu else 0
    k.mx_base["pair"] += PAIRS * CHUNKS
    k.mx_base["biased"] += 0 if swiglu else PAIRS * CHUNKS
    k.mx_base["acc"] += (PAIRS - 1) * CHUNKS
    k.mx_base["chunk"] += CHUNKS



def conv0(k, layer, turn):
    nc, x, xn, s = k.nc, k.x, k.xn, k.c0
    QUADS = HALVES * HEADS
    GROUP = 4
    GROUPS = TILES // GROUP
    with ExitStack() as ctx:
        def sb(name, shape):
            return ctx.enter_context(nc.sbuf_tensor("c0_" + name, shape, F32))
        wk, wqv, cols = sb("wk", [P, P]), sb("wqv", [P, 2 * P]), sb("cols", [P, 5])
        bqv, wrep, fc = sb("bqv", [P, 2 * P]), sb("wrep", [HK, HEADS * C]), sb("fc", [1, 14])
        halves, quads, heads = sb("halves", [P, P]), sb("quads", [P, QUADS]), sb("heads", [P, P])
        gamma, beta, bk, b_rep, b_se = (cols[:, i:i + 1] for i in range(5))
        fetch(k, [(wk, "c0_wk"), (wqv, "c0_wqv"), (cols, "c0_cols"), (wrep, "c0_wrep"), (fc, "c0_fc"),
                  (halves, "halves"), (quads, "quads"), (heads, "heads")], [(bqv, "c0_bqv")])
        layer_norm(k, turn, 1e-6)
        batch_norm(k, halves, gamma, beta)

        key = sb("key", [P, N])
        qv = sb("qv", [P, TILES, 2 * P])
        key_t = sb("key_t", [P, TILES, P])
        query = sb("query", [P, N])
        key_max, key_sum, key_scale = sb("key_max", [P, IMAGES]), sb("key_sum", [P, IMAGES]), sb("key_scale", [P, IMAGES])
        q_max, q_sum = sb("q_max", [P, TILES, QUADS]), sb("q_sum", [P, TILES, QUADS])
        context, rows = sb("context", [P, IMAGES, HK]), sb("rows", [P, IMAGES])
        tiny = sb("tiny", [1, 8, 2 * HALVES * IMAGES * HEADS])
        gate_row = sb("gate_row", [1, IMAGES * P])
        context_t = sb("context_t", [HK, IMAGES, P])
        matrix = sb("matrix", [P, IMAGES, P])
        ps = ctx.enter_context(nc.psum_tensor("c0_ps", [P, 8, BANK], F32))
        key_ps = ps[:, 0:2, :]
        block = ctx.enter_context(nc.Block())

        def q_quarter(r):
            return qv[:, r * 8:(r + 1) * 8, 0:P].rearrange("p t (g c) -> p t g c", c=HK)

        @block.tensor
        def _(pe):
            for c in range(N // BANK):
                if c >= 2:
                    pe.wait_ge(s.key, c - 1)
                pe.matmul(ps[:, c % 2, :], wk[:], xn[:, c * BANK:(c + 1) * BANK],
                          start=True, stop=True).then_inc(s.key_ps, 1)
            for g in range(GROUPS):
                if g >= 2:
                    pe.wait_ge(s.qv, g - 1)
                for t in range(GROUP):
                    tile = g * GROUP + t
                    last = pe.matmul(ps[:, 2 + 2 * (g % 2) + t // 2, (t % 2) * 2 * P:(t % 2 + 1) * 2 * P],
                                     xn[:, tile * P:(tile + 1) * P], wqv[:], start=True, stop=True)
                last.then_inc(s.qv_ps, 1)
            for g in range(2 * GROUPS):
                if g < GROUPS:
                    pe.wait_ge(s.key_exp, g // 2 + 1)
                else:
                    pe.wait_ge(s.q_soft, (g - GROUPS) // 2 + 1)
                if g >= 2:
                    pe.wait_ge(s.turned, g - 1)
                for t in range(GROUP):
                    tile = (g % GROUPS) * GROUP + t
                    source = key[:, tile * P:(tile + 1) * P] if g < GROUPS else qv[:, tile, 0:P]
                    last = pe.transpose(ps[:, 6 + g % 2, t * P:(t + 1) * P], source, k.identity[:])
                last.then_inc(s.turned_ps, 1)
                if g == GROUPS + 1:
                    pe.wait_ge(s.turned, GROUPS)
                    pe.wait_ge(s.key, N // BANK)
                    for j in range(IMAGES):
                        for t in range(PIX // P):
                            tile = j * (PIX // P) + t
                            last = pe.matmul(ps[:, 0, j * P:(j + 1) * P], key_t[:, tile, :],
                                             qv[:, tile, P:2 * P], start=(t == 0), stop=(t == PIX // P - 1))
                    last.then_inc(s.small_ps, 1)
            pe.wait_ge(s.small, 1)
            for j in range(IMAGES):
                last = pe.matmul(ps[0:1, 1, j * QUADS:(j + 1) * QUADS], rows[:, j:j + 1], quads[:],
                                 start=True, stop=True)
            last.then_inc(s.small_ps, 1)
            pe.wait_ge(s.small, 2)
            for j in range(IMAGES):
                last = pe.matmul(ps[:, 1, 32 + j:33 + j], gate_row[:, j * P:(j + 1) * P],
                                 k.identity[0:1, 0:1], start=True, stop=True)
            last.then_inc(s.small_ps, 1)
            pe.wait_ge(s.small, 3)
            for j in range(IMAGES):
                last = pe.matmul(ps[0:HK, 2, j * P:(j + 1) * P], context[:, j, :], heads[:],
                                 start=True, stop=True)
            last.then_inc(s.small_ps, 1)
            pe.wait_ge(s.small, 4)
            for g in range(QUADS):
                for j in range(IMAGES):
                    last = pe.matmul(ps[g * HK:(g + 1) * HK, 3, j * C:(j + 1) * C],
                                     context_t[:, j, g * HK:(g + 1) * HK],
                                     wrep[:, (g % HEADS) * C:(g % HEADS + 1) * C], start=True, stop=True)
            last.then_inc(s.small_ps, 1)
            pe.wait_ge(s.small, 5)
            pe.wait_ge(s.turned, 2 * GROUPS)
            for c in range(N // BANK):
                if c >= 2:
                    pe.wait_ge(s.added, c - 1)
                pe.matmul(ps[:, 6 + c % 2, :], matrix[:, c // 2, :], query[:, c * BANK:(c + 1) * BANK],
                          start=True, stop=True).then_inc(s.out_ps, 1)

        @block.scalar
        def _(act):
            for c in range(N // BANK):
                act.wait_ge(s.key_ps, c + 1)
                act.activation(key[:, c * BANK:(c + 1) * BANK], ps[:, c % 2, :], ACT.Identity,
                               bias=bk).then_inc(s.key, 1)
            for j in range(IMAGES):
                act.wait_ge(s.key_max, j + 1)
                act.activation(key[:, j * PIX:(j + 1) * PIX], key[:, j * PIX:(j + 1) * PIX], ACT.Exp,
                               bias=key_max[:, j:j + 1],
                               accum_out=key_sum[:, j:j + 1]).then_inc(s.key_exp, 1)
            for r in range(4):
                act.wait_ge(s.q_shift, r + 1)
                act.activation(q_quarter(r), q_quarter(r), ACT.Exp).then_inc(s.q_exp, 1)
            for g in range(2 * GROUPS):
                act.wait_ge(s.turned_ps, g + 1)
                to = (key_t[:, g * GROUP:(g + 1) * GROUP, :].rearrange("p t c -> p (t c)") if g < GROUPS
                      else query[:, (g - GROUPS) * BANK:(g - GROUPS + 1) * BANK])
                act.copy(to, ps[:, 6 + g % 2, :]).then_inc(s.turned, 1)
            act.wait_ge(s.sigmoid, 1)
            act.activation(tiny[:, 5, 0:16], tiny[:, 4, 0:16], ACT.Exp, scale=-1.0).then_inc(s.gate_exp, 1)

        @block.vector
        def _(dve):
            step = [0]

            def done(ins):
                step[0] += 1
                ins.then_inc(s.step, 1)
                dve.wait_ge(s.step, step[0])

            dve.memset(matrix[:], 0.0)
            for j in range(IMAGES):
                dve.wait_ge(s.key, 2 * (j + 1))
                dve.tensor_reduce(key_max[:, j:j + 1], key[:, j * PIX:(j + 1) * PIX], AX.X, ALU.max,
                                  negate=True).then_inc(s.key_max, 1)
            for g in range(GROUPS):
                dve.wait_ge(s.qv_ps, g + 1)
                b = 2 + 2 * (g % 2)
                dve.tensor_tensor(qv[:, g * GROUP:(g + 1) * GROUP, :],
                                  ps[:, b:b + 2, :].rearrange("p b (t c) -> p (b t) c", t=2),
                                  spread(bqv[:], 1, GROUP), ALU.add).then_inc(s.qv, 1)
            for r in range(4):
                dve.wait_ge(s.qv, 2 * (r + 1))
                done(dve.tensor_reduce(q_max[:, r * 8:(r + 1) * 8, :], q_quarter(r), AX.X, ALU.max))
                dve.tensor_tensor(q_quarter(r), q_quarter(r), spread(q_max[:, r * 8:(r + 1) * 8, :], 3, HK),
                                  ALU.subtract).then_inc(s.q_shift, 1)
            for r in range(4):
                dve.wait_ge(s.q_exp, r + 1)
                done(dve.tensor_reduce(q_sum[:, r * 8:(r + 1) * 8, :], q_quarter(r), AX.X, ALU.add))
                done(dve.reciprocal(q_max[:, r * 8:(r + 1) * 8, :], q_sum[:, r * 8:(r + 1) * 8, :]))
                dve.tensor_tensor(q_quarter(r), q_quarter(r), spread(q_max[:, r * 8:(r + 1) * 8, :], 3, HK),
                                  ALU.mult).then_inc(s.q_soft, 1)
            dve.wait_ge(s.key_exp, IMAGES)
            done(dve.reciprocal(key_scale[:], key_sum[:]))
            dve.wait_ge(s.small_ps, 1)
            product = ps[:, 0, :].rearrange("p (j c) -> p j c", c=P)
            for g in range(QUADS):
                q = slice(g * HK, (g + 1) * HK)
                last = dve.tensor_tensor(context[q], product[q, :, q], spread(key_scale[q, :], 2, HK), ALU.mult)
            done(last)
            dve.tensor_reduce(rows[:], context[:], AX.X, ALU.add).then_inc(s.small, 1)
            dve.wait_ge(s.small_ps, 2)
            BT = HALVES * IMAGES
            done(dve.tensor_copy(tiny[:, 0, 0:16], ps[0:1, 1, 0:16]))
            source = tiny[:, 0, 0:16]
            for i, (wo, bo) in enumerate(((0, 4), (6, 10))):
                w4 = fc[:, wo:wo + 4].rearrange("p (m n) -> p m n", n=HEADS)
                prod = tiny[:, 1, 0:32].rearrange("p (t m n) -> p t m n", m=HEADS, n=HEADS)
                done(dve.tensor_tensor(prod, spread(source.rearrange("p (t n) -> p t n", n=HEADS), 2, HEADS),
                                       spread(w4, 1, BT), ALU.mult))
                out = tiny[:, 2 + i, 0:16].rearrange("p (t m) -> p t m", m=HEADS)
                done(dve.tensor_reduce(out, prod, AX.X, ALU.add))
                ins = dve.tensor_tensor(tiny[:, 4 if i else 6, 0:16].rearrange("p (t m) -> p t m", m=HEADS),
                                        out, spread(fc[:, bo:bo + 2], 1, BT), ALU.add)
                if i == 0:
                    done(ins)
                    done(dve.tensor_scalar(tiny[:, 7, 0:16], tiny[:, 6, 0:16], 0.0, None, ALU.max))
                    source = tiny[:, 7, 0:16]
                else:
                    ins.then_inc(s.sigmoid, 1)
            dve.wait_ge(s.gate_exp, 1)
            done(dve.tensor_scalar(tiny[:, 6, 0:16], tiny[:, 5, 0:16], 1.0, None, ALU.add))
            done(dve.reciprocal(tiny[:, 7, 0:16], tiny[:, 6, 0:16]))
            done(dve.tensor_tensor(tiny[:, 1, 0:16].rearrange("p (t n) -> p t n", n=HEADS),
                                   tiny[:, 7, 0:16].rearrange("p (t n) -> p t n", n=HEADS),
                                   spread(fc[:, 12:14], 1, BT), ALU.mult))
            dve.tensor_copy(gate_row[:].rearrange("p (t c) -> p t c", c=HK),
                            spread(tiny[:, 1, 0:16], 2, HK)).then_inc(s.small, 1)
            dve.wait_ge(s.small_ps, 3)
            dve.tensor_tensor(context[:], context[:], spread(ps[:, 1, 32:32 + IMAGES], 2, HK),
                              ALU.mult).then_inc(s.small, 1)
            dve.wait_ge(s.small_ps, 4)
            dve.tensor_scalar(context_t[:].rearrange("p j c -> p (j c)"), ps[0:HK, 2, :], b_se[0:HK], None,
                              ALU.add).then_inc(s.small, 1)
            dve.wait_ge(s.small_ps, 5)
            for h in range(HALVES):
                q = slice(h * C, (h + 1) * C)
                last = dve.tensor_copy(matrix[q, :, q],
                                       ps[q, 3, 0:IMAGES * C].rearrange("p (j c) -> p j c", c=C))
            last.then_inc(s.small, 1)
            for c in range(N // BANK):
                dve.wait_ge(s.out_ps, c + 1)
                place = x[:, c * BANK:(c + 1) * BANK]
                dve.scalar_tensor_tensor(out=place, in0=ps[:, 6 + c % 2, :], scalar=b_rep, in1=place,
                                         op0=ALU.add, op1=ALU.add).then_inc(s.added, 1)
    return turn + 1


def batch_norm(k, halves, gamma, beta):
    nc, xn, s = k.nc, k.xn, k.bn
    with ExitStack() as ctx:
        stats = ctx.enter_context(nc.sbuf_tensor("bn_stats", [P, N // BANK, 6], F32))
        own = ctx.enter_context(nc.sbuf_tensor("bn_own", [P, 4], F32))
        both = ctx.enter_context(nc.sbuf_tensor("bn_both", [P, 8], F32))
        ps = ctx.enter_context(nc.psum_tensor("bn_ps", [P, 2], F32))
        block = ctx.enter_context(nc.Block())

        @block.tensor
        def _(pe):
            pe.wait_ge(s.own, 1)
            pe.wait_ge(k.fetched_sem, k.fetched)
            pe.matmul(ps[:], halves[:], own[:, 0:2], start=True, stop=True).then_inc(s.both, 1)

        @block.scalar
        def _(act):
            act.wait_ge(s.neg_var, 1)
            act.activation(both[:, 3:4], both[:, 2:3], ACT.Sqrt, bias=k.eps[1e-5][:],
                           scale=-1.0).then_inc(s.dev, 1)

        @block.vector
        def _(dve):
            step = [0]

            def done(ins):
                step[0] += 1
                ins.then_inc(s.step, 1)
                dve.wait_ge(s.step, step[0])

            dve.wait_ge(k.fetched_sem, k.fetched)
            for c in range(N // BANK):
                last = dve.bn_stats(stats[:, c, :], xn[:, c * BANK:(c + 1) * BANK])
            done(last)
            done(dve.bn_aggr(own[:, 2:4], stats[:]))
            dve.tensor_copy(own[:, 0:1], own[:, 2:3])
            dve.scalar_tensor_tensor(out=own[:, 1:2], in0=own[:, 2:3], scalar=own[:, 2:3], in1=own[:, 3:4],
                                     op0=ALU.mult, op1=ALU.add).then_inc(s.own, 1)
            dve.wait_ge(s.both, 1)
            done(dve.tensor_copy(both[:, 0:2], ps[:]))
            dve.scalar_tensor_tensor(out=both[:, 2:3], in0=both[:, 0:1], scalar=both[:, 0:1], in1=both[:, 1:2],
                                     op0=ALU.mult, op1=ALU.subtract).then_inc(s.neg_var, 1)
            dve.wait_ge(s.dev, 1)
            done(dve.reciprocal(both[:, 4:5], both[:, 3:4]))
            done(dve.tensor_tensor(both[:, 5:6], both[:, 4:5], gamma, ALU.mult))
            done(dve.tensor_tensor(both[:, 6:7], both[:, 0:1], both[:, 5:6], ALU.mult))
            done(dve.tensor_tensor(both[:, 7:8], beta, both[:, 6:7], ALU.subtract))
            dve.tensor_scalar(xn[:], xn[:], both[:, 5:6], both[:, 7:8], ALU.mult, ALU.add)



def conv1(k, layer, turn):
    nc, x, xn, s = k.nc, k.x, k.xn, k.c1
    EXPERTS, RED, POOL, TAPS = 8, 16, 4, 9
    CELL = H // POOL
    CELLS = POOL * POOL
    PAD = W + 2
    HALF = H // 2
    KERNEL = TAPS * C
    with ExitStack() as ctx:
        def sb(name, shape):
            return ctx.enter_context(nc.sbuf_tensor("c1_" + name, shape, F32))
        w1, w2 = sb("w1", [P, HALVES * RED]), sb("w2", [HALVES * RED, P])
        wexp, weight = sb("wexp", [P, EXPERTS * CELLS]), sb("weight", [P, EXPERTS, KERNEL])
        fetch(k, [(w1, "c1_w1"), (w2, "c1_w2"), (weight, "c1_weight")], [(wexp, "c1_wexp")])
        layer_norm(k, turn, 1e-6)
        padded = sb("padded", [P, IMAGES, PAD, PAD])
        row_sum, cells = sb("row_sum", [P, IMAGES * H * POOL]), sb("cells", [P, IMAGES * CELLS])
        total, squeezed = sb("total", [P, IMAGES]), sb("squeezed", [HALVES * RED, IMAGES])
        cell_mean, product = sb("cell_mean", [P, IMAGES, CELLS]), sb("product", [P, IMAGES, EXPERTS, CELLS])
        expert = sb("expert", [P, IMAGES, EXPERTS])
        routing = sb("routing", [P, IMAGES, EXPERTS])
        mixed = sb("mixed", [P, IMAGES, KERNEL])
        kernel = sb("kernel", [P, IMAGES, TAPS, P])
        ps = ctx.enter_context(nc.psum_tensor("c1_ps", [P, 2, BANK], F32))
        tiny = ctx.enter_context(nc.psum_tensor("c1_tiny", [P, BANK], F32))
        block = ctx.enter_context(nc.Block())
        image = xn[:].rearrange("p (j y x) -> p j y x", j=IMAGES, y=H)

        @block.gpsimd
        def _(pool):
            pool.memset(padded[:], 0.0).then_inc(s.cleared, 1)
            pool.memset(kernel[:], 0.0).then_inc(s.cleared, 1)

        @block.scalar
        def _(act):
            act.wait_ge(s.cleared, 1)
            for j in range(IMAGES):
                act.copy(padded[:, j, 1:1 + H, 1:1 + W], image[:, j]).then_inc(s.padded, 1)
            act.wait_ge(s.small_ps, 1)
            act.activation(squeezed[:], tiny[0:HALVES * RED, 0:IMAGES], ACT.Relu,
                           scale=1.0 / PIX).then_inc(s.squeezed, 1)
            act.wait_ge(s.logit, 1)
            act.activation(routing[:], expert[:], ACT.Sigmoid).then_inc(s.routing, 1)

        @block.tensor
        def _(pe):
            pe.wait_ge(k.fetched_sem, k.fetched)
            pe.wait_ge(s.total, 1)
            pe.matmul(tiny[0:HALVES * RED, 0:IMAGES], w1[:], total[:], start=True, stop=True).then_inc(s.small_ps, 1)
            pe.wait_ge(s.squeezed, 1)
            pe.matmul(tiny[:, 0:IMAGES], w2[:], squeezed[:], start=True, stop=True)
            pe.matmul(tiny[:, 64:128], k.average[:], cells[:], start=True, stop=True).then_inc(s.small_ps, 1)
            for c in range(2 * IMAGES):
                j, y = c // 2, (c % 2) * HALF
                pe.wait_ge(s.padded, j + 1)
                pe.wait_ge(s.kernel, j + 1)
                if c >= 2:
                    pe.wait_ge(s.added, c - 1)
                for t in range(TAPS):
                    last = pe.matmul(ps[:, c % 2, :], kernel[:, j, t, :],
                                     padded[:, j, y + t // 3:y + t // 3 + HALF, t % 3:t % 3 + W],
                                     start=(t == 0), stop=(t == TAPS - 1))
                last.then_inc(s.out_ps, 1)

        @block.vector
        def _(dve):
            step = [0]

            def done(ins):
                step[0] += 1
                ins.then_inc(s.step, 1)
                dve.wait_ge(s.step, step[0])

            done(dve.tensor_reduce(row_sum[:], xn[:].rearrange("p (n x) -> p n x", x=CELL), AX.X, ALU.add))
            done(dve.tensor_reduce(cells[:].rearrange("p (j q) -> p j q", q=POOL),
                                   row_sum[:].rearrange("p (j y q) -> p j q y", y=CELL, q=POOL), AX.X, ALU.add))
            dve.tensor_reduce(total[:], cells[:].rearrange("p (j c) -> p j c", c=CELLS), AX.X,
                              ALU.add).then_inc(s.total, 1)
            dve.wait_ge(s.small_ps, 2)
            done(dve.tensor_scalar(cell_mean[:].rearrange("p j c -> p (j c)"), tiny[:, 64:128],
                                   1.0 / (CELL * CELL), None, ALU.mult))
            dve.wait_ge(k.fetched_sem, k.fetched)
            done(dve.tensor_tensor(product[:], spread(cell_mean[:], 2, EXPERTS),
                                   spread(wexp[:].rearrange("p (k c) -> p k c", c=CELLS), 1, IMAGES), ALU.mult))
            done(dve.tensor_reduce(expert[:], product[:], AX.X, ALU.add))
            dve.tensor_tensor(expert[:], expert[:], spread(tiny[:, 0:IMAGES], 2, EXPERTS),
                              ALU.mult).then_inc(s.logit, 1)
            dve.wait_ge(s.routing, 1)
            dve.wait_ge(s.cleared, 2)
            start = step[0]
            for pair in range(IMAGES // 2):
                for e in range(EXPERTS):
                    for j in (2 * pair, 2 * pair + 1):
                        if e > 0:
                            dve.wait_ge(s.step, step[0] - (0 if e == EXPERTS - 1 and j % 2 else 1))
                        if e == 0:
                            ins = dve.tensor_scalar(mixed[:, j], weight[:, e], routing[:, j, e:e + 1], None, ALU.mult)
                        elif e < EXPERTS - 1:
                            ins = dve.scalar_tensor_tensor(out=mixed[:, j], in0=weight[:, e],
                                                           scalar=routing[:, j, e:e + 1], in1=mixed[:, j],
                                                           op0=ALU.mult, op1=ALU.add)
                        else:
                            for h in range(HALVES):
                                q = slice(h * C, (h + 1) * C)
                                tap = lambda a: a.rearrange("p (t c) -> p t c", c=C)
                                ins = dve.scalar_tensor_tensor(out=kernel[q, j, :, q], in0=tap(weight[q, e]),
                                                               scalar=routing[q, j, e:e + 1], in1=tap(mixed[q, j]),
                                                               op0=ALU.mult, op1=ALU.add)
                            ins.then_inc(s.kernel, 1)
                            continue
                        ins.then_inc(s.step, 1)
                        step[0] += 1
            for c in range(2 * IMAGES):
                dve.wait_ge(s.out_ps, c + 1)
                place = x[:, c * BANK:(c + 1) * BANK]
                dve.tensor_tensor(place, place, ps[:, c % 2, :], ALU.add).then_inc(s.added, 1)
    return turn + 1



def conv2(k, layer, turn):
    nc, x, xn, s = k.nc, k.x, k.xn, k.c2
    K, TAPS, A, ATAPS = 5, 25, 3, 9
    PAD = W + 4
    Q = HALVES * CM
    HALF = H // 2
    with ExitStack() as ctx:
        def sb(name, shape):
            return ctx.enter_context(nc.sbuf_tensor("c2_" + name, shape, F32))
        w, cols = sb("w", [P, Q]), sb("cols", [P, 4])
        row = sb("row", [P, 2 * TAPS + 2 * ATAPS + 4])
        fuse = sb("fuse", [P, 2, P])
        conv_b, adap_b, atrous_b, fuse_b = (cols[:, i:i + 1] for i in range(4))
        fetch(k, [(w, "c2_w"), (cols, "c2_cols"), (fuse, "c2_fuse")], [(row, "c2_row")])
        layer_norm(k, turn, 1e-6)
        total, g = sb("total", [P, IMAGES]), sb("g", [P, 1])
        taps, raw = sb("taps", [P, TAPS + ATAPS]), sb("raw", [P, TAPS + ATAPS])
        f = sb("f", [P, PAD, PAD])
        near, far, product = sb("near", [P, H, W]), sb("far", [P, H, W]), sb("product", [P, 2, H, W])
        f_ps = ctx.enter_context(nc.psum_tensor("c2_f_ps", [P, 2, BANK], F32))
        g_ps = ctx.enter_context(nc.psum_tensor("c2_g_ps", [P, BANK], F32))
        out_ps = ctx.enter_context(nc.psum_tensor("c2_out_ps", [P, 2, BANK], F32))
        block = ctx.enter_context(nc.Block())

        @block.tensor
        def _(pe):
            pe.wait_ge(k.fetched_sem, k.fetched)
            for c in range(2):
                for j in range(IMAGES):
                    last = pe.matmul(f_ps[j * Q:(j + 1) * Q, c, :], w[:],
                                     xn[:, j * PIX + c * BANK:j * PIX + (c + 1) * BANK], start=True, stop=True)
                last.then_inc(s.f_ps, 1)
            pe.wait_ge(s.total, 1)
            for j in range(IMAGES):
                last = pe.matmul(g_ps[j * Q:(j + 1) * Q, 0:1], w[:], total[:, j:j + 1], start=True, stop=True)
            last.then_inc(s.g_ps, 1)
            pe.wait_ge(s.near, TAPS)
            pe.wait_ge(s.far, ATAPS)
            for c in range(2 * IMAGES):
                j, y = c // 2, (c % 2) * HALF
                q = slice(j * Q, (j + 1) * Q)
                if c >= 2:
                    pe.wait_ge(s.added, c - 1)
                pe.matmul(out_ps[:, c % 2, :], fuse[q, 0, :], near[q, y:y + HALF, :], start=True, stop=False)
                pe.matmul(out_ps[:, c % 2, :], fuse[q, 1, :], far[q, y:y + HALF, :],
                          start=False, stop=True).then_inc(s.out_ps, 1)

        @block.scalar
        def _(act):
            act.wait_ge(k.fetched_sem, k.fetched)
            act.wait_ge(s.cleared, 1)
            for c in range(2):
                act.wait_ge(s.f_ps, c + 1)
                act.activation(f[:, 2 + c * HALF:2 + (c + 1) * HALF, 2:2 + W],
                               f_ps[:, c, :].rearrange("p (y x) -> p y x", x=W), ACT.Relu,
                               bias=conv_b).then_inc(s.f, 1)
            act.wait_ge(s.g_ps, 1)
            act.activation(g[:], g_ps[:, 0:1], ACT.Relu, bias=conv_b, scale=1.0 / PIX).then_inc(s.g, 1)
            act.wait_ge(s.taps, 1)
            act.wait_ge(s.f, 2)
            for t in range(ATAPS):
                dy, dx = 2 * (t // A), 2 * (t % A)
                view = f[:, dy:dy + H, dx:dx + W]
                if t == 0:
                    act.activation(far[:], view, ACT.Identity, bias=atrous_b,
                                   scale=taps[:, TAPS:TAPS + 1]).then_inc(s.product, 1)
                else:
                    if t >= 3:
                        act.wait_ge(s.far, t - 1)
                    act.activation(product[:, t % 2], view, ACT.Copy,
                                   scale=taps[:, TAPS + t:TAPS + t + 1]).then_inc(s.product, 1)

        @block.gpsimd
        def _(pool):
            pool.memset(f[:], 0.0).then_inc(s.cleared, 1)
            pool.wait_ge(s.product, 1)
            pool.engine_nop().then_inc(s.far, 1)
            for t in range(1, ATAPS):
                pool.wait_ge(s.product, t + 1)
                pool.wait_ge(s.far, t)
                pool.tensor_tensor(far[:], far[:], product[:, t % 2], ALU.add).then_inc(s.far, 1)

        @block.vector
        def _(dve):
            step = [0]

            def done(ins):
                step[0] += 1
                ins.then_inc(s.step, 1)
                dve.wait_ge(s.step, step[0])

            dve.tensor_reduce(total[:], xn[:].rearrange("p (j n) -> p j n", n=PIX), AX.X,
                              ALU.add).then_inc(s.total, 1)
            dve.wait_ge(k.fetched_sem, k.fetched)
            dve.wait_ge(s.g, 1)
            for o, n, b in ((0, TAPS, 0), (TAPS, ATAPS, 2 * TAPS)):
                scalars = 2 * (TAPS + ATAPS) + (0 if o == 0 else 2)
                done(dve.scalar_tensor_tensor(out=raw[:, o:o + n], in0=row[:, b:b + n], scalar=g[:],
                                              in1=row[:, b + n:b + 2 * n], op0=ALU.mult, op1=ALU.add))
                last = dve.tensor_scalar(taps[:, o:o + n], raw[:, o:o + n], row[:, scalars:scalars + 1],
                                         row[:, scalars + 1:scalars + 2], ALU.mult, ALU.add)
            last.then_inc(s.taps, 1)
            dve.wait_ge(s.taps, 1)
            dve.wait_ge(s.f, 2)
            for t in range(TAPS):
                view = f[:, t // K:t // K + H, t % K:t % K + W]
                if t == 0:
                    ins = dve.tensor_scalar(near[:], view, taps[:, 0:1], adap_b, ALU.mult, ALU.add)
                else:
                    dve.wait_ge(s.near, t)
                    ins = dve.scalar_tensor_tensor(out=near[:], in0=view, scalar=taps[:, t:t + 1], in1=near[:],
                                                   op0=ALU.mult, op1=ALU.add)
                ins.then_inc(s.near, 1)
            for c in range(2 * IMAGES):
                dve.wait_ge(s.out_ps, c + 1)
                place = x[:, c * BANK:(c + 1) * BANK]
                dve.scalar_tensor_tensor(out=place, in0=out_ps[:, c % 2, :], scalar=fuse_b, in1=place,
                                         op0=ALU.add, op1=ALU.add).then_inc(s.added, 1)
    return turn + 1



TAPS = 9
TILE_ROWS = P // W
QTILES = PIX // P
REACH = 2
XTILES = QTILES + 1
TAP_GROUP = 3


def conv3(k, layer, turn):
    nc, x, xn, s = k.nc, k.x, k.xn, k.c3
    GN = 2
    PAD = W + 2
    HALF = H // 2
    with ExitStack() as ctx:
        def sb(name, shape, dt=F32):
            return ctx.enter_context(nc.sbuf_tensor("c3_" + name, shape, dt))
        w_off, cols = sb("w_off", [P, TAPS, 4 * TAPS]), sb("cols", [P, 3])
        w_deform = sb("w_deform", [P, TAPS // TAP_GROUP, HALVES * TAP_GROUP * C])
        base, ints, pairs = sb("base", [P, 4 * TAPS]), sb("ints", [P, 2 * H + TILE_ROWS]), sb("pairs", [P, P])
        fetch(k, [(w_off, "c3_w_off"), (cols, "c3_cols"), (w_deform, "c3_w_deform"), (base, "c3_base"),
                  (pairs, "pairs")], [(ints, "c3_ints")])
        off_b, gn_gamma, gn_beta = (cols[:, i:i + 1] for i in range(3))
        start_at_one(k, k.c3_near.all + k.c3_rest.all)
        layer_norm(k, turn, 1e-6)
        coords = sb("coords", [P, TILES, 4 * TAPS])
        flag = sb("flag", [1, 2], mybir.dt.int32)
        offsets(k, PAD, HALF, w_off, off_b, coords, flag)
        sums = sb("sums", [P, TILES, HALVES, C])
        band = {ty: [(ty, ty + 1)] for ty in range(QTILES)}
        sample(k, "near", k.c3_near, band, w_deform, coords, base, ints, sums, None)
        rest = {}
        for ty in range(QTILES):
            q0, q1 = band[ty][0]
            rest[ty] = [(a, min(a + 2, end)) for start, end in ((0, q0 - 1), (q1 + 1, XTILES - 1))
                        for a in range(start, end + 1, 3)]
        sample(k, "rest", k.c3_rest, rest, w_deform, coords, base, ints, sums, flag)
        group_norm(k, sums, pairs, gn_gamma, gn_beta)
    return turn + 1


def start_at_one(k, semaphores):
    with ExitStack() as ctx:
        block = ctx.enter_context(k.nc.Block())

        @block.sync
        def _(sp):
            for semaphore in semaphores:
                sp.sem_inc(semaphore, 1)


def offsets(k, PAD, HALF, w_off, off_b, coords, flag):
    nc, xn, s = k.nc, k.xn, k.c3
    ROWS = 4 * TAPS
    PER_BANK = 8
    with ExitStack() as ctx:
        padded = ctx.enter_context(nc.sbuf_tensor("c3_padded", [P, IMAGES, PAD, PAD], F32))
        off = ctx.enter_context(nc.sbuf_tensor("c3_off", [ROWS, N], F32))
        reach = ctx.enter_context(nc.sbuf_tensor("c3_reach", [P, 4], F32))
        most = ctx.enter_context(nc.sbuf_tensor("c3_most", [1, 4], F32))
        ps = ctx.enter_context(nc.psum_tensor("c3_off_ps", [P, 2, BANK], F32))
        turned = ctx.enter_context(nc.psum_tensor("c3_turned", [P, 4, BANK], F32))
        block = ctx.enter_context(nc.Block())

        @block.gpsimd
        def _(pool):
            pool.memset(padded[:], 0.0).then_inc(s.cleared, 1)

        @block.scalar
        def _(act):
            act.wait_ge(s.cleared, 1)
            act.wait_ge(k.fetched_sem, k.fetched)
            for j in range(IMAGES):
                act.copy(padded[:, j, 1:1 + H, 1:1 + W],
                         xn[:, j * PIX:(j + 1) * PIX].rearrange("p (y x) -> p y x", x=W)).then_inc(s.padded, 1)
            for c in range(N // BANK):
                act.wait_ge(s.off_ps, c + 1)
                act.activation(off[:, c * BANK:(c + 1) * BANK], ps[0:ROWS, c % 2, :], ACT.Identity,
                               bias=off_b[0:ROWS]).then_inc(s.off, 1)

        @block.tensor
        def _(pe):
            pe.wait_ge(k.fetched_sem, k.fetched)
            for c in range(2 * IMAGES):
                j, y = c // 2, (c % 2) * HALF
                pe.wait_ge(s.padded, j + 1)
                if c >= 2:
                    pe.wait_ge(s.off, c - 1)
                for t in range(TAPS):
                    last = pe.matmul(ps[0:ROWS, c % 2, :], w_off[:, t, :],
                                     padded[:, j, y + t // 3:y + t // 3 + HALF, t % 3:t % 3 + W],
                                     start=(t == 0), stop=(t == TAPS - 1))
                last.then_inc(s.off_ps, 1)
            for t in range(TILES):
                pe.wait_ge(s.off, t * P // BANK + 1)
                last = pe.transpose(turned[:, t // PER_BANK, (t % PER_BANK) * ROWS:(t % PER_BANK + 1) * ROWS],
                                    off[:, t * P:(t + 1) * P], k.identity[0:ROWS, 0:ROWS])
                if t % PER_BANK == PER_BANK - 1:
                    last.then_inc(s.turned, 1)
            pe.wait_ge(s.reach, 1)
            pe.transpose(ps[0:1, 0, 0:P], reach[:, 2:3], k.identity[:]).then_inc(s.reach_ps, 1)

        @block.vector
        def _(dve):
            step = [0]

            def done(ins):
                step[0] += 1
                ins.then_inc(s.step, 1)
                dve.wait_ge(s.step, step[0])

            dve.wait_ge(s.turned, TILES // PER_BANK)
            rows = coords[:].rearrange("p t (n c) -> p t n c", c=2)[:, :, :, 0]
            for b in range(TILES // PER_BANK):
                last = dve.tensor_copy(coords[:, b * PER_BANK:(b + 1) * PER_BANK, :],
                                       turned[:, b, 0:PER_BANK * ROWS].rearrange("p (t r) -> p t r", r=ROWS))
            done(last)
            dve.tensor_reduce(reach[:, 0:1], rows, AX.XY, ALU.max)
            done(dve.tensor_reduce(reach[:, 1:2], rows, AX.XY, ALU.min))
            dve.scalar_tensor_tensor(out=reach[:, 2:3], in0=reach[:, 1:2], scalar=-1.0, in1=reach[:, 0:1],
                                     op0=ALU.mult, op1=ALU.max).then_inc(s.reach, 1)
            dve.wait_ge(s.reach_ps, 1)
            done(dve.tensor_reduce(most[:, 0:1], ps[0:1, 0, 0:P], AX.X, ALU.max))
            done(dve.tensor_scalar(most[:, 1:2], most[:, 0:1], float(REACH), None, ALU.is_ge))
            dve.tensor_copy(flag[:, 0:1], most[:, 1:2])


def sample(k, name, s, blocks, w_deform, coords, base, ints, sums, flag):
    nc, xn = k.nc, k.xn
    items = [(ty, h, q0, q1) for ty in range(QTILES) for h in range(HALVES) for q0, q1 in blocks[ty]]
    first = [i == 0 or items[i - 1][:2] != it[:2] for i, it in enumerate(items)]
    last_of = [i + 1 == len(items) or items[i + 1][:2] != it[:2] for i, it in enumerate(items)]
    G = TAPS // TAP_GROUP
    ITEMS, STEPS, SUMS, VALUES = len(items), len(items) * G, HALVES * QTILES, XTILES * G
    VCOLS = TAP_GROUP * C
    RMAX = max(q1 - q0 + 1 for _, _, q0, q1 in items) * TILE_ROWS
    EDGE = REACH + 1
    assert ITEMS % 2 == 0 and STEPS % 2 == 0
    with ExitStack() as ctx:
        def sb(nm, shape, dt=F32):
            return ctx.enter_context(nc.sbuf_tensor(f"c3_{name}_{nm}", shape, dt))
        staged = sb("staged", [P, (EDGE + H + EDGE) * W])
        position = sb("position", [P, QTILES, 4 * TAPS])
        values = sb("values", [P, XTILES, G, HALVES * VCOLS])
        dist = sb("dist", [P, 2, TAPS, W + RMAX])
        hats = sb("hats", [P, 2, TAPS, W + RMAX])
        weights = sb("weights", [P, 2, TAP_GROUP, RMAX * W])
        matrix = sb("matrix", [P, 2, TAP_GROUP, RMAX * W])
        turned = ctx.enter_context(nc.psum_tensor(f"c3_{name}_turned", [P, 2, TAP_GROUP, BANK], F32))
        sum_ps = ctx.enter_context(nc.psum_tensor(f"c3_{name}_sum_ps", [P, 2, BANK], F32))
        block = ctx.enter_context(nc.Block())

        def run(eng, body):
            def loop():
                with eng.Fori(0, IMAGES, 1) as j:
                    body(j)
            if flag is None:
                loop()
            else:
                beyond = eng.value_load(flag[0:1, 0:1], min_val=0, max_val=1)
                with eng.If(beyond > 0):
                    loop()

        @block.tensor
        def _(pe):
            def values_of(j):
                pe.wait_ge(s.staged, 1 + j + 1)
                pe.wait_ge(s.summed, 1 + j * SUMS)
                for v in range(VALUES):
                    q, g = v // G, v % G
                    pe.wait_ge(s.values, 1 + j * VALUES + max(v - 1, 0))
                    pe.matmul(sum_ps[:, v % 2, 0:HALVES * VCOLS], staged[:, q * P + g * W:(q + 1) * P + g * W],
                              w_deform[:, g, :],
                              start=True, stop=True).then_inc(s.values_ps, 1)

            def turn(j, n):
                q0, q1 = items[n // G][2:]
                pe.wait_ge(s.weights, 1 + j * STEPS + n + 1)
                pe.wait_ge(s.matrix, 1 + j * STEPS + max(n - 1, 0))
                for t in range(TAP_GROUP):
                    for q in range(q1 - q0 + 1):
                        last = pe.transpose(turned[:, n % 2, t, q * P:(q + 1) * P],
                                            weights[:, n % 2, t, q * P:(q + 1) * P], k.identity[:])
                last.then_inc(s.turned, 1)

            def multiply(j, n):
                i, g = n // G, n % G
                ty, h, q0, q1 = items[i]
                pe.wait_ge(s.matrix, 1 + j * STEPS + n + 1)
                tile = ty * HALVES + h
                if g == 0 and first[i]:
                    pe.wait_ge(s.summed, 1 + j * SUMS + max(tile - 1, 0))
                for t in range(TAP_GROUP):
                    for q in range(q1 - q0 + 1):
                        last = pe.matmul(sum_ps[:, tile % 2, 0:C], matrix[:, n % 2, t, q * P:(q + 1) * P],
                                         values[:, q0 + q, g, h * VCOLS + t * C:h * VCOLS + (t + 1) * C],
                                         start=(g == 0 and first[i] and t == 0 and q == 0),
                                         stop=(g == G - 1 and last_of[i] and t == TAP_GROUP - 1 and q == q1 - q0))
                last.then_inc(s.used, 1)

            def body(j):
                values_of(j)
                pe.wait_ge(s.values, 1 + (j + 1) * VALUES)
                for n in range(STEPS):
                    turn(j, n)
                    if n > 0:
                        multiply(j, n - 1)
                multiply(j, STEPS - 1)
            run(pe, body)

        @block.scalar
        def _(act):
            def body(j):
                act.wait_ge(s.used, 1 + j * STEPS)
                for v in range(VALUES):
                    q, g = v // G, v % G
                    act.wait_ge(s.values_ps, 1 + j * VALUES + v + 1)
                    act.copy(values[:, q, g, :], sum_ps[:, v % 2, 0:HALVES * VCOLS]).then_inc(s.values, 1)
                for n in range(STEPS):
                    q0, q1 = items[n // G][2:]
                    width = (q1 - q0 + 1) * P
                    act.wait_ge(s.turned, 1 + j * STEPS + n + 1)
                    act.wait_ge(s.used, 1 + j * STEPS + max(n - 1, 0))
                    act.copy(matrix[:, n % 2, :, 0:width], turned[:, n % 2, :, 0:width]).then_inc(s.matrix, 1)
            run(act, body)

        @block.gpsimd
        def _(pool):
            def body(j):
                pool.wait_ge(s.position, 1 + j + 1)
                for i, (ty, h, q0, q1) in enumerate(items):
                    pool.wait_ge(s.hats, 1 + j * ITEMS + max(i - 1, 0))
                    own = position[:, ty, h * 2 * TAPS:(h + 1) * 2 * TAPS].rearrange("p (t c) -> p t c", c=2)
                    rows = (q1 - q0 + 1) * TILE_ROWS
                    start = H + (q0 - ty) * TILE_ROWS - REACH
                    pool.tensor_tensor(dist[:, i % 2, :, 0:W], spread(own[:, :, 1], 2, W),
                                       spread(ints[:, H:H + W], 1, TAPS), ALU.subtract)
                    pool.tensor_tensor(dist[:, i % 2, :, W:W + rows], spread(own[:, :, 0], 2, rows),
                                       spread(ints[:, start:start + rows], 1, TAPS),
                                       ALU.subtract).then_inc(s.dist, 1)
            run(pool, body)

        @block.vector
        def _(dve):
            def body(j):
                def used(i):
                    q0, q1 = items[i][2:]
                    return W + (q1 - q0 + 1) * TILE_ROWS

                def negate(i):
                    dve.wait_ge(s.dist, 1 + j * ITEMS + i + 1)
                    dve.wait_ge(s.weights, 1 + j * STEPS + G * max(i - 1, 0))
                    own = dist[:, i % 2, :, 0:used(i)]
                    dve.scalar_tensor_tensor(out=hats[:, i % 2, :, 0:used(i)], in0=own, scalar=-1.0, in1=own,
                                             op0=ALU.mult, op1=ALU.min).then_inc(s.hats, 1)

                def hat(i):
                    dve.wait_ge(s.hats, 1 + j * ITEMS + i + 1)
                    dve.tensor_scalar(hats[:, i % 2, :, 0:used(i)], hats[:, i % 2, :, 0:used(i)], 1.0, 0.0,
                                      ALU.add, ALU.max).then_inc(s.hatted, 1)

                def weigh(n):
                    i, g = n // G, n % G
                    rows = used(i) - W
                    own = hats[:, i % 2, g * TAP_GROUP:(g + 1) * TAP_GROUP, :]
                    dve.wait_ge(s.hatted, 1 + j * ITEMS + i + 1)
                    dve.wait_ge(s.turned, 1 + j * STEPS + max(n - 1, 0))
                    dve.tensor_tensor(
                        weights[:, n % 2, :, 0:rows * W].rearrange("p t (r c) -> p t r c", c=W),
                        spread(own[:, :, W:W + rows], 3, W), spread(own[:, :, 0:W], 2, rows),
                        ALU.mult).then_inc(s.weights, 1)

                def keep(i):
                    ty, h = items[i][:2]
                    dve.wait_ge(s.used, 1 + j * STEPS + (i + 1) * G)
                    place = sums[:, bass.ds(j * QTILES + ty, 1), h, :].rearrange("p o c -> p (o c)")
                    source = sum_ps[:, (ty * HALVES + h) % 2, 0:C]
                    if flag is None:
                        dve.tensor_scalar(place, source, 1.0, None, ALU.mult).then_inc(s.summed, 1)
                    else:
                        dve.tensor_tensor(place, place, source, ALU.add).then_inc(s.summed, 1)

                dve.wait_ge(s.values_ps, 1 + j * VALUES)
                dve.tensor_scalar(staged[:, EDGE * W:(EDGE + H) * W], xn[:, bass.ds(j * PIX, PIX)], 1.0, None,
                                  ALU.mult).then_inc(s.staged, 1)
                dve.wait_ge(s.dist, 1 + j * ITEMS)
                dve.tensor_tensor(position[:], coords[:, bass.ds(j * QTILES, QTILES), :],
                                  spread(base[:], 1, QTILES), ALU.add).then_inc(s.position, 1)
                negate(0)
                hat(0)
                for i in range(ITEMS):
                    if i + 1 < ITEMS:
                        negate(i + 1)
                    weigh(G * i)
                    if i + 1 < ITEMS:
                        hat(i + 1)
                    weigh(G * i + 1)
                    if i > 0 and last_of[i - 1]:
                        keep(i - 1)
                    weigh(G * i + 2)
                keep(ITEMS - 1)
            for edge in (slice(0, EDGE * W), slice((EDGE + H) * W, (EDGE + H + EDGE) * W)):
                dve.memset(staged[:, edge], 0.0)
            run(dve, body)


def group_norm(k, sums, pairs, gamma, beta):
    nc, x, s = k.nc, k.x, k.c3
    STATS = PIX // BANK
    with ExitStack() as ctx:
        def sb(name, shape):
            return ctx.enter_context(nc.sbuf_tensor("gn_" + name, shape, F32))
        y = sb("y", [P, N])
        stats, own, group = sb("stats", [P, IMAGES * STATS, 6]), sb("own", [P, IMAGES, 4]), sb("group", [P, 7, IMAGES])
        ps = ctx.enter_context(nc.psum_tensor("gn_ps", [P, 2, BANK], F32))
        mean_ps = ctx.enter_context(nc.psum_tensor("gn_mean_ps", [P, IMAGES, 2], F32))
        block = ctx.enter_context(nc.Block())

        @block.tensor
        def _(pe):
            for g in range(N // BANK):
                if g >= 2:
                    pe.wait_ge(s.y, g - 1)
                for t in range(BANK // P):
                    last = pe.transpose(ps[:, g % 2, t * P:(t + 1) * P],
                                        sums[:, g * (BANK // P) + t].rearrange("p h c -> p (h c)"), k.identity[:])
                last.then_inc(s.y_ps, 1)
            pe.wait_ge(s.own, 1)
            pe.matmul(mean_ps[:], pairs[:], own[:, :, 0:2], start=True, stop=True).then_inc(s.group, 1)

        @block.scalar
        def _(act):
            for g in range(N // BANK):
                act.wait_ge(s.y_ps, g + 1)
                act.copy(y[:, g * BANK:(g + 1) * BANK], ps[:, g % 2, :]).then_inc(s.y, 1)
            act.wait_ge(s.neg_var, 1)
            act.activation(group[:, 3], group[:, 2], ACT.Sqrt, bias=k.eps[1e-5][:], scale=-1.0).then_inc(s.dev, 1)
            act.wait_ge(s.affine, 1)
            for j in range(IMAGES):
                act.activation(y[:, j * PIX:(j + 1) * PIX], y[:, j * PIX:(j + 1) * PIX], ACT.Relu,
                               bias=group[:, 6, j:j + 1], scale=group[:, 5, j:j + 1]).then_inc(s.relu, 1)

        @block.vector
        def _(dve):
            step = [k.c3_steps]

            def done(ins):
                step[0] += 1
                ins.then_inc(s.gn_step, 1)
                dve.wait_ge(s.gn_step, step[0])

            for g in range(N // BANK):
                dve.wait_ge(s.y, g + 1)
                last = dve.bn_stats(stats[:, g, :], y[:, g * BANK:(g + 1) * BANK])
            done(last)
            for j in range(IMAGES):
                last = dve.bn_aggr(own[:, j, 2:4], stats[:, j * STATS:(j + 1) * STATS, :])
            done(last)
            dve.tensor_copy(own[:, :, 0], own[:, :, 2])
            done(dve.tensor_tensor(own[:, :, 1], own[:, :, 2], own[:, :, 2], ALU.mult))
            dve.tensor_tensor(own[:, :, 1], own[:, :, 1], own[:, :, 3], ALU.add).then_inc(s.own, 1)
            dve.wait_ge(s.group, 1)
            done(dve.tensor_copy(group[:, 0:2], mean_ps[:].rearrange("p j c -> p c j")))
            done(dve.tensor_tensor(group[:, 3], group[:, 0], group[:, 0], ALU.mult))
            dve.tensor_tensor(group[:, 2], group[:, 3], group[:, 1], ALU.subtract).then_inc(s.neg_var, 1)
            dve.wait_ge(s.dev, 1)
            done(dve.reciprocal(group[:, 4], group[:, 3]))
            done(dve.tensor_scalar(group[:, 5], group[:, 4], gamma, None, ALU.mult))
            done(dve.tensor_tensor(group[:, 4], group[:, 0], group[:, 5], ALU.mult))
            dve.tensor_scalar(group[:, 6], group[:, 4], -1.0, beta, ALU.mult, ALU.add).then_inc(s.affine, 1)
            for j in range(IMAGES):
                dve.wait_ge(s.relu, j + 1)
                place = x[:, j * PIX:(j + 1) * PIX]
                dve.tensor_tensor(place, place, y[:, j * PIX:(j + 1) * PIX], ALU.add)



def load_inputs(k):
    nc = k.nc
    with ExitStack() as ctx:
        block = ctx.enter_context(nc.Block())

        @block.sync
        def _(sp):
            sp.dma_start(k.average[:], k.ins["average"]).then_inc(k.x_loaded, 16)
            sp.dma_start(k.identity[:], k.ins["identity"]).then_inc(k.x_loaded, 16)
            sp.dma_start(k.countdown[:], k.ins["countdown"]).then_inc(k.x_loaded, 16)
            sp.dma_start(k.shifted[:], k.ins["shifted"]).then_inc(k.x_loaded, 16)
            sp.dma_start(k.rows[:], k.ins["rows"]).then_inc(k.x_loaded, 16)
            k.x_all = 16 * (5 + HALVES)
            for h in range(HALVES):
                sp.dma_start(k.x[h * C:(h + 1) * C, :].rearrange("c (b s) -> c b s", b=IMAGES),
                             k.ins["x"][h * IMAGES:(h + 1) * IMAGES].rearrange("b c s -> c b s")
                             ).then_inc(k.x_loaded, 16)

        @block.vector
        def _(dve):
            for eps, place in k.eps.items():
                dve.memset(place[:], eps)


def store_output(k):
    nc = k.nc
    with ExitStack() as ctx:
        block = ctx.enter_context(nc.Block())

        @block.sync
        def _(sp):
            for h in range(HALVES):
                sp.dma_start(k.out[h * IMAGES:(h + 1) * IMAGES].rearrange("b c s -> c b s"),
                             k.x[h * C:(h + 1) * C, :].rearrange("c (b s) -> c b s", b=IMAGES)
                             ).then_inc(k.stored, 16)
            sp.wait_ge(k.stored, 16 * HALVES)


def fetch(k, copies, rows=()):
    with ExitStack() as ctx:
        block = ctx.enter_context(k.nc.Block())

        @block.sync
        def _(sp):
            for to, name in copies:
                sp.dma_start(to[:], k.ins[name]).then_inc(k.fetched_sem, 16)
            for to, name in rows:
                sp.dma_start(to[:], k.ins[name].partition_broadcast(P)).then_inc(k.fetched_sem, 16)
            k.fetched += 16 * (len(copies) + len(rows))


def fetch_mixture(k, layer):
    nc, w, ins = k.nc, k.w, k.ins
    swiglu = layer in (0, 3)
    m = SWIGLU if swiglu else GELU
    E = m.experts
    w.first = w.first_room[:, 0:2 * P * E]
    w.router = w.router_room[:, 0:HALVES * E]
    w.router_bias = w.router_bias_room[:, 0:E]
    with ExitStack() as ctx:
        block = ctx.enter_context(nc.Block())

        @block.sync
        def _(sp):
            copies = [(w.first[0:C], ins[f"f{layer}_first"]), (w.first[C:P], ins[f"f{layer}_first"]),
                      (w.second[:], ins[f"f{layer}_second"]), (w.router, ins[f"f{layer}_router"]),
                      (w.router_bias, ins[f"f{layer}_router_bias"].partition_broadcast(P))]
            if not swiglu:
                copies += [(w.bias1[:], ins[f"f{layer}_bias1"]),
                           (w.bias2[:].rearrange("p e c -> p (e c)"),
                            ins[f"f{layer}_bias2"].partition_broadcast(P))]
            for to, source in copies:
                sp.dma_start(to, source).then_inc(w.loaded, 16)
            w.all += 16 * len(copies)


def ffn(k, layer, turn):
    nc, w = k.nc, k.w
    swiglu = layer in (0, 3)
    m = SWIGLU if swiglu else GELU
    layer_norm(k, turn, 1e-5)
    with ExitStack() as ctx:
        k.parts = ctx.enter_context(nc.sbuf_tensor(f"parts{layer}", [P, HALVES, N], F32R))
        w.high = ctx.enter_context(nc.sbuf_tensor(f"high{layer}", [P, 2 * P * m.experts], F32R))
        w.low = ctx.enter_context(nc.sbuf_tensor(f"low{layer}", [P, 2 * P * m.experts], F32R))
        gates(k, k.mixtures, m, w)
        mixture(k, k.mixtures, m, w, swiglu)
        k.mixtures += 1


class Network:
    pass


class Weights:
    pass



class LayerNormSignals:
    def __init__(self, new):
        self.mean = new("ln_mean")
        self.centred = new("ln_centred")
        self.squared = new("ln_squared")
        self.var = new("ln_var")
        self.dev = new("ln_dev")
        self.scale = new("ln_scale")
        self.wide = new("ln_wide")
        self.normed = new("ln_normed")


class GateSignals:
    def __init__(self, new):
        self.logits = new("gt_logits")
        self.high = new("gt_high")
        self.w_high = new("gt_w_high")
        self.gap = new("gt_gap")
        self.exp = new("gt_exp")
        self.step = new("gt_step")


class MixtureSignals:
    def __init__(self, new):
        self.first = new("mx_first")
        self.act = new("mx_act")
        self.hidden = new("mx_hidden")
        self.second = new("mx_second")
        self.read = new("mx_read")
        self.biased = new("mx_biased")
        self.accumulated = new("mx_accumulated")
        self.summed = new("mx_summed")
        self.back = new("mx_back")
        self.added = new("mx_added")


class BatchNormSignals:
    def __init__(self, new):
        self.own = new("bn_own")
        self.both = new("bn_both")
        self.neg_var = new("bn_neg_var")
        self.dev = new("bn_dev")
        self.step = new("bn_step")


class Conv0Signals:
    def __init__(self, new):
        self.key_ps = new("c0_key_ps")
        self.key = new("c0_key")
        self.key_max = new("c0_key_max")
        self.key_exp = new("c0_key_exp")
        self.qv_ps = new("c0_qv_ps")
        self.qv = new("c0_qv")
        self.q_shift = new("c0_q_shift")
        self.q_exp = new("c0_q_exp")
        self.q_soft = new("c0_q_soft")
        self.turned_ps = new("c0_turned_ps")
        self.turned = new("c0_turned")
        self.small_ps = new("c0_small_ps")
        self.small = new("c0_small")
        self.sigmoid = new("c0_sigmoid")
        self.gate_exp = new("c0_gate_exp")
        self.out_ps = new("c0_out_ps")
        self.added = new("c0_added")
        self.step = new("c0_step")


class Conv1Signals:
    def __init__(self, new):
        self.cleared = new("c1_cleared")
        self.padded = new("c1_padded")
        self.small_ps = new("c1_small_ps")
        self.squeezed = new("c1_squeezed")
        self.logit = new("c1_logit")
        self.routing = new("c1_routing")
        self.total = new("c1_total")
        self.kernel = new("c1_kernel")
        self.out_ps = new("c1_out_ps")
        self.added = new("c1_added")
        self.step = new("c1_step")


class Conv2Signals:
    def __init__(self, new):
        self.cleared = new("c2_cleared")
        self.f_ps = new("c2_f_ps")
        self.f = new("c2_f")
        self.total = new("c2_total")
        self.g_ps = new("c2_g_ps")
        self.g = new("c2_g")
        self.taps = new("c2_taps")
        self.product = new("c2_product")
        self.far = new("c2_far")
        self.near = new("c2_near")
        self.out_ps = new("c2_out_ps")
        self.added = new("c2_added")
        self.step = new("c2_step")


class Conv3Signals:
    def __init__(self, new):
        self.cleared = new("c3_cleared")
        self.padded = new("c3_padded")
        self.off_ps = new("c3_off_ps")
        self.off = new("c3_off")
        self.turned = new("c3_turned")
        self.reach = new("c3_reach")
        self.reach_ps = new("c3_reach_ps")
        self.step = new("c3_step")
        self.y_ps = new("c3_y_ps")
        self.y = new("c3_y")
        self.own = new("c3_own")
        self.group = new("c3_group")
        self.neg_var = new("c3_neg_var")
        self.dev = new("c3_dev")
        self.affine = new("c3_affine")
        self.relu = new("c3_relu")
        self.gn_step = new("c3_gn_step")


class SampleSignals:
    def __init__(self, new, name):
        self.staged = new(f"{name}_staged")
        self.position = new(f"{name}_position")
        self.values_ps = new(f"{name}_values_ps")
        self.values = new(f"{name}_values")
        self.dist = new(f"{name}_dist")
        self.hats = new(f"{name}_hats")
        self.hatted = new(f"{name}_hatted")
        self.weights = new(f"{name}_weights")
        self.turned = new(f"{name}_turned")
        self.matrix = new(f"{name}_matrix")
        self.used = new(f"{name}_used")
        self.summed = new(f"{name}_summed")
        self.all = [self.staged, self.position, self.values_ps, self.values, self.dist, self.hats, self.hatted, self.weights, self.turned, self.matrix, self.used, self.summed]


def build(nc, ins, out, plan):
    with ExitStack() as ctx:
        def sb(name, shape, dt=F32):
            return ctx.enter_context(nc.sbuf_tensor(name, shape, dt))

        def new(name):
            return ctx.enter_context(nc.semaphore(name))

        k = Network()
        k.nc, k.ins, k.out = nc, ins, out
        k.x = sb("x", [P, N])
        k.xn = sb("xn", [P, N])
        k.gate = sb("gate", [P, HALVES * TILES * SWIGLU.experts])
        k.average = sb("average", [P, P])
        k.identity = sb("identity", [P, P])
        k.shifted = sb("shifted", [P, 2 * HALVES * LN_TILES])
        k.rows = sb("rows", [HALVES * LN_TILES, LN_TILES * P])
        k.countdown = sb("countdown", [P, SWIGLU.experts])
        k.eps = {e: sb(f"eps{i}", [P, 1]) for i, e in enumerate((1e-5, 1e-6))}
        k.x_loaded = ctx.enter_context(nc.semaphore("x_loaded"))
        k.stored = ctx.enter_context(nc.semaphore("stored"))
        k.ln = LayerNormSignals(new)
        k.gt = GateSignals(new)
        k.mx = MixtureSignals(new)
        k.mx_base = dict(expert=0, first=0, hidden=0, pair=0, biased=0, acc=0, chunk=0)
        k.w = Weights()
        k.w.first_room = sb("w_first", [P, 2 * P * SWIGLU.experts])
        k.w.second = sb("w_second", [P, C * SWIGLU.experts])
        k.w.router_room = sb("w_router", [P, HALVES * SWIGLU.experts])
        k.w.router_bias_room = sb("w_router_bias", [P, SWIGLU.experts])
        k.w.bias1 = sb("w_bias1", [P, 2 * GELU.experts])
        k.w.bias2 = sb("w_bias2", [P, GELU.experts, C])
        k.w.loaded = ctx.enter_context(nc.semaphore("w_loaded"))
        k.w.all = 0
        k.mixtures = 0
        k.fetched_sem = ctx.enter_context(nc.semaphore("fetched"))
        k.fetched = 0
        k.bn = BatchNormSignals(new)
        k.c0 = Conv0Signals(new)
        k.c1 = Conv1Signals(new)
        k.c2 = Conv2Signals(new)
        k.c3 = Conv3Signals(new)
        k.c3_steps = 0
        k.c3_near, k.c3_rest = SampleSignals(new, "near"), SampleSignals(new, "rest")
        load_inputs(k)
        turn = 0
        ready = None
        for what, layer in plan:
            if layer != ready:
                fetch_mixture(k, layer)
                ready = layer
            if what == "ffn":
                ffn(k, layer, turn)
                turn += 1
            else:
                turn = what(k, layer, turn)
        store_output(k)


def lay_out(inputs):
    f = lambda n: np.ascontiguousarray(inputs[n])
    stack = lambda a: np.concatenate([a, a], axis=0)

    def diagonal(a):
        z = np.zeros_like(a)
        return np.concatenate([np.concatenate([a, z], axis=1), np.concatenate([z, a], axis=1)])

    c = {
        "x": f("x").reshape(B, C, PIX),
        "average": diagonal(np.full((C, C), 1.0 / C, np.float32)),
        "identity": np.eye(P, dtype=np.float32),
        "rows": np.repeat(np.eye(HALVES * LN_TILES, dtype=np.float32), C, axis=1),
        "shifted": np.concatenate([np.zeros((P, 2 * LN_TILES - 2)), diagonal(np.full((C, 1), 1.0 / C)),
                                   np.zeros((P, 2 * LN_TILES))], axis=1).astype(np.float32),
        "countdown": np.broadcast_to(np.arange(SWIGLU.experts, 0, -1, dtype=np.float32), (P, SWIGLU.experts)),
    }
    p = "L0_conv_"
    c["c0_wk"] = diagonal(f(p + "wk").T)
    c["c0_wqv"] = np.concatenate([diagonal(f(p + "wq").T), diagonal(f(p + "wv").T)], axis=1)
    c["c0_bqv"] = np.concatenate([f(p + "bq"), f(p + "bq"), f(p + "bv"), f(p + "bv")])
    c["c0_cols"] = np.stack([stack(f(p + n)) for n in ("bn_gamma", "bn_beta", "bk", "b_rep")]
                            + [np.broadcast_to(f(p + "b_se"), (P,))], axis=1)
    c["c0_wrep"] = f(p + "w_rep").T.reshape(HEADS, HK, C).transpose(1, 0, 2).reshape(HK, HEADS * C)
    c["c0_fc"] = np.concatenate([f(p + n).reshape(-1) for n in
                                 ("w_fc1", "b_fc1", "w_fc2", "b_fc2", "w_se")]).reshape(1, 14)
    c["halves"] = np.tile(np.eye(C, dtype=np.float32) / HALVES, (HALVES, HALVES))
    c["quads"] = np.repeat(np.eye(HALVES * HEADS, dtype=np.float32), HK, axis=0) / (HK * HK)
    c["heads"] = diagonal(np.tile(np.eye(HK, dtype=np.float32), (HEADS, HEADS)))
    p = "L1_conv_"
    c["c1_w1"] = diagonal(f(p + "w1").T)
    c["c1_w2"] = diagonal(f(p + "w2").T)
    c["c1_wexp"] = f(p + "w_exp").reshape(-1)
    weight = f(p + "weight")
    c["c1_weight"] = stack(weight.transpose(2, 0, 3, 4, 1).reshape(C, weight.shape[0], 9 * C))
    p = "L2_conv_conv_"
    c["c2_w"] = diagonal(f(p + "w").T)
    c["c2_row"] = np.concatenate([f(p + n).reshape(-1) for n in (
        "kernel_w", "kernel_b", "kernel2_w", "kernel2_b", "k_w", "k_b", "k2_w", "k2_b")])
    p = "L2_conv_"
    c["c2_cols"] = np.stack([np.tile(f(p + n), B) for n in ("conv_b", "adap_b", "atrous_b")]
                            + [np.tile(f(p + "fuse_b"), 2 * HALVES)], axis=1)
    fw = f(p + "fuse_w").T
    near, far = np.concatenate([fw, np.zeros_like(fw)], axis=1), np.concatenate([np.zeros_like(fw), fw], axis=1)
    c["c2_fuse"] = np.stack([np.tile(diagonal(a), (IMAGES, 1)) for a in (near, far)], axis=1)
    p = "L3_conv_"
    off_w = f(p + "offset_w").reshape(2 * TAPS, C, TAPS).transpose(2, 1, 0)
    c["c3_w_off"] = np.stack([diagonal(a) for a in off_w], axis=1)
    off_b = f(p + "offset_b")
    c["c3_cols"] = np.stack([np.concatenate([off_b, off_b, np.zeros(P - 4 * TAPS, np.float32)]),
                             stack(f(p + "gn_gamma")), stack(f(p + "gn_beta"))], axis=1)
    deform = f(p + "deform_w").reshape(C, C, TAPS // TAP_GROUP, TAP_GROUP).transpose(2, 1, 3, 0)
    c["c3_w_deform"] = np.stack([diagonal(a.reshape(C, TAP_GROUP * C)) for a in deform], axis=1)
    at = np.arange(P)
    tap = np.arange(TAPS)
    base = np.stack([(at // W)[:, None] + 0 * tap[None], (at % W)[:, None] - 1 + (tap % 3)[None]], axis=2)
    c["c3_base"] = np.tile(base.reshape(P, 2 * TAPS), (1, HALVES)).astype(np.float32)
    c["c3_ints"] = np.arange(-H, H + TILE_ROWS, dtype=np.float32)
    c["pairs"] = np.kron(np.eye(P // 2), np.full((2, 2), 0.5)).astype(np.float32)
    for layer in (0, 3):
        p = f"L{layer}_ffn_"
        E = SWIGLU.experts
        first = np.stack([f(p + "w1"), f(p + "w2")], axis=1)
        c[f"f{layer}_first"] = first.transpose(2, 0, 1, 3).reshape(C, E * 2 * P)
        c[f"f{layer}_second"] = f(p + "w3").transpose(1, 0, 2).reshape(P, E * C)
        c[f"f{layer}_router"] = diagonal(f(p + "gate_w"))
        c[f"f{layer}_router_bias"] = f(p + "gate_b")
    for layer in (1, 2):
        p = f"L{layer}_ffn_"
        E = GELU.experts
        c[f"f{layer}_first"] = f(p + "W1").transpose(1, 0, 2).reshape(C, E * 2 * P)
        c[f"f{layer}_second"] = f(p + "W2").reshape(E, 2, P, C).transpose(2, 0, 1, 3).reshape(P, E * 2 * C)
        c[f"f{layer}_router"] = diagonal(f(p + "Wg"))
        c[f"f{layer}_router_bias"] = f(p + "bg")
        c[f"f{layer}_bias1"] = f(p + "b1").reshape(E, 2, P).transpose(2, 0, 1).reshape(P, E * 2)
        c[f"f{layer}_bias2"] = f(p + "b2").reshape(E * C)
    return {n: np.ascontiguousarray(a) for n, a in c.items()}



PLAN = [(conv0, 0), ("ffn", 0), (conv1, 1), ("ffn", 1), (conv2, 2), ("ffn", 2), (conv3, 3), ("ffn", 3)]


def kernel(**inputs):
    import concourse.bacc as bacc
    from concourse.bass_utils import run_bass_kernel_spmd

    arrays = lay_out(inputs)
    nc = bacc.Bacc("TRN2", target_bir_lowering=False, num_devices=1)
    ins = {name: nc.dram_tensor(f"in_{name}", a.shape, mybir.dt.from_np(a.dtype), kind="ExternalInput").ap()
           for name, a in arrays.items()}
    out = nc.dram_tensor("out_x", (B, C, PIX), F32, kind="ExternalOutput").ap()
    build(nc, ins, out, PLAN)
    result = run_bass_kernel_spmd(nc, [{f"in_{name}": a for name, a in arrays.items()}], core_ids=[0])
    return result.results[0]["out_x"].reshape(B, C, H, W)
```

```python
from contextlib import ExitStack

import numpy as np

import concourse.bass as bass
from concourse import mybir

ALU = mybir.AluOpType
ACT = mybir.ActivationFunctionType
F32 = mybir.dt.float32
F32R = mybir.dt.float32r
AX = mybir.AxisListType

P = 128
B, C, H, W = 8, 64, 32, 32
HALVES = 2
IMAGES = B // HALVES
PIX = H * W
N = IMAGES * PIX
TILES = N // P
BANK = 512

HEADS = 2
HK = C // HEADS
CM = 16
class Mixture:
    def __init__(self, experts, hidden):
        self.experts, self.hidden = experts, hidden


SWIGLU = Mixture(experts=16, hidden=128)
GELU = Mixture(experts=8, hidden=256)
CHUNK = 256
CHUNKS = N // CHUNK
SLOTS = HALVES * CHUNK // P
LOWEST = -3.0e38
LN_TILES = 4


def spread(ap, axis, count):
    shape = list(ap.shape)
    shape.insert(axis, count)
    return ap.unsqueeze(axis).broadcast_to(shape)



def layer_norm(k, turn, eps, loads, router=None):
    nc, x, xn = k.nc, k.x, k.xn
    WIDE = LN_TILES * P
    STEPS = N // WIDE
    ROWS = LN_TILES * HALVES
    t = turn * STEPS
    s, g = k.ln, k.gt
    with ExitStack() as ctx:
        def sb(name, shape):
            return ctx.enter_context(nc.sbuf_tensor(f"ln{turn}_{name}", shape, F32))

        def ps(name, shape):
            return ctx.enter_context(nc.psum_tensor(f"ln{turn}_{name}", shape, F32))
        square = sb("square", [P, 2, WIDE])
        dev = sb("dev", [ROWS, 2, P])
        scale = sb("scale", [ROWS, 2, P])
        mean = ps("mean", [P, 2, WIDE])
        var = ps("var", [ROWS, 2, BANK])
        wide = ps("wide", [P, 2, WIDE])
        if router:
            top_two, w = router
            raw = ps("raw", [P, TILES, HALVES * top_two.experts])
        block = ctx.enter_context(nc.Block())

        @block.sync
        def _(sp):
            if turn == 0:
                for j in range(1, IMAGES):
                    load_image(k, sp, j)
            for to, source, semaphore in loads:
                sp.dma_start(to, source).then_inc(semaphore, 16)

        def cols(i):
            return slice(i * WIDE, (i + 1) * WIDE)

        def staggered(*stages):
            for n in range(STEPS + len(stages) - 1):
                for behind, stage in enumerate(stages):
                    if 0 <= n - behind < STEPS:
                        stage(n - behind)

        @block.tensor
        def _(pe):
            def means(i):
                if i >= 2:
                    pe.wait_ge(s.squared, t + i - 1)
                if turn == 0:
                    pe.wait_ge(k.image_loaded[i * WIDE // PIX], 16 * HALVES)
                pe.matmul(mean[:, i % 2, :], k.centring[:], x[:, cols(i)],
                          start=True, stop=True).then_inc(s.mean, 1)

            def variances(i):
                pe.wait_ge(s.squared, t + i + 1)
                if i >= 2:
                    pe.wait_ge(s.dev, t + i - 1)
                for q in range(LN_TILES):
                    last = pe.matmul(var[:, i % 2, 0:P],
                                     k.shifted[:, ROWS - HALVES * (q + 1):2 * ROWS - HALVES * (q + 1)],
                                     square[:, i % 2, q * P:(q + 1) * P],
                                     start=(q == 0), stop=(q == LN_TILES - 1))
                last.then_inc(s.var, 1)

            def scales(i):
                pe.wait_ge(s.scale, t + i + 1)
                if i >= 2:
                    pe.wait_ge(s.normed, t + i - 1)
                for q in range(LN_TILES):
                    last = pe.matmul(wide[:, i % 2, q * P:(q + 1) * P], k.rows[:, q * P:(q + 1) * P],
                                     scale[:, i % 2, :], start=True, stop=True)
                last.then_inc(s.wide, 1)

            def route(i):
                if i == 0:
                    pe.wait_ge(w.loaded, w.all)
                pe.wait_ge(s.normed, t + i + 1)
                for q in range(i * LN_TILES, (i + 1) * LN_TILES):
                    last = pe.matmul(raw[:, q, :], xn[:, q * P:(q + 1) * P], w.router[:], start=True, stop=True)
                last.then_inc(g.logits, 1)

            if turn == 0:
                pe.wait_ge(k.constants, k.constants_all)
            staggered(means, variances, scales, *([route] if router else []))
            if turn == 0:
                pe.wait_ge(k.more_constants, 16 * 2)

        @block.scalar
        def _(act):
            def squares(i):
                act.wait_ge(s.mean, t + i + 1)
                act.copy(xn[:, cols(i)], mean[:, i % 2, :]).then_inc(s.centred, 1)
                if i >= 2:
                    act.wait_ge(s.var, t + i - 1)
                act.activation(square[:, i % 2, :], mean[:, i % 2, :], ACT.Square).then_inc(s.squared, 1)

            def deviations(i):
                act.wait_ge(s.var, t + i + 1)
                if i >= 2:
                    act.wait_ge(s.scale, t + i - 1)
                act.activation(dev[:, i % 2, :], var[:, i % 2, 0:P], ACT.Sqrt,
                               bias=k.eps[eps][0:ROWS]).then_inc(s.dev, 1)

            def highs(i):
                act.wait_ge(s.normed, t + i + 1)
                for h in range(HALVES):
                    half = slice(h * C, (h + 1) * C)
                    act.copy(k.parts[half, h, cols(i)], xn[half, cols(i)]).then_inc(g.high, 1)

            if router:
                staggered(squares, deviations, no_stage, highs)
            else:
                staggered(squares, deviations)

        @block.vector
        def _(dve):
            def scales(i):
                dve.wait_ge(s.dev, t + i + 1)
                if i >= 2:
                    dve.wait_ge(s.wide, t + i - 1)
                dve.reciprocal(scale[:, i % 2, :], dev[:, i % 2, :]).then_inc(s.scale, 1)

            def norm(i):
                dve.wait_ge(s.centred, t + i + 1)
                dve.wait_ge(s.wide, t + i + 1)
                dve.tensor_tensor(xn[:, cols(i)], xn[:, cols(i)], wide[:, i % 2, :],
                                  ALU.mult).then_inc(s.normed, 1)

            def lows(i):
                for h in range(HALVES):
                    half, other = slice(h * C, (h + 1) * C), slice((1 - h) * C, (2 - h) * C)
                    dve.wait_ge(g.high, (k.mixtures * STEPS + i) * HALVES + h + 1)
                    dve.tensor_tensor(k.parts[other, h, cols(i)], xn[half, cols(i)],
                                      k.parts[half, h, cols(i)].bitcast(F32), ALU.subtract)

            if router:
                staggered(scales, norm, lows)
                dve.wait_ge(g.logits, (k.mixtures + 1) * STEPS)
                dve.tensor_tensor(top_two.logits[:],
                                  raw[:].rearrange("p t (h e) -> p (t h) e", e=top_two.experts),
                                  spread(w.router_bias[:], 1, top_two.tiles), ALU.add)
            else:
                staggered(scales, norm)

        if router:
            @block.gpsimd
            def _(pool):
                size = w.first.shape[1]
                pool.wait_ge(w.loaded, w.all)
                pool.tensor_copy(w.high[:, 0:size], w.first[:]).then_inc(g.w_high, 1)
                pool.wait_ge(g.w_high, k.mixtures + 1)
                pool.tensor_tensor(w.low[:, 0:size], w.first[:], w.high[:, 0:size].bitcast(F32), ALU.subtract)


def no_stage(i):
    pass



class TopTwo:

    STEPS = 17

    def __init__(self, k, ctx, m):
        def sb(name, shape):
            return ctx.enter_context(k.nc.sbuf_tensor(f"gt{k.mixtures}_{name}", shape, F32))
        self.k, self.experts = k, m.experts
        T = self.tiles = HALVES * TILES
        self.logits, self.equal, self.rank = (sb(n, [P, T, m.experts]) for n in ("logits", "equal", "rank"))
        self.one_hot = [sb(f"one_hot{i}", [P, T, m.experts]) for i in range(2)]
        self.best = [sb(f"best{i}", [P, T]) for i in range(2)]
        self.place, self.small = sb("place", [P, T]), sb("small", [P, 4, T])
        self.step = k.mixtures * self.STEPS

    def done(self, dve, ins):
        self.step += 1
        ins.then_inc(self.k.gt.step, 1)
        dve.wait_ge(self.k.gt.step, self.step)

    def pick(self, dve, i):
        k, E, T = self.k, self.experts, self.tiles
        logits, equal, rank, place, hot, best = (self.logits, self.equal, self.rank, self.place,
                                                 self.one_hot[i], self.best[i])
        self.done(dve, dve.tensor_reduce(best[:], logits[:], AX.X, ALU.max))
        self.done(dve, dve.tensor_tensor(equal[:], logits[:], spread(best[:], 2, E), ALU.is_equal))
        self.done(dve, dve.tensor_tensor(rank[:], equal[:], spread(k.countdown[:, 0:E], 1, T), ALU.mult))
        self.done(dve, dve.tensor_reduce(place[:], rank[:], AX.X, ALU.max))
        self.done(dve, dve.tensor_tensor(hot[:], rank[:], spread(place[:], 2, E), ALU.is_equal))
        if i == 0:
            self.done(dve, dve.scalar_tensor_tensor(out=logits[:], in0=hot[:], scalar=LOWEST, in1=logits[:],
                                                    op0=ALU.mult, op1=ALU.add))
        else:
            dve.tensor_tensor(self.small[:, 0, :], best[:], self.best[0][:], ALU.subtract).then_inc(k.gt.gap, 1)

    def exponential(self, act):
        act.wait_ge(self.k.gt.gap, self.k.mixtures + 1)
        act.activation(self.small[:, 1, :], self.small[:, 0, :], ACT.Exp).then_inc(self.k.gt.exp, 1)

    def gates(self, dve):
        k, E, T, small = self.k, self.experts, self.tiles, self.small
        dve.wait_ge(k.gt.exp, k.mixtures + 1)
        self.done(dve, dve.tensor_scalar(small[:, 2, :], small[:, 1, :], 1.0, None, ALU.add))
        self.done(dve, dve.reciprocal(small[:, 3, :], small[:, 2, :]))
        self.done(dve, dve.tensor_tensor(small[:, 2, :], small[:, 1, :], small[:, 3, :], ALU.mult))
        self.done(dve, dve.tensor_tensor(self.equal[:], self.one_hot[0][:], spread(small[:, 3, :], 2, E), ALU.mult))
        self.done(dve, dve.tensor_tensor(self.rank[:], self.one_hot[1][:], spread(small[:, 2, :], 2, E), ALU.mult))
        self.done(dve, dve.tensor_tensor(k.gate[:, 0:T * E].rearrange("p (t e) -> p t e", e=E), self.equal[:],
                                         self.rank[:], ALU.add))
        assert self.step == (k.mixtures + 1) * self.STEPS


def mixture(k, turn, m, w, swiglu, top_two, last_layer):
    nc, x = k.nc, k.x
    E, HID = m.experts, m.hidden
    COLS = HALVES * CHUNK
    F = HID // P
    PAIRS = E // 2
    RING = 4
    s = k.mx
    eb, fb, hb, pb, cb = (k.mx_base[n] for n in ("expert", "first", "hidden", "pair", "chunk"))
    bb = k.mx_base["biased"]
    with ExitStack() as ctx:
        def sb(name, shape, dt=F32):
            return ctx.enter_context(nc.sbuf_tensor(f"mx{turn}_{name}", shape, dt))

        def ps(name, shape):
            return ctx.enter_context(nc.psum_tensor(f"mx{turn}_{name}", shape, F32))
        act_out = sb("act_out", [P, RING, F, COLS])
        hidden = sb("hidden", [P, RING, COLS]) if swiglu else act_out
        weighted = sb("weighted", [P, 2, 2, SLOTS, C])
        biased = None if swiglu else sb("biased", [P, 2, SLOTS, C])
        total = sb("total", [P, 2, SLOTS, C])
        summed = sb("summed", [P, SLOTS, C])
        first = ps("first", [P, 2, 2, COLS])
        second = ps("second", [P, 2, 2, SLOTS, C])
        back = ps("back", [P, CHUNK])
        gate = k.gate[:, 0:HALVES * TILES * E].rearrange("p (t e) -> p t e", e=E)
        block = ctx.enter_context(nc.Block())

        def hi(e, f):
            return w.high[:, (e * 2 + f) * P:(e * 2 + f + 1) * P]

        def lo(e, f):
            return w.low[:, (e * 2 + f) * P:(e * 2 + f + 1) * P]

        def w2(e, f):
            return w.second[:, (e * F + f) * C:(e * F + f + 1) * C]

        @block.tensor
        def _(pe):
            def first_layer(i, e):
                n = i * E + e
                tokens = k.parts[:, :, bass.ds(i * CHUNK, CHUNK)]
                for f in range(2):
                    if not (isinstance(n, int) and n < 2):
                        if f == 0 or not swiglu:
                            pe.wait_ge(s.act, fb + (n - 2) * (1 if swiglu else 2) + (1 if swiglu else f + 1))
                        else:
                            pe.wait_ge(s.hidden, hb + n - 1)
                    pe.matmul(first[:, e % 2, f, :], hi(e, f), tokens, start=True, stop=False)
                    pe.matmul(first[:, e % 2, f, :], lo(e, f), tokens,
                              start=False, stop=True).then_inc(s.first, 1)

            def second_layer(i, e):
                n = i * E + e
                if swiglu:
                    pe.wait_ge(s.hidden, hb + n + 1)
                else:
                    pe.wait_ge(s.act, fb + 2 * n + 2)
                pair = i * PAIRS + e // 2
                if e % 2 == 0 and not (isinstance(pair, int) and pair < 2):
                    pe.wait_ge(s.read if swiglu else s.biased, (pb if swiglu else bb) + pair - 1)
                for q in range(SLOTS):
                    h, t = q // (SLOTS // HALVES), q % (SLOTS // HALVES)
                    for f in range(F):
                        tile = hidden[:, e % RING, q * P:(q + 1) * P] if swiglu else \
                            hidden[:, e % RING, f, q * P:(q + 1) * P]
                        last = pe.matmul(second[:, (e // 2) % 2, e % 2, t * HALVES + h, :], tile,
                                         w2(e, f), start=(f == 0), stop=(f == F - 1))
                last.then_inc(s.second, 1)

            def turn_back(i):
                pe.wait_ge(s.summed, cb + i + 1)
                if not (isinstance(i, int) and i < 1):
                    pe.wait_ge(s.added, cb + i)
                for t in range(CHUNK // P):
                    last = pe.transpose(back[:, t * P:(t + 1) * P],
                                        summed[:, t * HALVES:(t + 1) * HALVES, :].rearrange("p h c -> p (h c)"),
                                        k.identity[:])
                last.then_inc(s.back, 1)

            def step(i, before):
                for e in range(E):
                    first_layer(i, e)
                    if e > 0:
                        second_layer(i, e - 1)
                    elif before is not None:
                        second_layer(before, E - 1)
                    if e == 3 and before is not None:
                        turn_back(before)

            step(0, None)
            with pe.Fori(1, CHUNKS, 1) as i:
                step(i, i - 1)
            second_layer(CHUNKS - 1, E - 1)
            turn_back(CHUNKS - 1)

        @block.scalar
        def _(act):
            def step(i, first_step):
                for e in range(E):
                    n = i * E + e
                    if first_step and e == (4 if swiglu else 3):
                        top_two.exponential(act)
                    if swiglu:
                        act.wait_ge(s.first, eb + 2 * n + 1)
                        if not (first_step and e < RING):
                            act.wait_ge(s.hidden, hb + n - RING + 1)
                        act.activation(act_out[:, e % RING, 0, :], first[:, e % 2, 0, :],
                                       ACT.Silu).then_inc(s.act, 1)
                    else:
                        for f in range(F):
                            act.wait_ge(s.first, eb + 2 * n + f + 1)
                            if not (first_step and e < RING) and f == 0:
                                act.wait_ge(s.second, pb * 2 + n - RING + 1)
                            act.activation(act_out[:, e % RING, f, :], first[:, e % 2, f, :], ACT.Gelu,
                                           bias=w.bias1[:, e * F + f:e * F + f + 1]).then_inc(s.act, 1)

            step(0, True)
            with act.Fori(1, CHUNKS, 1) as i:
                step(i, False)

        @block.vector
        def _(dve):
            def product(i, e):
                n = i * E + e
                dve.wait_ge(s.act, fb + n + 1)
                dve.wait_ge(s.first, eb + 2 * n + 2)
                if not (isinstance(n, int) and n < RING):
                    dve.wait_ge(s.second, pb * 2 + n - RING + 1)
                dve.tensor_tensor(hidden[:, e % RING, :], first[:, e % 2, 1, :], act_out[:, e % RING, 0, :],
                                  ALU.mult).then_inc(s.hidden, 1)

            def weigh(i, p):
                n = i * PAIRS + p
                dve.wait_ge(s.second, pb * 2 + 2 * n + 2)
                sums = second[:, p % 2, :, :, :]
                if not swiglu:
                    if not (isinstance(n, int) and n < 1):
                        dve.wait_ge(s.read, pb + n)
                    dve.tensor_tensor(biased[:], sums, spread(w.bias2[:, 2 * p:2 * p + 2, :], 2, SLOTS),
                                      ALU.add).then_inc(s.biased, 1)
                    dve.wait_ge(s.biased, bb + n + 1)
                    sums = biased[:]
                out = total if p == 0 else weighted[:, p % 2, :, :, :]
                if p == 0:
                    if not (isinstance(i, int) and i < 1):
                        dve.wait_ge(s.summed, cb + i)
                elif not (isinstance(n, int) and n < 3):
                    dve.wait_ge(s.accumulated, k.mx_base["acc"] + i * (PAIRS - 1) + max(p - 2, 0))
                tiles = gate[:, bass.ds(i * SLOTS, SLOTS), 2 * p:2 * p + 2].rearrange("p t e -> p e t")
                dve.tensor_tensor(out[:] if p == 0 else out, sums, spread(tiles, 3, C),
                                  ALU.mult).then_inc(s.read, 1)

            def add(i):
                dve.wait_ge(s.back, cb + i + 1)
                place = x[:, bass.ds(i * CHUNK, CHUNK)]
                dve.tensor_tensor(place, place, back[:], ALU.add).then_inc(s.added, 1)

            def step(i, before):
                for e in range(E):
                    if swiglu:
                        product(i, e)
                    if e % 2 == 0:
                        if e > 0:
                            weigh(i, e // 2 - 1)
                        else:
                            weigh(before, PAIRS - 1)
                    if e == 4:
                        add(before)

            def first_step():
                for e in range(E):
                    if swiglu:
                        product(0, e)
                    if e == 1:
                        top_two.pick(dve, 0)
                    if e == 2:
                        top_two.pick(dve, 1)
                    if e == 3:
                        top_two.gates(dve)
                        weigh(0, 0)
                    if e >= 4 and e % 2 == 0:
                        weigh(0, e // 2 - 1)

            first_step()
            with dve.Fori(1, CHUNKS, 1) as i:
                step(i, i - 1)
            weigh(CHUNKS - 1, PAIRS - 1)
            add(CHUNKS - 1)

        if last_layer:
            @block.sync
            def _(sp):
                for j in range(IMAGES):
                    sp.wait_ge(s.added, cb + (j + 1) * PIX // CHUNK)
                    store_image(k, sp, j)
                sp.wait_ge(k.stored, 16 * HALVES * IMAGES)

        @block.gpsimd
        def _(pool):
            ab = k.mx_base["acc"]

            def step(i):
                for p in range(1, PAIRS):
                    pool.wait_ge(s.read, pb + i * PAIRS + p + 1)
                    if not (isinstance(i, int) and i == 0 and p == 1):
                        pool.wait_ge(s.accumulated, ab + i * (PAIRS - 1) + p - 1)
                    pool.tensor_tensor(total[:], total[:], weighted[:, p % 2, :, :, :],
                                       ALU.add).then_inc(s.accumulated, 1)
                pool.wait_ge(s.accumulated, ab + (i + 1) * (PAIRS - 1))
                if not (isinstance(i, int) and i < 1):
                    pool.wait_ge(s.back, cb + i)
                pool.tensor_tensor(summed[:], total[:, 0], total[:, 1], ALU.add).then_inc(s.summed, 1)

            step(0)
            with pool.Fori(1, CHUNKS, 1) as i:
                step(i)
    k.mx_base["expert"] += 2 * E * CHUNKS
    k.mx_base["first"] += E * CHUNKS * (1 if swiglu else 2)
    k.mx_base["hidden"] += E * CHUNKS if swiglu else 0
    k.mx_base["pair"] += PAIRS * CHUNKS
    k.mx_base["biased"] += 0 if swiglu else PAIRS * CHUNKS
    k.mx_base["acc"] += (PAIRS - 1) * CHUNKS
    k.mx_base["chunk"] += CHUNKS



def conv0(k, layer, turn):
    nc, x, xn, s = k.nc, k.x, k.xn, k.c0
    QUADS = HALVES * HEADS
    GROUP = 4
    GROUPS = TILES // GROUP
    with ExitStack() as ctx:
        def sb(name, shape):
            return ctx.enter_context(nc.sbuf_tensor("c0_" + name, shape, F32))
        wk, wqv, cols = sb("wk", [P, P]), sb("wqv", [P, 2 * P]), sb("cols", [P, 5])
        bqv, wrep, fc = sb("bqv", [P, 2 * P]), sb("wrep", [HK, HEADS * C]), sb("fc", [1, 14])
        halves, quads, heads = sb("halves", [P, P]), sb("quads", [P, QUADS]), sb("heads", [P, P])
        gamma, beta, bk, b_rep, b_se = (cols[:, i:i + 1] for i in range(5))
        loads = layer_loads(k, [(wk, "c0_wk"), (wqv, "c0_wqv"), (cols, "c0_cols"), (wrep, "c0_wrep"), (fc, "c0_fc"),
                  (halves, "halves"), (quads, "quads"), (heads, "heads")], [(bqv, "c0_bqv")])
        layer_norm(k, turn, 1e-6, loads)
        batch_norm(k, halves, gamma, beta)

        key = sb("key", [P, N])
        qv = sb("qv", [P, TILES, 2 * P])
        key_t = sb("key_t", [P, TILES, P])
        query = sb("query", [P, N])
        key_max, key_sum, key_scale = sb("key_max", [P, IMAGES]), sb("key_sum", [P, IMAGES]), sb("key_scale", [P, IMAGES])
        q_max, q_sum = sb("q_max", [P, TILES, QUADS]), sb("q_sum", [P, TILES, QUADS])
        context, rows = sb("context", [P, IMAGES, HK]), sb("rows", [P, IMAGES])
        tiny = sb("tiny", [1, 8, 2 * HALVES * IMAGES * HEADS])
        gate_row = sb("gate_row", [1, IMAGES * P])
        context_t = sb("context_t", [HK, IMAGES, P])
        matrix = sb("matrix", [P, IMAGES, P])
        ps = ctx.enter_context(nc.psum_tensor("c0_ps", [P, 8, BANK], F32))
        key_ps = ps[:, 0:2, :]
        block = ctx.enter_context(nc.Block())

        def q_quarter(r):
            return qv[:, r * 8:(r + 1) * 8, 0:P].rearrange("p t (g c) -> p t g c", c=HK)

        @block.tensor
        def _(pe):
            for c in range(N // BANK):
                if c >= 2:
                    pe.wait_ge(s.key, c - 1)
                pe.matmul(ps[:, c % 2, :], wk[:], xn[:, c * BANK:(c + 1) * BANK],
                          start=True, stop=True).then_inc(s.key_ps, 1)
            for g in range(GROUPS):
                if g >= 2:
                    pe.wait_ge(s.qv, g - 1)
                for t in range(GROUP):
                    tile = g * GROUP + t
                    last = pe.matmul(ps[:, 2 + 2 * (g % 2) + t // 2, (t % 2) * 2 * P:(t % 2 + 1) * 2 * P],
                                     xn[:, tile * P:(tile + 1) * P], wqv[:], start=True, stop=True)
                last.then_inc(s.qv_ps, 1)
            for g in range(2 * GROUPS):
                if g < GROUPS:
                    pe.wait_ge(s.key_exp, g // 2 + 1)
                else:
                    pe.wait_ge(s.q_soft, (g - GROUPS) // 2 + 1)
                if g >= 2:
                    pe.wait_ge(s.turned, g - 1)
                for t in range(GROUP):
                    tile = (g % GROUPS) * GROUP + t
                    source = key[:, tile * P:(tile + 1) * P] if g < GROUPS else qv[:, tile, 0:P]
                    last = pe.transpose(ps[:, 6 + g % 2, t * P:(t + 1) * P], source, k.identity[:])
                last.then_inc(s.turned_ps, 1)
                if g == GROUPS + 1:
                    pe.wait_ge(s.turned, GROUPS)
                    pe.wait_ge(s.key, N // BANK)
                    for j in range(IMAGES):
                        for t in range(PIX // P):
                            tile = j * (PIX // P) + t
                            last = pe.matmul(ps[:, 0, j * P:(j + 1) * P], key_t[:, tile, :],
                                             qv[:, tile, P:2 * P], start=(t == 0), stop=(t == PIX // P - 1))
                    last.then_inc(s.small_ps, 1)
            pe.wait_ge(s.small, 1)
            for j in range(IMAGES):
                last = pe.matmul(ps[0:1, 1, j * QUADS:(j + 1) * QUADS], rows[:, j:j + 1], quads[:],
                                 start=True, stop=True)
            last.then_inc(s.small_ps, 1)
            pe.wait_ge(s.small, 2)
            for j in range(IMAGES):
                last = pe.matmul(ps[:, 1, 32 + j:33 + j], gate_row[:, j * P:(j + 1) * P],
                                 k.identity[0:1, 0:1], start=True, stop=True)
            last.then_inc(s.small_ps, 1)
            pe.wait_ge(s.small, 3)
            for j in range(IMAGES):
                last = pe.matmul(ps[0:HK, 2, j * P:(j + 1) * P], context[:, j, :], heads[:],
                                 start=True, stop=True)
            last.then_inc(s.small_ps, 1)
            pe.wait_ge(s.small, 4)
            for g in range(QUADS):
                for j in range(IMAGES):
                    last = pe.matmul(ps[g * HK:(g + 1) * HK, 3, j * C:(j + 1) * C],
                                     context_t[:, j, g * HK:(g + 1) * HK],
                                     wrep[:, (g % HEADS) * C:(g % HEADS + 1) * C], start=True, stop=True)
            last.then_inc(s.small_ps, 1)
            pe.wait_ge(s.small, 5)
            pe.wait_ge(s.turned, 2 * GROUPS)
            for c in range(N // BANK):
                if c >= 2:
                    pe.wait_ge(s.added, c - 1)
                pe.matmul(ps[:, 6 + c % 2, :], matrix[:, c // 2, :], query[:, c * BANK:(c + 1) * BANK],
                          start=True, stop=True).then_inc(s.out_ps, 1)

        @block.scalar
        def _(act):
            for c in range(N // BANK):
                act.wait_ge(s.key_ps, c + 1)
                act.activation(key[:, c * BANK:(c + 1) * BANK], ps[:, c % 2, :], ACT.Identity,
                               bias=bk).then_inc(s.key, 1)
            for j in range(IMAGES):
                act.wait_ge(s.key_max, j + 1)
                act.activation(key[:, j * PIX:(j + 1) * PIX], key[:, j * PIX:(j + 1) * PIX], ACT.Exp,
                               bias=key_max[:, j:j + 1],
                               accum_out=key_sum[:, j:j + 1]).then_inc(s.key_exp, 1)
            for r in range(4):
                act.wait_ge(s.q_shift, r + 1)
                act.activation(q_quarter(r), q_quarter(r), ACT.Exp).then_inc(s.q_exp, 1)
            for g in range(2 * GROUPS):
                act.wait_ge(s.turned_ps, g + 1)
                to = (key_t[:, g * GROUP:(g + 1) * GROUP, :].rearrange("p t c -> p (t c)") if g < GROUPS
                      else query[:, (g - GROUPS) * BANK:(g - GROUPS + 1) * BANK])
                act.copy(to, ps[:, 6 + g % 2, :]).then_inc(s.turned, 1)
            act.wait_ge(s.sigmoid, 1)
            act.activation(tiny[:, 5, 0:16], tiny[:, 4, 0:16], ACT.Exp, scale=-1.0).then_inc(s.gate_exp, 1)

        @block.vector
        def _(dve):
            step = [0]

            def done(ins):
                step[0] += 1
                ins.then_inc(s.step, 1)
                dve.wait_ge(s.step, step[0])

            dve.memset(matrix[:], 0.0)
            for j in range(IMAGES):
                dve.wait_ge(s.key, 2 * (j + 1))
                dve.tensor_reduce(key_max[:, j:j + 1], key[:, j * PIX:(j + 1) * PIX], AX.X, ALU.max,
                                  negate=True).then_inc(s.key_max, 1)
            for g in range(GROUPS):
                dve.wait_ge(s.qv_ps, g + 1)
                b = 2 + 2 * (g % 2)
                dve.tensor_tensor(qv[:, g * GROUP:(g + 1) * GROUP, :],
                                  ps[:, b:b + 2, :].rearrange("p b (t c) -> p (b t) c", t=2),
                                  spread(bqv[:], 1, GROUP), ALU.add).then_inc(s.qv, 1)
            for r in range(4):
                dve.wait_ge(s.qv, 2 * (r + 1))
                done(dve.tensor_reduce(q_max[:, r * 8:(r + 1) * 8, :], q_quarter(r), AX.X, ALU.max))
                dve.tensor_tensor(q_quarter(r), q_quarter(r), spread(q_max[:, r * 8:(r + 1) * 8, :], 3, HK),
                                  ALU.subtract).then_inc(s.q_shift, 1)
            for r in range(4):
                dve.wait_ge(s.q_exp, r + 1)
                done(dve.tensor_reduce(q_sum[:, r * 8:(r + 1) * 8, :], q_quarter(r), AX.X, ALU.add))
                done(dve.reciprocal(q_max[:, r * 8:(r + 1) * 8, :], q_sum[:, r * 8:(r + 1) * 8, :]))
                dve.tensor_tensor(q_quarter(r), q_quarter(r), spread(q_max[:, r * 8:(r + 1) * 8, :], 3, HK),
                                  ALU.mult).then_inc(s.q_soft, 1)
            dve.wait_ge(s.key_exp, IMAGES)
            done(dve.reciprocal(key_scale[:], key_sum[:]))
            dve.wait_ge(s.small_ps, 1)
            product = ps[:, 0, :].rearrange("p (j c) -> p j c", c=P)
            for g in range(QUADS):
                q = slice(g * HK, (g + 1) * HK)
                last = dve.tensor_tensor(context[q], product[q, :, q], spread(key_scale[q, :], 2, HK), ALU.mult)
            done(last)
            dve.tensor_reduce(rows[:], context[:], AX.X, ALU.add).then_inc(s.small, 1)
            dve.wait_ge(s.small_ps, 2)
            BT = HALVES * IMAGES
            done(dve.tensor_copy(tiny[:, 0, 0:16], ps[0:1, 1, 0:16]))
            source = tiny[:, 0, 0:16]
            for i, (wo, bo) in enumerate(((0, 4), (6, 10))):
                w4 = fc[:, wo:wo + 4].rearrange("p (m n) -> p m n", n=HEADS)
                prod = tiny[:, 1, 0:32].rearrange("p (t m n) -> p t m n", m=HEADS, n=HEADS)
                done(dve.tensor_tensor(prod, spread(source.rearrange("p (t n) -> p t n", n=HEADS), 2, HEADS),
                                       spread(w4, 1, BT), ALU.mult))
                out = tiny[:, 2 + i, 0:16].rearrange("p (t m) -> p t m", m=HEADS)
                done(dve.tensor_reduce(out, prod, AX.X, ALU.add))
                ins = dve.tensor_tensor(tiny[:, 4 if i else 6, 0:16].rearrange("p (t m) -> p t m", m=HEADS),
                                        out, spread(fc[:, bo:bo + 2], 1, BT), ALU.add)
                if i == 0:
                    done(ins)
                    done(dve.tensor_scalar(tiny[:, 7, 0:16], tiny[:, 6, 0:16], 0.0, None, ALU.max))
                    source = tiny[:, 7, 0:16]
                else:
                    ins.then_inc(s.sigmoid, 1)
            dve.wait_ge(s.gate_exp, 1)
            done(dve.tensor_scalar(tiny[:, 6, 0:16], tiny[:, 5, 0:16], 1.0, None, ALU.add))
            done(dve.reciprocal(tiny[:, 7, 0:16], tiny[:, 6, 0:16]))
            done(dve.tensor_tensor(tiny[:, 1, 0:16].rearrange("p (t n) -> p t n", n=HEADS),
                                   tiny[:, 7, 0:16].rearrange("p (t n) -> p t n", n=HEADS),
                                   spread(fc[:, 12:14], 1, BT), ALU.mult))
            dve.tensor_copy(gate_row[:].rearrange("p (t c) -> p t c", c=HK),
                            spread(tiny[:, 1, 0:16], 2, HK)).then_inc(s.small, 1)
            dve.wait_ge(s.small_ps, 3)
            dve.tensor_tensor(context[:], context[:], spread(ps[:, 1, 32:32 + IMAGES], 2, HK),
                              ALU.mult).then_inc(s.small, 1)
            dve.wait_ge(s.small_ps, 4)
            dve.tensor_scalar(context_t[:].rearrange("p j c -> p (j c)"), ps[0:HK, 2, :], b_se[0:HK], None,
                              ALU.add).then_inc(s.small, 1)
            dve.wait_ge(s.small_ps, 5)
            for h in range(HALVES):
                q = slice(h * C, (h + 1) * C)
                last = dve.tensor_copy(matrix[q, :, q],
                                       ps[q, 3, 0:IMAGES * C].rearrange("p (j c) -> p j c", c=C))
            last.then_inc(s.small, 1)
            for c in range(N // BANK):
                dve.wait_ge(s.out_ps, c + 1)
                place = x[:, c * BANK:(c + 1) * BANK]
                dve.scalar_tensor_tensor(out=place, in0=ps[:, 6 + c % 2, :], scalar=b_rep, in1=place,
                                         op0=ALU.add, op1=ALU.add).then_inc(s.added, 1)
    return turn + 1


def batch_norm(k, halves, gamma, beta):
    nc, xn, s = k.nc, k.xn, k.bn
    with ExitStack() as ctx:
        stats = ctx.enter_context(nc.sbuf_tensor("bn_stats", [P, N // BANK, 6], F32))
        own = ctx.enter_context(nc.sbuf_tensor("bn_own", [P, 4], F32))
        both = ctx.enter_context(nc.sbuf_tensor("bn_both", [P, 8], F32))
        ps = ctx.enter_context(nc.psum_tensor("bn_ps", [P, 2], F32))
        block = ctx.enter_context(nc.Block())

        @block.tensor
        def _(pe):
            pe.wait_ge(s.own, 1)
            pe.wait_ge(k.fetched_sem, k.fetched)
            pe.matmul(ps[:], halves[:], own[:, 0:2], start=True, stop=True).then_inc(s.both, 1)

        @block.scalar
        def _(act):
            act.wait_ge(s.neg_var, 1)
            act.activation(both[:, 3:4], both[:, 2:3], ACT.Sqrt, bias=k.eps[1e-5][:],
                           scale=-1.0).then_inc(s.dev, 1)

        @block.vector
        def _(dve):
            step = [0]

            def done(ins):
                step[0] += 1
                ins.then_inc(s.step, 1)
                dve.wait_ge(s.step, step[0])

            dve.wait_ge(k.fetched_sem, k.fetched)
            for c in range(N // BANK):
                last = dve.bn_stats(stats[:, c, :], xn[:, c * BANK:(c + 1) * BANK])
            done(last)
            done(dve.bn_aggr(own[:, 2:4], stats[:]))
            dve.tensor_copy(own[:, 0:1], own[:, 2:3])
            dve.scalar_tensor_tensor(out=own[:, 1:2], in0=own[:, 2:3], scalar=own[:, 2:3], in1=own[:, 3:4],
                                     op0=ALU.mult, op1=ALU.add).then_inc(s.own, 1)
            dve.wait_ge(s.both, 1)
            done(dve.tensor_copy(both[:, 0:2], ps[:]))
            dve.scalar_tensor_tensor(out=both[:, 2:3], in0=both[:, 0:1], scalar=both[:, 0:1], in1=both[:, 1:2],
                                     op0=ALU.mult, op1=ALU.subtract).then_inc(s.neg_var, 1)
            dve.wait_ge(s.dev, 1)
            done(dve.reciprocal(both[:, 4:5], both[:, 3:4]))
            done(dve.tensor_tensor(both[:, 5:6], both[:, 4:5], gamma, ALU.mult))
            done(dve.tensor_tensor(both[:, 6:7], both[:, 0:1], both[:, 5:6], ALU.mult))
            done(dve.tensor_tensor(both[:, 7:8], beta, both[:, 6:7], ALU.subtract))
            dve.tensor_scalar(xn[:], xn[:], both[:, 5:6], both[:, 7:8], ALU.mult, ALU.add)



def conv1(k, layer, turn):
    nc, x, xn, s = k.nc, k.x, k.xn, k.c1
    EXPERTS, RED, POOL, TAPS = 8, 16, 4, 9
    CELL = H // POOL
    CELLS = POOL * POOL
    PAD = W + 2
    HALF = H // 2
    KERNEL = TAPS * C
    RING = 4
    with ExitStack() as ctx:
        def sb(name, shape):
            return ctx.enter_context(nc.sbuf_tensor("c1_" + name, shape, F32))
        w1, w2, average = sb("w1", [P, HALVES * RED]), sb("w2", [HALVES * RED, P]), sb("average", [P, P])
        wexp, weight = sb("wexp", [P, EXPERTS * CELLS]), sb("weight", [P, EXPERTS, KERNEL])
        loads = layer_loads(k, [(average, "average"), (w1, "c1_w1"), (w2, "c1_w2"), (weight, "c1_weight")], [(wexp, "c1_wexp")])
        layer_norm(k, turn, 1e-6, loads)
        padded = sb("padded", [P, IMAGES, PAD, PAD])
        row_sum, cells = sb("row_sum", [P, IMAGES * H * POOL]), sb("cells", [P, IMAGES * CELLS])
        total, squeezed = sb("total", [P, IMAGES]), sb("squeezed", [HALVES * RED, IMAGES])
        cell_mean, product = sb("cell_mean", [P, IMAGES, CELLS]), sb("product", [P, IMAGES, EXPERTS, CELLS])
        expert = sb("expert", [P, IMAGES, EXPERTS])
        routing = sb("routing", [P, IMAGES, EXPERTS])
        mixed = sb("mixed", [P, IMAGES, KERNEL])
        kernel = sb("kernel", [P, IMAGES, TAPS, P])
        ps = ctx.enter_context(nc.psum_tensor("c1_ps", [P, RING, BANK], F32))
        tiny = ctx.enter_context(nc.psum_tensor("c1_tiny", [P, BANK], F32))
        block = ctx.enter_context(nc.Block())
        image = xn[:].rearrange("p (j y x) -> p j y x", j=IMAGES, y=H)

        def by_tap(a):
            return a.rearrange("p (t c) -> p t c", c=C)

        @block.gpsimd
        def _(pool):
            pool.memset(padded[:], 0.0).then_inc(s.cleared, 1)
            pool.memset(kernel[:], 0.0).then_inc(s.cleared, 1)

        @block.scalar
        def _(act):
            act.wait_ge(s.cleared, 1)
            for j in range(IMAGES):
                act.copy(padded[:, j, 1:1 + H, 1:1 + W], image[:, j]).then_inc(s.padded, 1)
            act.wait_ge(s.small_ps, 1)
            act.activation(squeezed[:], tiny[0:HALVES * RED, 0:IMAGES], ACT.Relu,
                           scale=1.0 / PIX).then_inc(s.squeezed, 1)
            act.wait_ge(s.logit, 1)
            act.activation(routing[:], expert[:], ACT.Sigmoid).then_inc(s.routing, 1)

        @block.tensor
        def _(pe):
            pe.wait_ge(k.fetched_sem, k.fetched)
            pe.wait_ge(s.total, 1)
            pe.matmul(tiny[0:HALVES * RED, 0:IMAGES], w1[:], total[:], start=True, stop=True).then_inc(s.small_ps, 1)
            pe.wait_ge(s.squeezed, 1)
            pe.matmul(tiny[:, 0:IMAGES], w2[:], squeezed[:], start=True, stop=True)
            pe.matmul(tiny[:, 64:128], average[:], cells[:], start=True, stop=True).then_inc(s.small_ps, 1)
            for c in range(2 * IMAGES):
                j, y = c // 2, (c % 2) * HALF
                pe.wait_ge(s.padded, j + 1)
                pe.wait_ge(s.kernel, j + 1)
                if c >= RING:
                    pe.wait_ge(s.added, c - RING + 1)
                for t in range(TAPS):
                    last = pe.matmul(ps[:, c % RING, :], kernel[:, j, t, :],
                                     padded[:, j, y + t // 3:y + t // 3 + HALF, t % 3:t % 3 + W],
                                     start=(t == 0), stop=(t == TAPS - 1))
                last.then_inc(s.out_ps, 1)

        @block.vector
        def _(dve):
            step = [0]

            def done(ins):
                step[0] += 1
                ins.then_inc(s.step, 1)
                dve.wait_ge(s.step, step[0])

            done(dve.tensor_reduce(row_sum[:], xn[:].rearrange("p (n x) -> p n x", x=CELL), AX.X, ALU.add))
            done(dve.tensor_reduce(cells[:].rearrange("p (j q) -> p j q", q=POOL),
                                   row_sum[:].rearrange("p (j y q) -> p j q y", y=CELL, q=POOL), AX.X, ALU.add))
            dve.tensor_reduce(total[:], cells[:].rearrange("p (j c) -> p j c", c=CELLS), AX.X,
                              ALU.add).then_inc(s.total, 1)
            dve.wait_ge(s.small_ps, 2)
            done(dve.tensor_scalar(cell_mean[:].rearrange("p j c -> p (j c)"), tiny[:, 64:128],
                                   1.0 / (CELL * CELL), None, ALU.mult))
            dve.wait_ge(k.fetched_sem, k.fetched)
            done(dve.tensor_tensor(product[:], spread(cell_mean[:], 2, EXPERTS),
                                   spread(wexp[:].rearrange("p (k c) -> p k c", c=CELLS), 1, IMAGES), ALU.mult))
            done(dve.tensor_reduce(expert[:], product[:], AX.X, ALU.add))
            dve.tensor_tensor(expert[:], expert[:], spread(tiny[:, 0:IMAGES], 2, EXPERTS),
                              ALU.mult).then_inc(s.logit, 1)
            dve.wait_ge(s.routing, 1)
            dve.wait_ge(s.cleared, 2)
            for j in range(IMAGES):
                done(dve.tensor_scalar(mixed[:, j], weight[:, 0], routing[:, j, 0:1], None, ALU.mult))
                for e in range(1, EXPERTS - 1):
                    done(dve.scalar_tensor_tensor(out=mixed[:, j], in0=weight[:, e], scalar=routing[:, j, e:e + 1],
                                                  in1=mixed[:, j], op0=ALU.mult, op1=ALU.add))
                e = EXPERTS - 1
                for h in range(HALVES):
                    q = slice(h * C, (h + 1) * C)
                    last = dve.scalar_tensor_tensor(out=kernel[q, j, :, q], in0=by_tap(weight[q, e]),
                                                    scalar=routing[q, j, e:e + 1], in1=by_tap(mixed[q, j]),
                                                    op0=ALU.mult, op1=ALU.add)
                last.then_inc(s.kernel, 1)
            for c in range(2 * IMAGES):
                dve.wait_ge(s.out_ps, c + 1)
                place = x[:, c * BANK:(c + 1) * BANK]
                dve.tensor_tensor(place, place, ps[:, c % RING, :], ALU.add).then_inc(s.added, 1)
    return turn + 1



def conv2(k, layer, turn):
    nc, x, xn, s = k.nc, k.x, k.xn, k.c2
    K, TAPS, A, ATAPS = 5, 25, 3, 9
    PAD = W + 4
    Q = HALVES * CM
    HALF = H // 2
    with ExitStack() as ctx:
        def sb(name, shape):
            return ctx.enter_context(nc.sbuf_tensor("c2_" + name, shape, F32))
        w, cols = sb("w", [P, Q]), sb("cols", [P, 4])
        row = sb("row", [P, 2 * TAPS + 2 * ATAPS + 4])
        fuse = sb("fuse", [P, 2, P])
        conv_b, adap_b, atrous_b, fuse_b = (cols[:, i:i + 1] for i in range(4))
        loads = layer_loads(k, [(w, "c2_w"), (cols, "c2_cols"), (fuse, "c2_fuse")], [(row, "c2_row")])
        layer_norm(k, turn, 1e-6, loads)
        total, g = sb("total", [P, IMAGES]), sb("g", [P, 1])
        taps, raw = sb("taps", [P, TAPS + ATAPS]), sb("raw", [P, TAPS + ATAPS])
        f = sb("f", [P, PAD, PAD])
        near, far, product = sb("near", [P, H, W]), sb("far", [P, H, W]), sb("product", [P, 2, H, W])
        f_ps = ctx.enter_context(nc.psum_tensor("c2_f_ps", [P, 2, BANK], F32))
        g_ps = ctx.enter_context(nc.psum_tensor("c2_g_ps", [P, BANK], F32))
        out_ps = ctx.enter_context(nc.psum_tensor("c2_out_ps", [P, 2, BANK], F32))
        block = ctx.enter_context(nc.Block())

        @block.tensor
        def _(pe):
            pe.wait_ge(k.fetched_sem, k.fetched)
            for c in range(2):
                for j in range(IMAGES):
                    last = pe.matmul(f_ps[j * Q:(j + 1) * Q, c, :], w[:],
                                     xn[:, j * PIX + c * BANK:j * PIX + (c + 1) * BANK], start=True, stop=True)
                last.then_inc(s.f_ps, 1)
            pe.wait_ge(s.total, 1)
            for j in range(IMAGES):
                last = pe.matmul(g_ps[j * Q:(j + 1) * Q, 0:1], w[:], total[:, j:j + 1], start=True, stop=True)
            last.then_inc(s.g_ps, 1)
            pe.wait_ge(s.near, TAPS)
            pe.wait_ge(s.far, ATAPS)
            for c in range(2 * IMAGES):
                j, y = c // 2, (c % 2) * HALF
                q = slice(j * Q, (j + 1) * Q)
                if c >= 2:
                    pe.wait_ge(s.added, c - 1)
                pe.matmul(out_ps[:, c % 2, :], fuse[q, 0, :], near[q, y:y + HALF, :], start=True, stop=False)
                pe.matmul(out_ps[:, c % 2, :], fuse[q, 1, :], far[q, y:y + HALF, :],
                          start=False, stop=True).then_inc(s.out_ps, 1)

        @block.scalar
        def _(act):
            act.wait_ge(k.fetched_sem, k.fetched)
            act.wait_ge(s.cleared, 1)
            for c in range(2):
                act.wait_ge(s.f_ps, c + 1)
                act.activation(f[:, 2 + c * HALF:2 + (c + 1) * HALF, 2:2 + W],
                               f_ps[:, c, :].rearrange("p (y x) -> p y x", x=W), ACT.Relu,
                               bias=conv_b).then_inc(s.f, 1)
            act.wait_ge(s.g_ps, 1)
            act.activation(g[:], g_ps[:, 0:1], ACT.Relu, bias=conv_b, scale=1.0 / PIX).then_inc(s.g, 1)
            act.wait_ge(s.taps, 1)
            act.wait_ge(s.f, 2)
            for t in range(ATAPS):
                dy, dx = 2 * (t // A), 2 * (t % A)
                view = f[:, dy:dy + H, dx:dx + W]
                if t == 0:
                    act.activation(far[:], view, ACT.Identity, bias=atrous_b,
                                   scale=taps[:, TAPS:TAPS + 1]).then_inc(s.product, 1)
                else:
                    if t >= 3:
                        act.wait_ge(s.far, t - 1)
                    act.activation(product[:, t % 2], view, ACT.Copy,
                                   scale=taps[:, TAPS + t:TAPS + t + 1]).then_inc(s.product, 1)

        @block.gpsimd
        def _(pool):
            pool.memset(f[:], 0.0).then_inc(s.cleared, 1)
            pool.wait_ge(s.product, 1)
            pool.engine_nop().then_inc(s.far, 1)
            for t in range(1, ATAPS):
                pool.wait_ge(s.product, t + 1)
                pool.wait_ge(s.far, t)
                pool.tensor_tensor(far[:], far[:], product[:, t % 2], ALU.add).then_inc(s.far, 1)

        @block.vector
        def _(dve):
            step = [0]

            def done(ins):
                step[0] += 1
                ins.then_inc(s.step, 1)
                dve.wait_ge(s.step, step[0])

            dve.tensor_reduce(total[:], xn[:].rearrange("p (j n) -> p j n", n=PIX), AX.X,
                              ALU.add).then_inc(s.total, 1)
            dve.wait_ge(k.fetched_sem, k.fetched)
            dve.wait_ge(s.g, 1)
            for o, n, b in ((0, TAPS, 0), (TAPS, ATAPS, 2 * TAPS)):
                scalars = 2 * (TAPS + ATAPS) + (0 if o == 0 else 2)
                done(dve.scalar_tensor_tensor(out=raw[:, o:o + n], in0=row[:, b:b + n], scalar=g[:],
                                              in1=row[:, b + n:b + 2 * n], op0=ALU.mult, op1=ALU.add))
                last = dve.tensor_scalar(taps[:, o:o + n], raw[:, o:o + n], row[:, scalars:scalars + 1],
                                         row[:, scalars + 1:scalars + 2], ALU.mult, ALU.add)
            last.then_inc(s.taps, 1)
            dve.wait_ge(s.taps, 1)
            dve.wait_ge(s.f, 2)
            for t in range(TAPS):
                view = f[:, t // K:t // K + H, t % K:t % K + W]
                if t == 0:
                    ins = dve.tensor_scalar(near[:], view, taps[:, 0:1], adap_b, ALU.mult, ALU.add)
                else:
                    dve.wait_ge(s.near, t)
                    ins = dve.scalar_tensor_tensor(out=near[:], in0=view, scalar=taps[:, t:t + 1], in1=near[:],
                                                   op0=ALU.mult, op1=ALU.add)
                ins.then_inc(s.near, 1)
            for c in range(2 * IMAGES):
                dve.wait_ge(s.out_ps, c + 1)
                place = x[:, c * BANK:(c + 1) * BANK]
                dve.scalar_tensor_tensor(out=place, in0=out_ps[:, c % 2, :], scalar=fuse_b, in1=place,
                                         op0=ALU.add, op1=ALU.add).then_inc(s.added, 1)
    return turn + 1



TAPS = 9
TILE_ROWS = P // W
QTILES = PIX // P
REACH = 2
XTILES = QTILES + 1
TAP_GROUP = 3


def conv3(k, layer, turn):
    nc, x, xn, s = k.nc, k.x, k.xn, k.c3
    GN = 2
    PAD = W + 2
    HALF = H // 2
    with ExitStack() as ctx:
        def sb(name, shape, dt=F32):
            return ctx.enter_context(nc.sbuf_tensor("c3_" + name, shape, dt))
        w_off, cols = sb("w_off", [P, TAPS, 4 * TAPS]), sb("cols", [P, 3])
        w_deform = sb("w_deform", [P, TAPS // TAP_GROUP, HALVES * TAP_GROUP * C])
        base, ints, pairs = sb("base", [P, 4 * TAPS]), sb("ints", [P, 2 * H + TILE_ROWS]), sb("pairs", [P, P])
        loads = layer_loads(k, [(w_off, "c3_w_off"), (cols, "c3_cols"), (w_deform, "c3_w_deform"), (base, "c3_base"),
                  (pairs, "pairs")], [(ints, "c3_ints")])
        off_b, gn_gamma, gn_beta = (cols[:, i:i + 1] for i in range(3))
        start_at_one(k, k.c3_near.all + k.c3_rest.all)
        layer_norm(k, turn, 1e-6, loads)
        coords = sb("coords", [P, TILES, 4 * TAPS])
        flag = sb("flag", [1, 2], mybir.dt.int32)
        offsets(k, PAD, HALF, w_off, off_b, coords, flag)
        sums = sb("sums", [P, TILES, HALVES, C])
        band = {ty: [(ty, ty + 1)] for ty in range(QTILES)}
        sample(k, "near", k.c3_near, band, w_deform, coords, base, ints, sums, None)
        rest = {}
        for ty in range(QTILES):
            q0, q1 = band[ty][0]
            rest[ty] = [(a, min(a + 2, end)) for start, end in ((0, q0 - 1), (q1 + 1, XTILES - 1))
                        for a in range(start, end + 1, 3)]
        sample(k, "rest", k.c3_rest, rest, w_deform, coords, base, ints, sums, flag)
        group_norm(k, sums, pairs, gn_gamma, gn_beta)
    return turn + 1


def start_at_one(k, semaphores):
    with ExitStack() as ctx:
        block = ctx.enter_context(k.nc.Block())

        @block.sync
        def _(sp):
            for semaphore in semaphores:
                sp.sem_inc(semaphore, 1)


def offsets(k, PAD, HALF, w_off, off_b, coords, flag):
    nc, xn, s = k.nc, k.xn, k.c3
    ROWS = 4 * TAPS
    LOW_ROW = 64
    PER_BANK = 8
    with ExitStack() as ctx:
        high, low = (ctx.enter_context(nc.sbuf_tensor(f"c3_padded_{n}", [P, IMAGES, PAD, PAD], F32R))
                     for n in ("high", "low"))
        w_parts = ctx.enter_context(nc.sbuf_tensor("c3_w_parts", [P, TAPS, LOW_ROW + ROWS], F32R))
        off = ctx.enter_context(nc.sbuf_tensor("c3_off", [ROWS, N], F32))
        reach = ctx.enter_context(nc.sbuf_tensor("c3_reach", [P, 4], F32))
        most = ctx.enter_context(nc.sbuf_tensor("c3_most", [1, 4], F32))
        ps = ctx.enter_context(nc.psum_tensor("c3_off_ps", [P, 2, BANK], F32))
        turned = ctx.enter_context(nc.psum_tensor("c3_turned", [P, 4, BANK], F32))
        block = ctx.enter_context(nc.Block())

        def image(j):
            return xn[:, j * PIX:(j + 1) * PIX].rearrange("p (y x) -> p y x", x=W)

        def inner(part, j):
            return part[:, j, 1:1 + H, 1:1 + W]

        @block.gpsimd
        def _(pool):
            pool.memset(w_parts[:, :, ROWS:LOW_ROW].bitcast(F32), 0.0).then_inc(s.filled, 1)
            for j in range(IMAGES):
                for part in (high, low):
                    pool.memset(part[:, j].bitcast(F32), 0.0).then_inc(s.cleared, 1)

        @block.scalar
        def _(act):
            act.wait_ge(k.fetched_sem, k.fetched)
            act.copy(w_parts[:, :, 0:ROWS], w_off[:]).then_inc(s.w_high, 1)
            for j in range(IMAGES):
                act.wait_ge(s.cleared, 2 * j + 2)
                act.copy(inner(high, j), image(j)).then_inc(s.high, 1)
            for c in range(N // BANK):
                act.wait_ge(s.off_ps, c + 1)
                act.activation(off[:, c * BANK:(c + 1) * BANK], ps[0:ROWS, c % 2, :], ACT.Identity,
                               bias=off_b[0:ROWS]).then_inc(s.off_high, 1)

        @block.tensor
        def _(pe):
            pe.wait_ge(s.w_low, 1)
            for c in range(2 * IMAGES):
                j, y = c // 2, (c % 2) * HALF
                pe.wait_ge(s.padded, j + 1)
                if c >= 2:
                    pe.wait_ge(s.off, c - 1)
                for t in range(TAPS):
                    for part in (high, low):
                        last = pe.matmul(ps[0:LOW_ROW + ROWS, c % 2, :], w_parts[:, t, :],
                                         part[:, j, y + t // 3:y + t // 3 + HALF, t % 3:t % 3 + W],
                                         start=(t == 0 and part is high), stop=(t == TAPS - 1 and part is low))
                last.then_inc(s.off_ps, 1)
            for t in range(TILES):
                pe.wait_ge(s.off, t * P // BANK + 1)
                last = pe.transpose(turned[:, t // PER_BANK, (t % PER_BANK) * ROWS:(t % PER_BANK + 1) * ROWS],
                                    off[:, t * P:(t + 1) * P], k.identity[0:ROWS, 0:ROWS])
                if t % PER_BANK == PER_BANK - 1:
                    last.then_inc(s.turned, 1)
            pe.wait_ge(s.reach, 1)
            pe.transpose(ps[0:1, 0, 0:P], reach[:, 2:3], k.identity[:]).then_inc(s.reach_ps, 1)

        @block.vector
        def _(dve):
            step = [0]

            def done(ins):
                step[0] += 1
                ins.then_inc(s.step, 1)
                dve.wait_ge(s.step, step[0])

            dve.wait_ge(s.filled, 1)
            dve.wait_ge(s.w_high, 1)
            dve.tensor_tensor(w_parts[:, :, LOW_ROW:LOW_ROW + ROWS], w_off[:], w_parts[:, :, 0:ROWS].bitcast(F32),
                              ALU.subtract).then_inc(s.w_low, 1)
            for j in range(IMAGES):
                dve.wait_ge(s.high, j + 1)
                dve.tensor_tensor(inner(low, j), image(j), inner(high, j).bitcast(F32),
                                  ALU.subtract).then_inc(s.padded, 1)
            for c in range(N // BANK):
                dve.wait_ge(s.off_high, c + 1)
                own = off[:, c * BANK:(c + 1) * BANK]
                dve.tensor_tensor(own, own, ps[LOW_ROW:LOW_ROW + ROWS, c % 2, :], ALU.add).then_inc(s.off, 1)
            dve.wait_ge(s.turned, TILES // PER_BANK)
            rows = coords[:].rearrange("p t (n c) -> p t n c", c=2)[:, :, :, 0]
            for b in range(TILES // PER_BANK):
                last = dve.tensor_copy(coords[:, b * PER_BANK:(b + 1) * PER_BANK, :],
                                       turned[:, b, 0:PER_BANK * ROWS].rearrange("p (t r) -> p t r", r=ROWS))
            done(last)
            dve.tensor_reduce(reach[:, 0:1], rows, AX.XY, ALU.max)
            done(dve.tensor_reduce(reach[:, 1:2], rows, AX.XY, ALU.min))
            dve.scalar_tensor_tensor(out=reach[:, 2:3], in0=reach[:, 1:2], scalar=-1.0, in1=reach[:, 0:1],
                                     op0=ALU.mult, op1=ALU.max).then_inc(s.reach, 1)
            dve.wait_ge(s.reach_ps, 1)
            done(dve.tensor_reduce(most[:, 0:1], ps[0:1, 0, 0:P], AX.X, ALU.max))
            done(dve.tensor_scalar(most[:, 1:2], most[:, 0:1], float(REACH), None, ALU.is_ge))
            dve.tensor_copy(flag[:, 0:1], most[:, 1:2])


def sample(k, name, s, blocks, w_deform, coords, base, ints, sums, flag):
    nc, xn = k.nc, k.xn
    items = [(ty, h, q0, q1) for ty in range(QTILES) for h in range(HALVES) for q0, q1 in blocks[ty]]
    first = [i == 0 or items[i - 1][:2] != it[:2] for i, it in enumerate(items)]
    last_of = [i + 1 == len(items) or items[i + 1][:2] != it[:2] for i, it in enumerate(items)]
    G = TAPS // TAP_GROUP
    ITEMS, STEPS, SUMS, VALUES = len(items), len(items) * G, HALVES * QTILES, XTILES * G
    VCOLS = TAP_GROUP * C
    RMAX = max(q1 - q0 + 1 for _, _, q0, q1 in items) * TILE_ROWS
    EDGE = REACH + 1
    assert ITEMS % 2 == 0 and STEPS % 2 == 0
    with ExitStack() as ctx:
        def sb(nm, shape, dt=F32):
            return ctx.enter_context(nc.sbuf_tensor(f"c3_{name}_{nm}", shape, dt))
        staged = sb("staged", [P, (EDGE + H + EDGE) * W])
        position = sb("position", [P, QTILES, 4 * TAPS])
        values = sb("values", [P, XTILES, G, HALVES * VCOLS])
        dist = sb("dist", [P, 2, TAPS, W + RMAX])
        hats = sb("hats", [P, 2, TAPS, W + RMAX])
        weights = sb("weights", [P, 2, TAP_GROUP, RMAX * W])
        matrix = sb("matrix", [P, 2, TAP_GROUP, RMAX * W])
        turned = ctx.enter_context(nc.psum_tensor(f"c3_{name}_turned", [P, 2, TAP_GROUP, BANK], F32))
        sum_ps = ctx.enter_context(nc.psum_tensor(f"c3_{name}_sum_ps", [P, 2, BANK], F32))
        block = ctx.enter_context(nc.Block())

        def run(eng, body):
            def loop():
                with eng.Fori(0, IMAGES, 1) as j:
                    body(j)
            if flag is None:
                loop()
            else:
                beyond = eng.value_load(flag[0:1, 0:1], min_val=0, max_val=1)
                with eng.If(beyond > 0):
                    loop()

        @block.tensor
        def _(pe):
            def values_of(j):
                pe.wait_ge(s.staged, 1 + j + 1)
                pe.wait_ge(s.summed, 1 + j * SUMS)
                for v in range(VALUES):
                    q, g = v // G, v % G
                    pe.wait_ge(s.values, 1 + j * VALUES + max(v - 1, 0))
                    pe.matmul(sum_ps[:, v % 2, 0:HALVES * VCOLS], staged[:, q * P + g * W:(q + 1) * P + g * W],
                              w_deform[:, g, :],
                              start=True, stop=True).then_inc(s.values_ps, 1)

            def turn(j, n):
                q0, q1 = items[n // G][2:]
                pe.wait_ge(s.weights, 1 + j * STEPS + n + 1)
                pe.wait_ge(s.matrix, 1 + j * STEPS + max(n - 1, 0))
                for t in range(TAP_GROUP):
                    for q in range(q1 - q0 + 1):
                        last = pe.transpose(turned[:, n % 2, t, q * P:(q + 1) * P],
                                            weights[:, n % 2, t, q * P:(q + 1) * P], k.identity[:])
                last.then_inc(s.turned, 1)

            def multiply(j, n):
                i, g = n // G, n % G
                ty, h, q0, q1 = items[i]
                pe.wait_ge(s.matrix, 1 + j * STEPS + n + 1)
                tile = ty * HALVES + h
                if g == 0 and first[i]:
                    pe.wait_ge(s.summed, 1 + j * SUMS + max(tile - 1, 0))
                for t in range(TAP_GROUP):
                    for q in range(q1 - q0 + 1):
                        last = pe.matmul(sum_ps[:, tile % 2, 0:C], matrix[:, n % 2, t, q * P:(q + 1) * P],
                                         values[:, q0 + q, g, h * VCOLS + t * C:h * VCOLS + (t + 1) * C],
                                         start=(g == 0 and first[i] and t == 0 and q == 0),
                                         stop=(g == G - 1 and last_of[i] and t == TAP_GROUP - 1 and q == q1 - q0))
                last.then_inc(s.used, 1)

            def body(j):
                values_of(j)
                pe.wait_ge(s.values, 1 + (j + 1) * VALUES)
                for n in range(STEPS):
                    turn(j, n)
                    if n > 0:
                        multiply(j, n - 1)
                multiply(j, STEPS - 1)
            run(pe, body)

        @block.scalar
        def _(act):
            def body(j):
                act.wait_ge(s.used, 1 + j * STEPS)
                for v in range(VALUES):
                    q, g = v // G, v % G
                    act.wait_ge(s.values_ps, 1 + j * VALUES + v + 1)
                    act.copy(values[:, q, g, :], sum_ps[:, v % 2, 0:HALVES * VCOLS]).then_inc(s.values, 1)
                for n in range(STEPS):
                    q0, q1 = items[n // G][2:]
                    width = (q1 - q0 + 1) * P
                    act.wait_ge(s.turned, 1 + j * STEPS + n + 1)
                    act.wait_ge(s.used, 1 + j * STEPS + max(n - 1, 0))
                    act.copy(matrix[:, n % 2, :, 0:width], turned[:, n % 2, :, 0:width]).then_inc(s.matrix, 1)
            run(act, body)

        @block.gpsimd
        def _(pool):
            def body(j):
                pool.wait_ge(s.position, 1 + j + 1)
                for i, (ty, h, q0, q1) in enumerate(items):
                    pool.wait_ge(s.hats, 1 + j * ITEMS + max(i - 1, 0))
                    own = position[:, ty, h * 2 * TAPS:(h + 1) * 2 * TAPS].rearrange("p (t c) -> p t c", c=2)
                    rows = (q1 - q0 + 1) * TILE_ROWS
                    start = H + (q0 - ty) * TILE_ROWS - REACH
                    pool.tensor_tensor(dist[:, i % 2, :, 0:W], spread(own[:, :, 1], 2, W),
                                       spread(ints[:, H:H + W], 1, TAPS), ALU.subtract)
                    pool.tensor_tensor(dist[:, i % 2, :, W:W + rows], spread(own[:, :, 0], 2, rows),
                                       spread(ints[:, start:start + rows], 1, TAPS),
                                       ALU.subtract).then_inc(s.dist, 1)
            run(pool, body)

        @block.vector
        def _(dve):
            def body(j):
                def used(i):
                    q0, q1 = items[i][2:]
                    return W + (q1 - q0 + 1) * TILE_ROWS

                def negate(i):
                    dve.wait_ge(s.dist, 1 + j * ITEMS + i + 1)
                    dve.wait_ge(s.weights, 1 + j * STEPS + G * max(i - 1, 0))
                    own = dist[:, i % 2, :, 0:used(i)]
                    dve.scalar_tensor_tensor(out=hats[:, i % 2, :, 0:used(i)], in0=own, scalar=-1.0, in1=own,
                                             op0=ALU.mult, op1=ALU.min).then_inc(s.hats, 1)

                def hat(i):
                    dve.wait_ge(s.hats, 1 + j * ITEMS + i + 1)
                    dve.tensor_scalar(hats[:, i % 2, :, 0:used(i)], hats[:, i % 2, :, 0:used(i)], 1.0, 0.0,
                                      ALU.add, ALU.max).then_inc(s.hatted, 1)

                def weigh(n):
                    i, g = n // G, n % G
                    rows = used(i) - W
                    own = hats[:, i % 2, g * TAP_GROUP:(g + 1) * TAP_GROUP, :]
                    dve.wait_ge(s.hatted, 1 + j * ITEMS + i + 1)
                    dve.wait_ge(s.turned, 1 + j * STEPS + max(n - 1, 0))
                    dve.tensor_tensor(
                        weights[:, n % 2, :, 0:rows * W].rearrange("p t (r c) -> p t r c", c=W),
                        spread(own[:, :, W:W + rows], 3, W), spread(own[:, :, 0:W], 2, rows),
                        ALU.mult).then_inc(s.weights, 1)

                def keep(i):
                    ty, h = items[i][:2]
                    dve.wait_ge(s.used, 1 + j * STEPS + (i + 1) * G)
                    place = sums[:, bass.ds(j * QTILES + ty, 1), h, :].rearrange("p o c -> p (o c)")
                    source = sum_ps[:, (ty * HALVES + h) % 2, 0:C]
                    if flag is None:
                        dve.tensor_scalar(place, source, 1.0, None, ALU.mult).then_inc(s.summed, 1)
                    else:
                        dve.tensor_tensor(place, place, source, ALU.add).then_inc(s.summed, 1)

                dve.wait_ge(s.values_ps, 1 + j * VALUES)
                dve.tensor_scalar(staged[:, EDGE * W:(EDGE + H) * W], xn[:, bass.ds(j * PIX, PIX)], 1.0, None,
                                  ALU.mult).then_inc(s.staged, 1)
                dve.wait_ge(s.dist, 1 + j * ITEMS)
                dve.tensor_tensor(position[:], coords[:, bass.ds(j * QTILES, QTILES), :],
                                  spread(base[:], 1, QTILES), ALU.add).then_inc(s.position, 1)
                negate(0)
                hat(0)
                for i in range(ITEMS):
                    if i + 1 < ITEMS:
                        negate(i + 1)
                    weigh(G * i)
                    if i + 1 < ITEMS:
                        hat(i + 1)
                    weigh(G * i + 1)
                    if i > 0 and last_of[i - 1]:
                        keep(i - 1)
                    weigh(G * i + 2)
                keep(ITEMS - 1)
            for edge in (slice(0, EDGE * W), slice((EDGE + H) * W, (EDGE + H + EDGE) * W)):
                dve.memset(staged[:, edge], 0.0)
            run(dve, body)


def group_norm(k, sums, pairs, gamma, beta):
    nc, x, s = k.nc, k.x, k.c3
    STATS = PIX // BANK
    with ExitStack() as ctx:
        def sb(name, shape):
            return ctx.enter_context(nc.sbuf_tensor("gn_" + name, shape, F32))
        y = sb("y", [P, N])
        stats, own, group = sb("stats", [P, IMAGES * STATS, 6]), sb("own", [P, IMAGES, 4]), sb("group", [P, 7, IMAGES])
        ps = ctx.enter_context(nc.psum_tensor("gn_ps", [P, 2, BANK], F32))
        mean_ps = ctx.enter_context(nc.psum_tensor("gn_mean_ps", [P, IMAGES, 2], F32))
        block = ctx.enter_context(nc.Block())

        @block.tensor
        def _(pe):
            for g in range(N // BANK):
                if g >= 2:
                    pe.wait_ge(s.y, g - 1)
                for t in range(BANK // P):
                    last = pe.transpose(ps[:, g % 2, t * P:(t + 1) * P],
                                        sums[:, g * (BANK // P) + t].rearrange("p h c -> p (h c)"), k.identity[:])
                last.then_inc(s.y_ps, 1)
            pe.wait_ge(s.own, 1)
            pe.matmul(mean_ps[:], pairs[:], own[:, :, 0:2], start=True, stop=True).then_inc(s.group, 1)

        @block.scalar
        def _(act):
            for g in range(N // BANK):
                act.wait_ge(s.y_ps, g + 1)
                act.copy(y[:, g * BANK:(g + 1) * BANK], ps[:, g % 2, :]).then_inc(s.y, 1)
            act.wait_ge(s.neg_var, 1)
            act.activation(group[:, 3], group[:, 2], ACT.Sqrt, bias=k.eps[1e-5][:], scale=-1.0).then_inc(s.dev, 1)
            act.wait_ge(s.affine, 1)
            for j in range(IMAGES):
                act.activation(y[:, j * PIX:(j + 1) * PIX], y[:, j * PIX:(j + 1) * PIX], ACT.Relu,
                               bias=group[:, 6, j:j + 1], scale=group[:, 5, j:j + 1]).then_inc(s.relu, 1)

        @block.vector
        def _(dve):
            step = [k.c3_steps]

            def done(ins):
                step[0] += 1
                ins.then_inc(s.gn_step, 1)
                dve.wait_ge(s.gn_step, step[0])

            for g in range(N // BANK):
                dve.wait_ge(s.y, g + 1)
                last = dve.bn_stats(stats[:, g, :], y[:, g * BANK:(g + 1) * BANK])
            done(last)
            for j in range(IMAGES):
                last = dve.bn_aggr(own[:, j, 2:4], stats[:, j * STATS:(j + 1) * STATS, :])
            done(last)
            dve.tensor_copy(own[:, :, 0], own[:, :, 2])
            done(dve.tensor_tensor(own[:, :, 1], own[:, :, 2], own[:, :, 2], ALU.mult))
            dve.tensor_tensor(own[:, :, 1], own[:, :, 1], own[:, :, 3], ALU.add).then_inc(s.own, 1)
            dve.wait_ge(s.group, 1)
            done(dve.tensor_copy(group[:, 0:2], mean_ps[:].rearrange("p j c -> p c j")))
            done(dve.tensor_tensor(group[:, 3], group[:, 0], group[:, 0], ALU.mult))
            dve.tensor_tensor(group[:, 2], group[:, 3], group[:, 1], ALU.subtract).then_inc(s.neg_var, 1)
            dve.wait_ge(s.dev, 1)
            done(dve.reciprocal(group[:, 4], group[:, 3]))
            done(dve.tensor_scalar(group[:, 5], group[:, 4], gamma, None, ALU.mult))
            done(dve.tensor_tensor(group[:, 4], group[:, 0], group[:, 5], ALU.mult))
            dve.tensor_scalar(group[:, 6], group[:, 4], -1.0, beta, ALU.mult, ALU.add).then_inc(s.affine, 1)
            for j in range(IMAGES):
                dve.wait_ge(s.relu, j + 1)
                place = x[:, j * PIX:(j + 1) * PIX]
                dve.tensor_tensor(place, place, y[:, j * PIX:(j + 1) * PIX], ALU.add)



def load_image(k, sp, j):
    for h in range(HALVES):
        sp.dma_start(k.x[h * C:(h + 1) * C, j * PIX:(j + 1) * PIX],
                     k.ins["x"][h * IMAGES + j]).then_inc(k.image_loaded[j], 16)


def load_first(k):
    nc = k.nc
    with ExitStack() as ctx:
        block = ctx.enter_context(nc.Block())

        @block.sync
        def _(sp):
            sp.dma_start(k.centring[:], k.ins["centring"]).then_inc(k.constants, 16)
            load_image(k, sp, 0)
            for to, name in ((k.shifted, "shifted"), (k.rows, "rows")):
                sp.dma_start(to[:], k.ins[name]).then_inc(k.constants, 16)
            k.constants_all = 16 * 3

        @block.vector
        def _(dve):
            for eps, place in k.eps.items():
                dve.memset(place[:], eps)


def store_image(k, sp, j):
    for h in range(HALVES):
        sp.dma_start(k.out[h * IMAGES + j], k.x[h * C:(h + 1) * C, j * PIX:(j + 1) * PIX]).then_inc(k.stored, 16)


def layer_loads(k, copies, rows):
    k.fetched += 16 * (len(copies) + len(rows))
    loads = [(to[:], k.ins[name], k.fetched_sem) for to, name in copies]
    loads += [(to[:], k.ins[name].partition_broadcast(P), k.fetched_sem) for to, name in rows]
    return loads + pending_loads(k)


def pending_loads(k):
    loads, k.loads = k.loads, []
    return loads


def mixture_loads(k, layer):
    w, ins = k.w, k.ins
    swiglu = layer in (0, 3)
    m = SWIGLU if swiglu else GELU
    E = m.experts
    w.first = w.first_room[:, 0:2 * P * E]
    w.router = w.router_room[:, 0:HALVES * E]
    w.router_bias = w.router_bias_room[:, 0:E]
    copies = [(w.first[0:C], ins[f"f{layer}_first"]), (w.first[C:P], ins[f"f{layer}_first"]),
              (w.second[:], ins[f"f{layer}_second"]), (w.router, ins[f"f{layer}_router"]),
              (w.router_bias, ins[f"f{layer}_router_bias"].partition_broadcast(P))]
    if not swiglu:
        copies += [(w.bias1[:], ins[f"f{layer}_bias1"]),
                   (w.bias2[:].rearrange("p e c -> p (e c)"), ins[f"f{layer}_bias2"].partition_broadcast(P))]
    w.all += 16 * len(copies)
    return [(to, source, w.loaded) for to, source in copies]


def ffn(k, layer, turn, last_layer):
    nc, w = k.nc, k.w
    swiglu = layer in (0, 3)
    m = SWIGLU if swiglu else GELU
    with ExitStack() as ctx:
        k.parts = ctx.enter_context(nc.sbuf_tensor(f"parts{layer}", [P, HALVES, N], F32R))
        w.high = ctx.enter_context(nc.sbuf_tensor(f"high{layer}", [P, 2 * P * m.experts], F32R))
        w.low = ctx.enter_context(nc.sbuf_tensor(f"low{layer}", [P, 2 * P * m.experts], F32R))
        top_two = TopTwo(k, ctx, m)
        layer_norm(k, turn, 1e-5, pending_loads(k), router=(top_two, w))
        mixture(k, k.mixtures, m, w, swiglu, top_two, last_layer)
        k.mixtures += 1


class Network:
    pass


class Weights:
    pass



class LayerNormSignals:
    def __init__(self, new):
        self.mean = new("ln_mean")
        self.centred = new("ln_centred")
        self.squared = new("ln_squared")
        self.var = new("ln_var")
        self.dev = new("ln_dev")
        self.scale = new("ln_scale")
        self.wide = new("ln_wide")
        self.normed = new("ln_normed")


class GateSignals:
    def __init__(self, new):
        self.logits = new("gt_logits")
        self.high = new("gt_high")
        self.w_high = new("gt_w_high")
        self.gap = new("gt_gap")
        self.exp = new("gt_exp")
        self.step = new("gt_step")


class MixtureSignals:
    def __init__(self, new):
        self.first = new("mx_first")
        self.act = new("mx_act")
        self.hidden = new("mx_hidden")
        self.second = new("mx_second")
        self.read = new("mx_read")
        self.biased = new("mx_biased")
        self.accumulated = new("mx_accumulated")
        self.summed = new("mx_summed")
        self.back = new("mx_back")
        self.added = new("mx_added")


class BatchNormSignals:
    def __init__(self, new):
        self.own = new("bn_own")
        self.both = new("bn_both")
        self.neg_var = new("bn_neg_var")
        self.dev = new("bn_dev")
        self.step = new("bn_step")


class Conv0Signals:
    def __init__(self, new):
        self.key_ps = new("c0_key_ps")
        self.key = new("c0_key")
        self.key_max = new("c0_key_max")
        self.key_exp = new("c0_key_exp")
        self.qv_ps = new("c0_qv_ps")
        self.qv = new("c0_qv")
        self.q_shift = new("c0_q_shift")
        self.q_exp = new("c0_q_exp")
        self.q_soft = new("c0_q_soft")
        self.turned_ps = new("c0_turned_ps")
        self.turned = new("c0_turned")
        self.small_ps = new("c0_small_ps")
        self.small = new("c0_small")
        self.sigmoid = new("c0_sigmoid")
        self.gate_exp = new("c0_gate_exp")
        self.out_ps = new("c0_out_ps")
        self.added = new("c0_added")
        self.step = new("c0_step")


class Conv1Signals:
    def __init__(self, new):
        self.cleared = new("c1_cleared")
        self.padded = new("c1_padded")
        self.small_ps = new("c1_small_ps")
        self.squeezed = new("c1_squeezed")
        self.logit = new("c1_logit")
        self.routing = new("c1_routing")
        self.total = new("c1_total")
        self.kernel = new("c1_kernel")
        self.out_ps = new("c1_out_ps")
        self.added = new("c1_added")
        self.step = new("c1_step")


class Conv2Signals:
    def __init__(self, new):
        self.cleared = new("c2_cleared")
        self.f_ps = new("c2_f_ps")
        self.f = new("c2_f")
        self.total = new("c2_total")
        self.g_ps = new("c2_g_ps")
        self.g = new("c2_g")
        self.taps = new("c2_taps")
        self.product = new("c2_product")
        self.far = new("c2_far")
        self.near = new("c2_near")
        self.out_ps = new("c2_out_ps")
        self.added = new("c2_added")
        self.step = new("c2_step")


class Conv3Signals:
    def __init__(self, new):
        self.cleared = new("c3_cleared")
        self.padded = new("c3_padded")
        self.filled = new("c3_filled")
        self.w_high = new("c3_w_high")
        self.w_low = new("c3_w_low")
        self.high = new("c3_high")
        self.off_high = new("c3_off_high")
        self.off_ps = new("c3_off_ps")
        self.off = new("c3_off")
        self.turned = new("c3_turned")
        self.reach = new("c3_reach")
        self.reach_ps = new("c3_reach_ps")
        self.step = new("c3_step")
        self.y_ps = new("c3_y_ps")
        self.y = new("c3_y")
        self.own = new("c3_own")
        self.group = new("c3_group")
        self.neg_var = new("c3_neg_var")
        self.dev = new("c3_dev")
        self.affine = new("c3_affine")
        self.relu = new("c3_relu")
        self.gn_step = new("c3_gn_step")


class SampleSignals:
    def __init__(self, new, name):
        self.staged = new(f"{name}_staged")
        self.position = new(f"{name}_position")
        self.values_ps = new(f"{name}_values_ps")
        self.values = new(f"{name}_values")
        self.dist = new(f"{name}_dist")
        self.hats = new(f"{name}_hats")
        self.hatted = new(f"{name}_hatted")
        self.weights = new(f"{name}_weights")
        self.turned = new(f"{name}_turned")
        self.matrix = new(f"{name}_matrix")
        self.used = new(f"{name}_used")
        self.summed = new(f"{name}_summed")
        self.all = [self.staged, self.position, self.values_ps, self.values, self.dist, self.hats, self.hatted, self.weights, self.turned, self.matrix, self.used, self.summed]


def build(nc, ins, out, plan):
    with ExitStack() as ctx:
        def sb(name, shape, dt=F32):
            return ctx.enter_context(nc.sbuf_tensor(name, shape, dt))

        def new(name):
            return ctx.enter_context(nc.semaphore(name))

        k = Network()
        k.nc, k.ins, k.out = nc, ins, out
        k.x = sb("x", [P, N])
        k.xn = sb("xn", [P, N])
        k.gate = sb("gate", [P, HALVES * TILES * SWIGLU.experts])
        k.centring = sb("centring", [P, P])
        k.identity = sb("identity", [P, P])
        k.shifted = sb("shifted", [P, 2 * HALVES * LN_TILES])
        k.rows = sb("rows", [HALVES * LN_TILES, LN_TILES * P])
        k.countdown = sb("countdown", [P, SWIGLU.experts])
        k.eps = {e: sb(f"eps{i}", [P, 1]) for i, e in enumerate((1e-5, 1e-6))}
        k.constants, k.more_constants = new("constants"), new("more_constants")
        k.image_loaded = [new(f"image{j}_loaded") for j in range(IMAGES)]
        k.stored = ctx.enter_context(nc.semaphore("stored"))
        k.ln = LayerNormSignals(new)
        k.gt = GateSignals(new)
        k.mx = MixtureSignals(new)
        k.mx_base = dict(expert=0, first=0, hidden=0, pair=0, biased=0, acc=0, chunk=0)
        k.w = Weights()
        k.w.first_room = sb("w_first", [P, 2 * P * SWIGLU.experts])
        k.w.second = sb("w_second", [P, C * SWIGLU.experts])
        k.w.router_room = sb("w_router", [P, HALVES * SWIGLU.experts])
        k.w.router_bias_room = sb("w_router_bias", [P, SWIGLU.experts])
        k.w.bias1 = sb("w_bias1", [P, 2 * GELU.experts])
        k.w.bias2 = sb("w_bias2", [P, GELU.experts, C])
        k.w.loaded = ctx.enter_context(nc.semaphore("w_loaded"))
        k.w.all = 0
        k.mixtures = 0
        k.fetched_sem = ctx.enter_context(nc.semaphore("fetched"))
        k.fetched = 0
        k.bn = BatchNormSignals(new)
        k.c0 = Conv0Signals(new)
        k.c1 = Conv1Signals(new)
        k.c2 = Conv2Signals(new)
        k.c3 = Conv3Signals(new)
        k.c3_steps = 0
        k.c3_near, k.c3_rest = SampleSignals(new, "near"), SampleSignals(new, "rest")
        load_first(k)
        k.loads = [(k.identity[:], ins["identity"], k.more_constants),
                   (k.countdown[:], ins["countdown"], k.more_constants)]
        turn = 0
        ready = None
        for place, (what, layer) in enumerate(plan):
            if layer != ready:
                k.loads += mixture_loads(k, layer)
                ready = layer
            if what == "ffn":
                ffn(k, layer, turn, last_layer=(place == len(plan) - 1))
                turn += 1
            else:
                turn = what(k, layer, turn)


def lay_out(inputs):
    f = lambda n: np.ascontiguousarray(inputs[n])
    stack = lambda a: np.concatenate([a, a], axis=0)

    def diagonal(a):
        z = np.zeros_like(a)
        return np.concatenate([np.concatenate([a, z], axis=1), np.concatenate([z, a], axis=1)])

    c = {
        "x": f("x").reshape(B, C, PIX),
        "average": diagonal(np.full((C, C), 1.0 / C, np.float32)),
        "centring": diagonal(np.eye(C, dtype=np.float32) - np.float32(1.0 / C)),
        "identity": np.eye(P, dtype=np.float32),
        "rows": np.repeat(np.eye(HALVES * LN_TILES, dtype=np.float32), C, axis=1),
        "shifted": np.concatenate([np.zeros((P, 2 * LN_TILES - 2)), diagonal(np.full((C, 1), 1.0 / C)),
                                   np.zeros((P, 2 * LN_TILES))], axis=1).astype(np.float32),
        "countdown": np.broadcast_to(np.arange(SWIGLU.experts, 0, -1, dtype=np.float32), (P, SWIGLU.experts)),
    }
    p = "L0_conv_"
    c["c0_wk"] = diagonal(f(p + "wk").T)
    c["c0_wqv"] = np.concatenate([diagonal(f(p + "wq").T), diagonal(f(p + "wv").T)], axis=1)
    c["c0_bqv"] = np.concatenate([f(p + "bq"), f(p + "bq"), f(p + "bv"), f(p + "bv")])
    c["c0_cols"] = np.stack([stack(f(p + n)) for n in ("bn_gamma", "bn_beta", "bk", "b_rep")]
                            + [np.broadcast_to(f(p + "b_se"), (P,))], axis=1)
    c["c0_wrep"] = f(p + "w_rep").T.reshape(HEADS, HK, C).transpose(1, 0, 2).reshape(HK, HEADS * C)
    c["c0_fc"] = np.concatenate([f(p + n).reshape(-1) for n in
                                 ("w_fc1", "b_fc1", "w_fc2", "b_fc2", "w_se")]).reshape(1, 14)
    c["halves"] = np.tile(np.eye(C, dtype=np.float32) / HALVES, (HALVES, HALVES))
    c["quads"] = np.repeat(np.eye(HALVES * HEADS, dtype=np.float32), HK, axis=0) / (HK * HK)
    c["heads"] = diagonal(np.tile(np.eye(HK, dtype=np.float32), (HEADS, HEADS)))
    p = "L1_conv_"
    c["c1_w1"] = diagonal(f(p + "w1").T)
    c["c1_w2"] = diagonal(f(p + "w2").T)
    c["c1_wexp"] = f(p + "w_exp").reshape(-1)
    weight = f(p + "weight")
    c["c1_weight"] = stack(weight.transpose(2, 0, 3, 4, 1).reshape(C, weight.shape[0], 9 * C))
    p = "L2_conv_conv_"
    c["c2_w"] = diagonal(f(p + "w").T)
    c["c2_row"] = np.concatenate([f(p + n).reshape(-1) for n in (
        "kernel_w", "kernel_b", "kernel2_w", "kernel2_b", "k_w", "k_b", "k2_w", "k2_b")])
    p = "L2_conv_"
    c["c2_cols"] = np.stack([np.tile(f(p + n), B) for n in ("conv_b", "adap_b", "atrous_b")]
                            + [np.tile(f(p + "fuse_b"), 2 * HALVES)], axis=1)
    fw = f(p + "fuse_w").T
    near, far = np.concatenate([fw, np.zeros_like(fw)], axis=1), np.concatenate([np.zeros_like(fw), fw], axis=1)
    c["c2_fuse"] = np.stack([np.tile(diagonal(a), (IMAGES, 1)) for a in (near, far)], axis=1)
    p = "L3_conv_"
    off_w = f(p + "offset_w").reshape(2 * TAPS, C, TAPS).transpose(2, 1, 0)
    c["c3_w_off"] = np.stack([diagonal(a) for a in off_w], axis=1)
    off_b = f(p + "offset_b")
    c["c3_cols"] = np.stack([np.concatenate([off_b, off_b, np.zeros(P - 4 * TAPS, np.float32)]),
                             stack(f(p + "gn_gamma")), stack(f(p + "gn_beta"))], axis=1)
    deform = f(p + "deform_w").reshape(C, C, TAPS // TAP_GROUP, TAP_GROUP).transpose(2, 1, 3, 0)
    c["c3_w_deform"] = np.stack([diagonal(a.reshape(C, TAP_GROUP * C)) for a in deform], axis=1)
    at = np.arange(P)
    tap = np.arange(TAPS)
    base = np.stack([(at // W)[:, None] + 0 * tap[None], (at % W)[:, None] - 1 + (tap % 3)[None]], axis=2)
    c["c3_base"] = np.tile(base.reshape(P, 2 * TAPS), (1, HALVES)).astype(np.float32)
    c["c3_ints"] = np.arange(-H, H + TILE_ROWS, dtype=np.float32)
    c["pairs"] = np.kron(np.eye(P // 2), np.full((2, 2), 0.5)).astype(np.float32)
    for layer in (0, 3):
        p = f"L{layer}_ffn_"
        E = SWIGLU.experts
        first = np.stack([f(p + "w1"), f(p + "w2")], axis=1)
        c[f"f{layer}_first"] = first.transpose(2, 0, 1, 3).reshape(C, E * 2 * P)
        c[f"f{layer}_second"] = f(p + "w3").transpose(1, 0, 2).reshape(P, E * C)
        c[f"f{layer}_router"] = diagonal(f(p + "gate_w"))
        c[f"f{layer}_router_bias"] = f(p + "gate_b")
    for layer in (1, 2):
        p = f"L{layer}_ffn_"
        E = GELU.experts
        c[f"f{layer}_first"] = f(p + "W1").transpose(1, 0, 2).reshape(C, E * 2 * P)
        c[f"f{layer}_second"] = f(p + "W2").reshape(E, 2, P, C).transpose(2, 0, 1, 3).reshape(P, E * 2 * C)
        c[f"f{layer}_router"] = diagonal(f(p + "Wg"))
        c[f"f{layer}_router_bias"] = f(p + "bg")
        c[f"f{layer}_bias1"] = f(p + "b1").reshape(E, 2, P).transpose(2, 0, 1).reshape(P, E * 2)
        c[f"f{layer}_bias2"] = f(p + "b2").reshape(E * C)
    return {n: np.ascontiguousarray(a) for n, a in c.items()}



PLAN = [(conv0, 0), ("ffn", 0), (conv1, 1), ("ffn", 1), (conv2, 2), ("ffn", 2), (conv3, 3), ("ffn", 3)]


def kernel(**inputs):
    import concourse.bacc as bacc
    from concourse.bass_utils import run_bass_kernel_spmd

    arrays = lay_out(inputs)
    nc = bacc.Bacc("TRN2", target_bir_lowering=False, num_devices=1)
    ins = {name: nc.dram_tensor(f"in_{name}", a.shape, mybir.dt.from_np(a.dtype), kind="ExternalInput").ap()
           for name, a in arrays.items()}
    out = nc.dram_tensor("out_x", (B, C, PIX), F32, kind="ExternalOutput").ap()
    build(nc, ins, out, PLAN)
    result = run_bass_kernel_spmd(nc, [{f"in_{name}": a for name, a in arrays.items()}], core_ids=[0])
    return result.results[0]["out_x"].reshape(B, C, H, W)
```

```python
from contextlib import ExitStack

import numpy as np

import concourse.bass as bass
from concourse import mybir

ALU = mybir.AluOpType
ACT = mybir.ActivationFunctionType
F32 = mybir.dt.float32
F32R = mybir.dt.float32r
AX = mybir.AxisListType

P = 128
B, C, H, W = 8, 64, 32, 32
HALVES = 2
IMAGES = B // HALVES
PIX = H * W
N = IMAGES * PIX
TILES = N // P
BANK = 512

HEADS = 2
HK = C // HEADS
CM = 16
class Mixture:
    def __init__(self, experts, hidden):
        self.experts, self.hidden = experts, hidden


SWIGLU = Mixture(experts=16, hidden=128)
GELU = Mixture(experts=8, hidden=256)
CHUNK = 256
CHUNKS = N // CHUNK
SLOTS = HALVES * CHUNK // P
LOW_GATES = 32
GATE_ROWS = LOW_GATES + 16
LOWEST = -3.0e38
LN_TILES = 4


def spread(ap, axis, count):
    shape = list(ap.shape)
    shape.insert(axis, count)
    return ap.unsqueeze(axis).broadcast_to(shape)



def layer_norm(k, turn, eps, loads, router=None, stats=None):
    nc, x, xn = k.nc, k.x, k.xn
    WIDE = LN_TILES * P
    STEPS = N // WIDE
    ROWS = LN_TILES * HALVES
    t = turn * STEPS
    s, g = k.ln, k.gt
    with ExitStack() as ctx:
        def sb(name, shape):
            return ctx.enter_context(nc.sbuf_tensor(f"ln{turn}_{name}", shape, F32))

        def ps(name, shape):
            return ctx.enter_context(nc.psum_tensor(f"ln{turn}_{name}", shape, F32))
        square = sb("square", [P, 2, WIDE])
        dev = sb("dev", [ROWS, 2, P])
        scale = sb("scale", [ROWS, 2, P])
        mean = ps("mean", [P, 2, WIDE])
        var = ps("var", [ROWS, 2, BANK])
        wide = ps("wide", [P, 2, WIDE])
        if router:
            top_two, w = router
            raw = ps("raw", [P, TILES, HALVES * top_two.experts])
        block = ctx.enter_context(nc.Block())

        @block.sync
        def _(sp):
            if turn == 0:
                for j in range(1, IMAGES):
                    load_image(k, sp, j)
            for to, source, semaphore in loads:
                sp.dma_start(to, source).then_inc(semaphore, 16)

        def cols(i):
            return slice(i * WIDE, (i + 1) * WIDE)

        def staggered(*stages):
            for n in range(STEPS + len(stages) - 1):
                for behind, stage in enumerate(stages):
                    if 0 <= n - behind < STEPS:
                        stage(n - behind)

        @block.tensor
        def _(pe):
            def means(i):
                if i >= 2:
                    pe.wait_ge(s.squared, t + i - 1)
                if turn == 0:
                    pe.wait_ge(k.image_loaded[i * WIDE // PIX], 16 * HALVES)
                pe.matmul(mean[:, i % 2, :], k.centring[:], x[:, cols(i)],
                          start=True, stop=True).then_inc(s.mean, 1)

            def variances(i):
                pe.wait_ge(s.squared, t + i + 1)
                if i >= 2:
                    pe.wait_ge(s.dev, t + i - 1)
                for q in range(LN_TILES):
                    last = pe.matmul(var[:, i % 2, 0:P],
                                     k.shifted[:, ROWS - HALVES * (q + 1):2 * ROWS - HALVES * (q + 1)],
                                     square[:, i % 2, q * P:(q + 1) * P],
                                     start=(q == 0), stop=(q == LN_TILES - 1))
                last.then_inc(s.var, 1)

            def scales(i):
                pe.wait_ge(s.scale, t + i + 1)
                if i >= 2:
                    pe.wait_ge(s.normed, t + i - 1)
                for q in range(LN_TILES):
                    last = pe.matmul(wide[:, i % 2, q * P:(q + 1) * P], k.rows[:, q * P:(q + 1) * P],
                                     scale[:, i % 2, :], start=True, stop=True)
                last.then_inc(s.wide, 1)

            def route(i):
                if i == 0:
                    pe.wait_ge(w.loaded, w.all)
                pe.wait_ge(s.normed, t + i + 1)
                for q in range(i * LN_TILES, (i + 1) * LN_TILES):
                    last = pe.matmul(raw[:, q, :], xn[:, q * P:(q + 1) * P], w.router[:], start=True, stop=True)
                last.then_inc(g.logits, 1)

            if turn == 0:
                pe.wait_ge(k.constants, k.constants_all)
            staggered(means, variances, scales, *([route] if router else []))
            if turn == 0:
                pe.wait_ge(k.more_constants, 16 * 2)

        @block.scalar
        def _(act):
            def squares(i):
                act.wait_ge(s.mean, t + i + 1)
                act.copy(xn[:, cols(i)], mean[:, i % 2, :]).then_inc(s.centred, 1)
                if i >= 2:
                    act.wait_ge(s.var, t + i - 1)
                act.activation(square[:, i % 2, :], mean[:, i % 2, :], ACT.Square).then_inc(s.squared, 1)

            def deviations(i):
                act.wait_ge(s.var, t + i + 1)
                if i >= 2:
                    act.wait_ge(s.scale, t + i - 1)
                act.activation(dev[:, i % 2, :], var[:, i % 2, 0:P], ACT.Sqrt,
                               bias=k.eps[eps][0:ROWS]).then_inc(s.dev, 1)

            def highs(i):
                act.wait_ge(s.normed, t + i + 1)
                for h in range(HALVES):
                    half = slice(h * C, (h + 1) * C)
                    act.copy(k.parts[half, h, cols(i)], xn[half, cols(i)]).then_inc(g.high, 1)

            def weights(i):
                if i == 0:
                    act.wait_ge(w.loaded, w.all)
                size = w.first.shape[1]
                piece = slice(i * size // STEPS, (i + 1) * size // STEPS)
                act.copy(w.high[:, piece], w.first[:, piece]).then_inc(g.first_high, 1)

            if router:
                staggered(squares, deviations, weights, highs)
            else:
                staggered(squares, deviations)

        @block.vector
        def _(dve):
            def scales(i):
                dve.wait_ge(s.dev, t + i + 1)
                if i >= 2:
                    dve.wait_ge(s.wide, t + i - 1)
                dve.reciprocal(scale[:, i % 2, :], dev[:, i % 2, :]).then_inc(s.scale, 1)

            def norm(i):
                dve.wait_ge(s.centred, t + i + 1)
                dve.wait_ge(s.wide, t + i + 1)
                dve.tensor_tensor(xn[:, cols(i)], xn[:, cols(i)], wide[:, i % 2, :],
                                  ALU.mult).then_inc(s.normed, 1)

            def lows(i):
                for h in range(HALVES):
                    half, other = slice(h * C, (h + 1) * C), slice((1 - h) * C, (2 - h) * C)
                    dve.wait_ge(g.high, (k.mixtures * STEPS + i) * HALVES + h + 1)
                    dve.tensor_tensor(k.parts[other, h, cols(i)], xn[half, cols(i)],
                                      k.parts[half, h, cols(i)].bitcast(F32), ALU.subtract)

            if router:
                staggered(scales, norm, lows)
                dve.wait_ge(g.logits, (k.mixtures + 1) * STEPS)
                dve.tensor_tensor(top_two.logits[:],
                                  raw[:].rearrange("p t (h e) -> p (t h) e", e=top_two.experts),
                                  spread(w.router_bias[:], 1, top_two.tiles), ALU.add)
            elif stats:
                def statistics(i):
                    dve.wait_ge(s.normed, t + i + 1)
                    ins = dve.bn_stats(stats[:, i, :], xn[:, cols(i)])
                    if i == STEPS - 1:
                        ins.then_inc(k.bn.stats, 1)

                staggered(scales, norm, statistics)
                dve.wait_ge(k.bn.stats, 1)
            else:
                staggered(scales, norm)

        if router:
            @block.gpsimd
            def _(pool):
                size = w.first.shape[1]
                pool.wait_ge(w.loaded, w.all)
                second = w.second[:, 0:w.second_parts.shape[1] * C].rearrange("p (n c) -> p n c", c=C)
                if w.bias2_parts is not None:
                    pool.tensor_copy(w.bias2_parts[:, 0:C], w.bias2[:])
                pool.tensor_copy(w.second_parts[:, :, 0:C], second).then_inc(g.w_high, 1)
                pool.wait_ge(g.w_high, k.mixtures + 1)
                pool.tensor_tensor(w.second_parts[:, :, C:2 * C], second, w.second_parts[:, :, 0:C].bitcast(F32),
                                   ALU.subtract)
                if w.bias2_parts is not None:
                    pool.tensor_tensor(w.bias2_parts[:, C:2 * C], w.bias2[:], w.bias2_parts[:, 0:C].bitcast(F32),
                                       ALU.subtract)
                for i in range(STEPS):
                    pool.wait_ge(g.first_high, k.mixtures * STEPS + i + 1)
                    piece = slice(i * size // STEPS, (i + 1) * size // STEPS)
                    pool.tensor_tensor(w.low[:, piece], w.first[:, piece], w.high[:, piece].bitcast(F32),
                                       ALU.subtract)
                if k.mixtures == 0:
                    E = SWIGLU.experts
                    pool.tensor_tensor(k.selection[:].rearrange("p (e c) -> p e c", c=P),
                                       spread(k.identity[0:GATE_ROWS, 0:E], 2, P),
                                       spread(k.identity[0:GATE_ROWS, LOW_GATES:LOW_GATES + E], 2, P), ALU.add)



class TopTwo:

    STEPS = 17

    def __init__(self, k, ctx, m):
        def sb(name, shape):
            return ctx.enter_context(k.nc.sbuf_tensor(f"gt{k.mixtures}_{name}", shape, F32))
        self.k, self.experts = k, m.experts
        T = self.tiles = HALVES * TILES
        self.logits, self.equal, self.rank = (sb(n, [P, T, m.experts]) for n in ("logits", "equal", "rank"))
        self.one_hot = [sb(f"one_hot{i}", [P, T, m.experts]) for i in range(2)]
        self.best = [sb(f"best{i}", [P, T]) for i in range(2)]
        self.place, self.small = sb("place", [P, T]), sb("small", [P, 4, T])
        self.step = k.mixtures * self.STEPS

    def done(self, dve, ins):
        self.step += 1
        ins.then_inc(self.k.gt.step, 1)
        dve.wait_ge(self.k.gt.step, self.step)

    def pick(self, dve, i):
        k, E, T = self.k, self.experts, self.tiles
        logits, equal, rank, place, hot, best = (self.logits, self.equal, self.rank, self.place,
                                                 self.one_hot[i], self.best[i])
        self.done(dve, dve.tensor_reduce(best[:], logits[:], AX.X, ALU.max))
        self.done(dve, dve.tensor_tensor(equal[:], logits[:], spread(best[:], 2, E), ALU.is_equal))
        self.done(dve, dve.tensor_tensor(rank[:], equal[:], spread(k.countdown[:, 0:E], 1, T), ALU.mult))
        self.done(dve, dve.tensor_reduce(place[:], rank[:], AX.X, ALU.max))
        self.done(dve, dve.tensor_tensor(hot[:], rank[:], spread(place[:], 2, E), ALU.is_equal))
        if i == 0:
            self.done(dve, dve.scalar_tensor_tensor(out=logits[:], in0=hot[:], scalar=LOWEST, in1=logits[:],
                                                    op0=ALU.mult, op1=ALU.add))
        else:
            dve.tensor_tensor(self.small[:, 0, :], best[:], self.best[0][:], ALU.subtract).then_inc(k.gt.gap, 1)

    def exponential(self, act):
        act.wait_ge(self.k.gt.gap, self.k.mixtures + 1)
        act.activation(self.small[:, 1, :], self.small[:, 0, :], ACT.Exp).then_inc(self.k.gt.exp, 1)

    def gates(self, dve):
        k, E, T, small = self.k, self.experts, self.tiles, self.small
        dve.wait_ge(k.gt.exp, k.mixtures + 1)
        self.done(dve, dve.tensor_scalar(small[:, 2, :], small[:, 1, :], 1.0, None, ALU.add))
        self.done(dve, dve.reciprocal(small[:, 3, :], small[:, 2, :]))
        self.done(dve, dve.tensor_tensor(small[:, 2, :], small[:, 1, :], small[:, 3, :], ALU.mult))
        self.done(dve, dve.tensor_tensor(self.equal[:], self.one_hot[0][:], spread(small[:, 3, :], 2, E), ALU.mult))
        self.done(dve, dve.tensor_tensor(self.rank[:], self.one_hot[1][:], spread(small[:, 2, :], 2, E), ALU.mult))
        self.done(dve, dve.tensor_tensor(k.gate[:, 0:T * E].rearrange("p (t e) -> p t e", e=E), self.equal[:],
                                         self.rank[:], ALU.add))
        assert self.step == (k.mixtures + 1) * self.STEPS


def mixture(k, turn, m, w, swiglu, top_two, last_layer):
    nc, x = k.nc, k.x
    E = m.experts
    COLS = HALVES * CHUNK
    F = m.hidden // P
    RING = 4
    LAG = 3
    ADD_AT = LAG + 1 if swiglu else LAG
    ACTS = 1 if swiglu else F
    REST = slice(5 * COLS // 8, COLS)
    split = ((0, slice(0, COLS)),) if swiglu else ((0, slice(0, REST.start)), (1, slice(0, COLS)))
    s = k.mx
    eb, rb, hb, gb, cb, db = (k.mx_base[n] for n in ("expert", "gelu", "swiglu", "tile", "step", "picked"))
    with ExitStack() as ctx:
        def sb(name, shape, dt=F32):
            return ctx.enter_context(nc.sbuf_tensor(f"mx{turn}_{name}", shape, dt))

        def ps(name, shape):
            return ctx.enter_context(nc.psum_tensor(f"mx{turn}_{name}", shape, F32))
        hidden = sb("hidden", [P, RING, F, COLS])
        high, low = sb("hidden_high", [P, RING, F, COLS], F32R), sb("hidden_low", [P, RING, F, COLS], F32R)
        own_gates = sb("own_gates", [P, SLOTS, E])
        gate_parts = sb("gate_parts", [GATE_ROWS, 2, COLS], F32R)
        first = ps("first", [P, 2, 2, COLS])
        spread_gate = ps("spread_gate", [P, COLS])
        out = ps("out", [P, 2, COLS])
        turned = ps("turned", [E, COLS])
        block = ctx.enter_context(nc.Block())

        def loop(eng, step):
            step(0, 0, None)
            step(1, 1, 0)
            with eng.Fori(1, CHUNKS // 2, 1) as pair:
                step(2 * pair, 0, 2 * pair - 1)
                step(2 * pair + 1, 1, 2 * pair)

        def follows(n, count):
            return not (isinstance(n, int) and n < count)

        @block.tensor
        def _(pe):
            def first_layer(i, e):
                n = i * E + e
                tokens = k.parts[:, :, bass.ds(i * CHUNK, CHUNK)]
                for f in range(2):
                    if follows(n, 2):
                        if swiglu and f == 1:
                            pe.wait_ge(s.hidden, hb + n - 1)
                        else:
                            pe.wait_ge(s.act, gb + (n - 2) * ACTS + f + 1)
                    place = slice((e * 2 + f) * P, (e * 2 + f + 1) * P)
                    pe.matmul(first[:, e % 2, f, :], w.high[:, place], tokens, start=True, stop=False)
                    pe.matmul(first[:, e % 2, f, :], w.low[:, place], tokens,
                              start=False, stop=True).then_inc(s.first, 1)

            def spread_gates(i, e, bank):
                n = i * E + e
                if e == 0:
                    pe.wait_ge(s.gate_low, db + i + 1)
                if follows(n, 1):
                    pe.wait_ge(s.gated, gb + n * F)
                if e == E - 1 and not swiglu:
                    pe.matmul(out[:, bank, :], w.bias2_parts[:], gate_parts[:, bank, :], start=False, stop=False)
                pe.matmul(spread_gate[:], k.selection[:, e * P:(e + 1) * P], gate_parts[:, bank, :],
                          start=True, stop=True).then_inc(s.spread, 1)

            def second_layer(i, e, bank):
                n = i * E + e
                pe.wait_ge(s.low, eb + n + 1)
                if not swiglu:
                    pe.wait_ge(s.low_rest, rb + n + 1)
                if e == 0 and follows(i, 2):
                    pe.wait_ge(s.added, cb + i - 1)
                for f in range(F):
                    for part in (high, low):
                        last = pe.matmul(out[:, bank, :], w.second_parts[:, e * F + f, :],
                                         part[:, e % RING, f, :], start=(e == 0 and f == 0 and part is high),
                                         stop=(e == E - 1 and f == F - 1 and part is low))
                last.then_inc(s.second, 1)

            def turn_gates(i):
                pe.wait_ge(s.own_gates, db + i + 1)
                if follows(i, 1):
                    pe.wait_ge(s.gate_low, db + i)
                for q in range(SLOTS):
                    tile, half = q // HALVES, q % HALVES
                    last = pe.transpose(turned[:, half * CHUNK + tile * P:half * CHUNK + (tile + 1) * P],
                                        own_gates[:, q, :], k.identity[:])
                last.then_inc(s.gates_turned, 1)

            def step(i, bank, before):
                for e in range(E):
                    first_layer(i, e)
                    if before is None and e == 0:
                        turn_gates(0)
                    spread_gates(i, e, bank)
                    if e >= LAG:
                        second_layer(i, e - LAG, bank)
                    elif before is not None:
                        second_layer(before, E - LAG + e, 1 - bank)
                    if e == E // 2 - 2:
                        turn_gates(i + 1)

            loop(pe, step)
            for e in range(E - LAG, E):
                second_layer(CHUNKS - 1, e, 1)

        @block.scalar
        def _(act):
            def activate(i, e):
                n = i * E + e
                for f in range(ACTS):
                    act.wait_ge(s.first, 2 * eb + 2 * n + f + 1)
                    if follows(n, RING) and f == 0:
                        act.wait_ge(s.low, eb + n - RING + 1)
                        if not swiglu:
                            act.wait_ge(s.low_rest, rb + n - RING + 1)
                    if swiglu:
                        ins = act.activation(hidden[:, e % RING, f, :], first[:, e % 2, f, :], ACT.Silu)
                    else:
                        ins = act.activation(hidden[:, e % RING, f, :], first[:, e % 2, f, :], ACT.Gelu,
                                             bias=w.bias1[:, e * F + f:e * F + f + 1])
                    ins.then_inc(s.act, 1)

            def split_high(i, e):
                n = i * E + e
                for f, cols in split:
                    if swiglu:
                        act.wait_ge(s.hidden, hb + n + 1)
                    else:
                        act.wait_ge(s.gated, gb + n * F + f + 1)
                    if follows(n, RING) and f == 0:
                        act.wait_ge(s.second, eb + n - RING + 1)
                    act.copy(high[:, e % RING, f, cols], hidden[:, e % RING, f, cols]).then_inc(s.high, 1)

            def high_gates(i, bank):
                act.wait_ge(s.gates_turned, db + i + 1)
                if follows(i, 2):
                    act.wait_ge(s.spread, eb + (i - 1) * E)
                act.copy(gate_parts[0:E, bank, :], turned[:]).then_inc(s.gate_high, 1)

            def step(i, bank, before):
                for e in range(E):
                    activate(i, e)
                    if e > 0:
                        split_high(i, e - 1)
                    elif before is not None:
                        split_high(before, E - 1)
                    if e == E // 2:
                        high_gates(i + 1, 1 - bank)

            top_two.exponential(act)
            act.wait_ge(s.cleared, k.mixtures + 1)
            high_gates(0, 0)
            loop(act, step)
            split_high(CHUNKS - 1, E - 1)

        @block.vector
        def _(dve):
            def multiply(i, e):
                n = i * E + e
                dve.wait_ge(s.spread, eb + n + 1)
                for f in range(F):
                    own = hidden[:, e % RING, f, :]
                    dve.wait_ge(s.act, gb + n * ACTS + f + 1)
                    dve.tensor_tensor(own, spread_gate[:], own, ALU.mult).then_inc(s.gated, 1)
                if swiglu:
                    dve.wait_ge(s.first, 2 * eb + 2 * n + 2)
                    dve.wait_ge(s.gated, gb + n + 1)
                    dve.tensor_tensor(own, first[:, e % 2, 1, :], own, ALU.mult).then_inc(s.hidden, 1)

            def split_rest(i, e):
                n = i * E + e
                own = hidden[:, e % RING, 0, REST]
                dve.wait_ge(s.gated, gb + n * F + 1)
                if follows(n, RING):
                    dve.wait_ge(s.second, eb + n - RING + 1)
                dve.tensor_copy(high[:, e % RING, 0, REST], own).then_inc(s.high_rest, 1)
                dve.wait_ge(s.high_rest, rb + n + 1)
                dve.tensor_tensor(low[:, e % RING, 0, REST], own, high[:, e % RING, 0, REST].bitcast(F32),
                                  ALU.subtract).then_inc(s.low_rest, 1)

            def pick_gates(i):
                if follows(i, 1):
                    dve.wait_ge(s.gates_turned, db + i)
                tiles = k.gate[:, bass.ds(i * SLOTS * E, SLOTS * E)]
                dve.tensor_scalar(own_gates[:].rearrange("p t e -> p (t e)"), tiles, 1.0, None,
                                  ALU.mult).then_inc(s.own_gates, 1)

            def add(i, bank, parts):
                dve.wait_ge(s.second, eb + (i + 1) * E)
                for part in parts:
                    for h in range(HALVES):
                        place = x[h * C:(h + 1) * C, bass.ds(i * CHUNK, CHUNK)]
                        if part == 1:
                            dve.wait_ge(s.added_high, HALVES * (cb + i) + h + 1)
                        ins = dve.tensor_tensor(place, place, out[part * C:(part + 1) * C, bank,
                                                                  h * CHUNK:(h + 1) * CHUNK], ALU.add)
                        if part == 0:
                            ins.then_inc(s.added_high, 1)
                        elif h == HALVES - 1:
                            ins.then_inc(s.added, 1)

            def low_gates(i, bank):
                dve.wait_ge(s.gate_high, db + i + 1)
                dve.tensor_tensor(gate_parts[LOW_GATES:LOW_GATES + E, bank, :], turned[:],
                                  gate_parts[0:E, bank, :].bitcast(F32), ALU.subtract).then_inc(s.gate_low, 1)

            def step(i, bank, before):
                for e in range(E):
                    multiply(i, e)
                    if not swiglu:
                        split_rest(i, e)
                    if e == 0:
                        pick_gates(i + 1)
                    if e == E // 2 + 1:
                        low_gates(i + 1, 1 - bank)
                    if ADD_AT <= e < ADD_AT + 2 and before is not None:
                        add(before, 1 - bank, [e - ADD_AT])

            dve.memset(k.gate[:, HALVES * TILES * E:(HALVES * TILES + SLOTS) * E], 0.0)
            for i in range(2):
                top_two.pick(dve, i)
            top_two.gates(dve)
            pick_gates(0)
            low_gates(0, 0)
            loop(dve, step)
            add(CHUNKS - 1, 1, [0, 1])

        @block.gpsimd
        def _(pool):
            def split_low(i, e):
                n = i * E + e
                for f, cols in split:
                    pool.wait_ge(s.high, gb + n * F + f + 1)
                    last = pool.tensor_tensor(low[:, e % RING, f, cols], hidden[:, e % RING, f, cols],
                                              high[:, e % RING, f, cols].bitcast(F32), ALU.subtract)
                last.then_inc(s.low, 1)

            def step(i, bank, before):
                for e in range(E):
                    split_low(i, e)

            pool.memset(gate_parts[:].bitcast(F32), 0.0).then_inc(s.cleared, 1)
            loop(pool, step)

        if last_layer:
            @block.sync
            def _(sp):
                for j in range(IMAGES):
                    sp.wait_ge(s.added, cb + (j + 1) * PIX // CHUNK)
                    store_image(k, sp, j)
                sp.wait_ge(k.stored, 16 * HALVES * IMAGES)

    k.mx_base["expert"] += E * CHUNKS
    k.mx_base["gelu"] += 0 if swiglu else E * CHUNKS
    k.mx_base["swiglu"] += E * CHUNKS if swiglu else 0
    k.mx_base["tile"] += E * CHUNKS * F
    k.mx_base["step"] += CHUNKS
    k.mx_base["picked"] += CHUNKS + 1



def conv0(k, layer, turn):
    nc, x, xn, s = k.nc, k.x, k.xn, k.c0
    QUADS = HALVES * HEADS
    GROUP = 4
    GROUPS = TILES // GROUP
    with ExitStack() as ctx:
        def sb(name, shape):
            return ctx.enter_context(nc.sbuf_tensor("c0_" + name, shape, F32))
        wk, wqv, cols = sb("wk", [P, P]), sb("wqv", [P, 2 * P]), sb("cols", [P, 5])
        bqv, wrep, fc = sb("bqv", [P, 2 * P]), sb("wrep", [HK, HEADS * C]), sb("fc", [1, 14])
        halves, quads, heads = sb("halves", [P, P]), sb("quads", [P, QUADS]), sb("heads", [P, P])
        gamma, beta, bk, b_rep, b_se = (cols[:, i:i + 1] for i in range(5))
        loads = layer_loads(k, [(wk, "c0_wk"), (wqv, "c0_wqv"), (cols, "c0_cols"), (wrep, "c0_wrep"), (fc, "c0_fc"),
                  (halves, "halves"), (quads, "quads"), (heads, "heads")], [(bqv, "c0_bqv")])
        assert LN_TILES * P == BANK
        stats = sb("stats", [P, N // BANK, 6])
        layer_norm(k, turn, 1e-6, loads, stats=stats)
        batch_norm(k, stats, halves, gamma, beta)

        key = sb("key", [P, N])
        qv = sb("qv", [P, TILES, 2 * P])
        key_t = sb("key_t", [P, TILES, P])
        query = sb("query", [P, N])
        key_max, key_sum = sb("key_max", [P, IMAGES]), sb("key_sum", [P, IMAGES])
        key_scale = sb("key_scale", [P, IMAGES])
        q_max, q_sum = sb("q_max", [P, TILES, QUADS]), sb("q_sum", [P, TILES, QUADS])
        context, rows = sb("context", [P, IMAGES, HK]), sb("rows", [P, IMAGES])
        tiny = sb("tiny", [1, 8, 2 * HALVES * IMAGES * HEADS])
        gate_row = sb("gate_row", [1, IMAGES * P])
        context_t = sb("context_t", [HK, IMAGES, P])
        matrix = sb("matrix", [P, IMAGES, P])
        ps = ctx.enter_context(nc.psum_tensor("c0_ps", [P, 8, BANK], F32))
        key_ps = ps[:, 0:2, :]
        block = ctx.enter_context(nc.Block())

        def q_quarter(r):
            return qv[:, r * 8:(r + 1) * 8, 0:P].rearrange("p t (g c) -> p t g c", c=HK)

        @block.tensor
        def _(pe):
            for c in range(N // BANK):
                if c >= 2:
                    pe.wait_ge(s.key, c - 1)
                pe.matmul(ps[:, c % 2, :], wk[:], xn[:, c * BANK:(c + 1) * BANK],
                          start=True, stop=True).then_inc(s.key_ps, 1)
            for g in range(GROUPS):
                if g >= 2:
                    pe.wait_ge(s.qv, g - 1)
                for t in range(GROUP):
                    tile = g * GROUP + t
                    last = pe.matmul(ps[:, 2 + 2 * (g % 2) + t // 2, (t % 2) * 2 * P:(t % 2 + 1) * 2 * P],
                                     xn[:, tile * P:(tile + 1) * P], wqv[:], start=True, stop=True)
                last.then_inc(s.qv_ps, 1)
            for g in range(2 * GROUPS):
                if g < GROUPS:
                    pe.wait_ge(s.key_exp, g // 2 + 1)
                else:
                    pe.wait_ge(s.q_soft, (g - GROUPS) // 2 + 1)
                if g >= 2:
                    pe.wait_ge(s.turned, g - 1)
                for t in range(GROUP):
                    tile = (g % GROUPS) * GROUP + t
                    source = key[:, tile * P:(tile + 1) * P] if g < GROUPS else qv[:, tile, 0:P]
                    last = pe.transpose(ps[:, 6 + g % 2, t * P:(t + 1) * P], source, k.identity[:])
                last.then_inc(s.turned_ps, 1)
                if g == GROUPS + 1:
                    pe.wait_ge(s.turned, GROUPS)
                    pe.wait_ge(s.key, N // BANK)
                    for j in range(IMAGES):
                        for t in range(PIX // P):
                            tile = j * (PIX // P) + t
                            last = pe.matmul(ps[:, 0, j * P:(j + 1) * P], key_t[:, tile, :],
                                             qv[:, tile, P:2 * P], start=(t == 0), stop=(t == PIX // P - 1))
                    last.then_inc(s.small_ps, 1)
            pe.wait_ge(s.small, 1)
            for j in range(IMAGES):
                last = pe.matmul(ps[0:1, 1, j * QUADS:(j + 1) * QUADS], rows[:, j:j + 1], quads[:],
                                 start=True, stop=True)
            last.then_inc(s.small_ps, 1)
            pe.wait_ge(s.small, 2)
            for j in range(IMAGES):
                last = pe.matmul(ps[:, 1, 32 + j:33 + j], gate_row[:, j * P:(j + 1) * P],
                                 k.identity[0:1, 0:1], start=True, stop=True)
            last.then_inc(s.small_ps, 1)
            pe.wait_ge(s.small, 3)
            for j in range(IMAGES):
                last = pe.matmul(ps[0:HK, 2, j * P:(j + 1) * P], context[:, j, :], heads[:],
                                 start=True, stop=True)
            last.then_inc(s.small_ps, 1)
            pe.wait_ge(s.small, 4)
            for g in range(QUADS):
                for j in range(IMAGES):
                    last = pe.matmul(ps[g * HK:(g + 1) * HK, 3, j * C:(j + 1) * C],
                                     context_t[:, j, g * HK:(g + 1) * HK],
                                     wrep[:, (g % HEADS) * C:(g % HEADS + 1) * C], start=True, stop=True)
            last.then_inc(s.small_ps, 1)
            pe.wait_ge(s.small, 5)
            pe.wait_ge(s.turned, 2 * GROUPS)
            for c in range(N // BANK):
                if c >= 2:
                    pe.wait_ge(s.added, c - 1)
                pe.matmul(ps[:, 6 + c % 2, :], matrix[:, c // 2, :], query[:, c * BANK:(c + 1) * BANK],
                          start=True, stop=True).then_inc(s.out_ps, 1)

        @block.gpsimd
        def _(pool):
            for r in range(4):
                pool.wait_ge(s.q_max, r + 1)
                pool.tensor_tensor(q_quarter(r), q_quarter(r), spread(q_max[:, r * 8:(r + 1) * 8, :], 3, HK),
                                   ALU.subtract).then_inc(s.q_shift, 1)

        @block.scalar
        def _(act):
            for c in range(N // BANK):
                act.wait_ge(s.key_ps, c + 1)
                act.activation(key[:, c * BANK:(c + 1) * BANK], ps[:, c % 2, :], ACT.Identity,
                               bias=bk).then_inc(s.key, 1)
            for j in range(IMAGES):
                act.wait_ge(s.key_max, j + 1)
                act.activation(key[:, j * PIX:(j + 1) * PIX], key[:, j * PIX:(j + 1) * PIX], ACT.Exp,
                               bias=key_max[:, j:j + 1],
                               accum_out=key_sum[:, j:j + 1]).then_inc(s.key_exp, 1)
            for r in range(4):
                act.wait_ge(s.q_shift, r + 1)
                act.activation(q_quarter(r), q_quarter(r), ACT.Exp).then_inc(s.q_exp, 1)
            for g in range(2 * GROUPS):
                act.wait_ge(s.turned_ps, g + 1)
                to = (key_t[:, g * GROUP:(g + 1) * GROUP, :].rearrange("p t c -> p (t c)") if g < GROUPS
                      else query[:, (g - GROUPS) * BANK:(g - GROUPS + 1) * BANK])
                act.copy(to, ps[:, 6 + g % 2, :]).then_inc(s.turned, 1)
            act.wait_ge(s.sigmoid, 1)
            act.activation(tiny[:, 5, 0:16], tiny[:, 4, 0:16], ACT.Exp, scale=-1.0).then_inc(s.gate_exp, 1)

        @block.vector
        def _(dve):
            step = [0]

            def done(ins):
                step[0] += 1
                ins.then_inc(s.step, 1)
                dve.wait_ge(s.step, step[0])

            dve.memset(matrix[:], 0.0)
            for j in range(IMAGES):
                dve.wait_ge(s.key, 2 * (j + 1))
                dve.tensor_reduce(key_max[:, j:j + 1], key[:, j * PIX:(j + 1) * PIX], AX.X, ALU.max,
                                  negate=True).then_inc(s.key_max, 1)
            for g in range(GROUPS):
                dve.wait_ge(s.qv_ps, g + 1)
                b = 2 + 2 * (g % 2)
                dve.tensor_tensor(qv[:, g * GROUP:(g + 1) * GROUP, :],
                                  ps[:, b:b + 2, :].rearrange("p b (t c) -> p (b t) c", t=2),
                                  spread(bqv[:], 1, GROUP), ALU.add).then_inc(s.qv, 1)
            for r in range(4):
                dve.wait_ge(s.qv, 2 * (r + 1))
                dve.tensor_reduce(q_max[:, r * 8:(r + 1) * 8, :], q_quarter(r), AX.X, ALU.max).then_inc(s.q_max, 1)
            for r in range(4):
                dve.wait_ge(s.q_exp, r + 1)
                done(dve.tensor_reduce(q_sum[:, r * 8:(r + 1) * 8, :], q_quarter(r), AX.X, ALU.add))
                done(dve.reciprocal(q_max[:, r * 8:(r + 1) * 8, :], q_sum[:, r * 8:(r + 1) * 8, :]))
                dve.tensor_tensor(q_quarter(r), q_quarter(r), spread(q_max[:, r * 8:(r + 1) * 8, :], 3, HK),
                                  ALU.mult).then_inc(s.q_soft, 1)
            dve.wait_ge(s.key_exp, IMAGES)
            done(dve.reciprocal(key_scale[:], key_sum[:]))
            dve.wait_ge(s.small_ps, 1)
            product = ps[:, 0, :].rearrange("p (j c) -> p j c", c=P)
            for g in range(QUADS):
                q = slice(g * HK, (g + 1) * HK)
                last = dve.tensor_tensor(context[q], product[q, :, q], spread(key_scale[q, :], 2, HK), ALU.mult)
            done(last)
            dve.tensor_reduce(rows[:], context[:], AX.X, ALU.add).then_inc(s.small, 1)
            dve.wait_ge(s.small_ps, 2)
            BT = HALVES * IMAGES
            done(dve.tensor_copy(tiny[:, 0, 0:16], ps[0:1, 1, 0:16]))
            source = tiny[:, 0, 0:16]
            for i, (wo, bo) in enumerate(((0, 4), (6, 10))):
                w4 = fc[:, wo:wo + 4].rearrange("p (m n) -> p m n", n=HEADS)
                prod = tiny[:, 1, 0:32].rearrange("p (t m n) -> p t m n", m=HEADS, n=HEADS)
                done(dve.tensor_tensor(prod, spread(source.rearrange("p (t n) -> p t n", n=HEADS), 2, HEADS),
                                       spread(w4, 1, BT), ALU.mult))
                out = tiny[:, 2 + i, 0:16].rearrange("p (t m) -> p t m", m=HEADS)
                done(dve.tensor_reduce(out, prod, AX.X, ALU.add))
                ins = dve.tensor_tensor(tiny[:, 4 if i else 6, 0:16].rearrange("p (t m) -> p t m", m=HEADS),
                                        out, spread(fc[:, bo:bo + 2], 1, BT), ALU.add)
                if i == 0:
                    done(ins)
                    done(dve.tensor_scalar(tiny[:, 7, 0:16], tiny[:, 6, 0:16], 0.0, None, ALU.max))
                    source = tiny[:, 7, 0:16]
                else:
                    ins.then_inc(s.sigmoid, 1)
            dve.wait_ge(s.gate_exp, 1)
            done(dve.tensor_scalar(tiny[:, 6, 0:16], tiny[:, 5, 0:16], 1.0, None, ALU.add))
            done(dve.reciprocal(tiny[:, 7, 0:16], tiny[:, 6, 0:16]))
            done(dve.tensor_tensor(tiny[:, 1, 0:16].rearrange("p (t n) -> p t n", n=HEADS),
                                   tiny[:, 7, 0:16].rearrange("p (t n) -> p t n", n=HEADS),
                                   spread(fc[:, 12:14], 1, BT), ALU.mult))
            dve.tensor_copy(gate_row[:].rearrange("p (t c) -> p t c", c=HK),
                            spread(tiny[:, 1, 0:16], 2, HK)).then_inc(s.small, 1)
            dve.wait_ge(s.small_ps, 3)
            dve.tensor_tensor(context[:], context[:], spread(ps[:, 1, 32:32 + IMAGES], 2, HK),
                              ALU.mult).then_inc(s.small, 1)
            dve.wait_ge(s.small_ps, 4)
            dve.tensor_scalar(context_t[:].rearrange("p j c -> p (j c)"), ps[0:HK, 2, :], b_se[0:HK], None,
                              ALU.add).then_inc(s.small, 1)
            dve.wait_ge(s.small_ps, 5)
            for h in range(HALVES):
                q = slice(h * C, (h + 1) * C)
                last = dve.tensor_copy(matrix[q, :, q],
                                       ps[q, 3, 0:IMAGES * C].rearrange("p (j c) -> p j c", c=C))
            last.then_inc(s.small, 1)
            for c in range(N // BANK):
                dve.wait_ge(s.out_ps, c + 1)
                place = x[:, c * BANK:(c + 1) * BANK]
                dve.scalar_tensor_tensor(out=place, in0=ps[:, 6 + c % 2, :], scalar=b_rep, in1=place,
                                         op0=ALU.add, op1=ALU.add).then_inc(s.added, 1)
    return turn + 1


def batch_norm(k, stats, halves, gamma, beta):
    nc, xn, s = k.nc, k.xn, k.bn
    with ExitStack() as ctx:
        own = ctx.enter_context(nc.sbuf_tensor("bn_own", [P, 4], F32))
        both = ctx.enter_context(nc.sbuf_tensor("bn_both", [P, 8], F32))
        ps = ctx.enter_context(nc.psum_tensor("bn_ps", [P, 2], F32))
        block = ctx.enter_context(nc.Block())

        @block.tensor
        def _(pe):
            pe.wait_ge(s.own, 1)
            pe.wait_ge(k.fetched_sem, k.fetched)
            pe.matmul(ps[:], halves[:], own[:, 0:2], start=True, stop=True).then_inc(s.both, 1)

        @block.scalar
        def _(act):
            act.wait_ge(s.neg_var, 1)
            act.activation(both[:, 3:4], both[:, 2:3], ACT.Sqrt, bias=k.eps[1e-5][:],
                           scale=-1.0).then_inc(s.dev, 1)

        @block.vector
        def _(dve):
            step = [0]

            def done(ins):
                step[0] += 1
                ins.then_inc(s.step, 1)
                dve.wait_ge(s.step, step[0])

            dve.wait_ge(k.fetched_sem, k.fetched)
            done(dve.bn_aggr(own[:, 2:4], stats[:]))
            dve.tensor_copy(own[:, 0:1], own[:, 2:3])
            dve.scalar_tensor_tensor(out=own[:, 1:2], in0=own[:, 2:3], scalar=own[:, 2:3], in1=own[:, 3:4],
                                     op0=ALU.mult, op1=ALU.add).then_inc(s.own, 1)
            dve.wait_ge(s.both, 1)
            done(dve.tensor_copy(both[:, 0:2], ps[:]))
            dve.scalar_tensor_tensor(out=both[:, 2:3], in0=both[:, 0:1], scalar=both[:, 0:1], in1=both[:, 1:2],
                                     op0=ALU.mult, op1=ALU.subtract).then_inc(s.neg_var, 1)
            dve.wait_ge(s.dev, 1)
            done(dve.reciprocal(both[:, 4:5], both[:, 3:4]))
            done(dve.tensor_tensor(both[:, 5:6], both[:, 4:5], gamma, ALU.mult))
            done(dve.tensor_tensor(both[:, 6:7], both[:, 0:1], both[:, 5:6], ALU.mult))
            done(dve.tensor_tensor(both[:, 7:8], beta, both[:, 6:7], ALU.subtract))
            dve.tensor_scalar(xn[:], xn[:], both[:, 5:6], both[:, 7:8], ALU.mult, ALU.add)



def conv1(k, layer, turn):
    nc, x, xn, s = k.nc, k.x, k.xn, k.c1
    EXPERTS, RED, POOL, TAPS = 8, 16, 4, 9
    CELL = H // POOL
    CELLS = POOL * POOL
    PAD = W + 2
    HALF = H // 2
    KERNEL = TAPS * C
    RING = 4
    with ExitStack() as ctx:
        def sb(name, shape):
            return ctx.enter_context(nc.sbuf_tensor("c1_" + name, shape, F32))
        w1, w2, average = sb("w1", [P, HALVES * RED]), sb("w2", [HALVES * RED, P]), sb("average", [P, P])
        wexp, weight = sb("wexp", [P, EXPERTS * CELLS]), sb("weight", [P, EXPERTS, KERNEL])
        loads = layer_loads(k, [(average, "average"), (w1, "c1_w1"), (w2, "c1_w2"), (weight, "c1_weight")],
                            [(wexp, "c1_wexp")])
        layer_norm(k, turn, 1e-6, loads)
        padded = sb("padded", [P, IMAGES, PAD, PAD])
        row_sum, cells = sb("row_sum", [P, IMAGES * H * POOL]), sb("cells", [P, IMAGES * CELLS])
        total, squeezed = sb("total", [P, IMAGES]), sb("squeezed", [HALVES * RED, IMAGES])
        cell_mean, product = sb("cell_mean", [P, IMAGES, CELLS]), sb("product", [P, IMAGES, EXPERTS, CELLS])
        expert = sb("expert", [P, IMAGES, EXPERTS])
        routing = sb("routing", [P, IMAGES, EXPERTS])
        mixed = sb("mixed", [P, IMAGES, KERNEL])
        kernel = sb("kernel", [P, IMAGES, TAPS, P])
        ps = ctx.enter_context(nc.psum_tensor("c1_ps", [P, RING, BANK], F32))
        tiny = ctx.enter_context(nc.psum_tensor("c1_tiny", [P, BANK], F32))
        block = ctx.enter_context(nc.Block())
        image = xn[:].rearrange("p (j y x) -> p j y x", j=IMAGES, y=H)

        def by_tap(a):
            return a.rearrange("p (t c) -> p t c", c=C)

        @block.gpsimd
        def _(pool):
            pool.memset(padded[:], 0.0).then_inc(s.cleared, 1)
            pool.memset(kernel[:], 0.0).then_inc(s.cleared, 1)

        @block.scalar
        def _(act):
            act.wait_ge(s.cleared, 1)
            for j in range(IMAGES):
                act.copy(padded[:, j, 1:1 + H, 1:1 + W], image[:, j]).then_inc(s.padded, 1)
            act.wait_ge(s.small_ps, 1)
            act.activation(squeezed[:], tiny[0:HALVES * RED, 0:IMAGES], ACT.Relu,
                           scale=1.0 / PIX).then_inc(s.squeezed, 1)
            act.wait_ge(s.logit, 1)
            act.activation(routing[:], expert[:], ACT.Sigmoid).then_inc(s.routing, 1)

        @block.tensor
        def _(pe):
            pe.wait_ge(k.fetched_sem, k.fetched)
            pe.wait_ge(s.total, 1)
            pe.matmul(tiny[0:HALVES * RED, 0:IMAGES], w1[:], total[:], start=True, stop=True).then_inc(s.small_ps, 1)
            pe.wait_ge(s.squeezed, 1)
            pe.matmul(tiny[:, 0:IMAGES], w2[:], squeezed[:], start=True, stop=True)
            pe.matmul(tiny[:, 64:128], average[:], cells[:], start=True, stop=True).then_inc(s.small_ps, 1)
            for c in range(2 * IMAGES):
                j, y = c // 2, (c % 2) * HALF
                pe.wait_ge(s.padded, j + 1)
                pe.wait_ge(s.kernel, j + 1)
                if c >= RING:
                    pe.wait_ge(s.added, c - RING + 1)
                for t in range(TAPS):
                    last = pe.matmul(ps[:, c % RING, :], kernel[:, j, t, :],
                                     padded[:, j, y + t // 3:y + t // 3 + HALF, t % 3:t % 3 + W],
                                     start=(t == 0), stop=(t == TAPS - 1))
                last.then_inc(s.out_ps, 1)

        @block.vector
        def _(dve):
            step = [0]

            def done(ins):
                step[0] += 1
                ins.then_inc(s.step, 1)
                dve.wait_ge(s.step, step[0])

            done(dve.tensor_reduce(row_sum[:], xn[:].rearrange("p (n x) -> p n x", x=CELL), AX.X, ALU.add))
            done(dve.tensor_reduce(cells[:].rearrange("p (j q) -> p j q", q=POOL),
                                   row_sum[:].rearrange("p (j y q) -> p j q y", y=CELL, q=POOL), AX.X, ALU.add))
            dve.tensor_reduce(total[:], cells[:].rearrange("p (j c) -> p j c", c=CELLS), AX.X,
                              ALU.add).then_inc(s.total, 1)
            dve.wait_ge(s.small_ps, 2)
            done(dve.tensor_scalar(cell_mean[:].rearrange("p j c -> p (j c)"), tiny[:, 64:128],
                                   1.0 / (CELL * CELL), None, ALU.mult))
            dve.wait_ge(k.fetched_sem, k.fetched)
            done(dve.tensor_tensor(product[:], spread(cell_mean[:], 2, EXPERTS),
                                   spread(wexp[:].rearrange("p (k c) -> p k c", c=CELLS), 1, IMAGES), ALU.mult))
            done(dve.tensor_reduce(expert[:], product[:], AX.X, ALU.add))
            dve.tensor_tensor(expert[:], expert[:], spread(tiny[:, 0:IMAGES], 2, EXPERTS),
                              ALU.mult).then_inc(s.logit, 1)
            dve.wait_ge(s.routing, 1)
            dve.wait_ge(s.cleared, 2)
            for j in range(IMAGES):
                done(dve.tensor_scalar(mixed[:, j], weight[:, 0], routing[:, j, 0:1], None, ALU.mult))
                for e in range(1, EXPERTS - 1):
                    done(dve.scalar_tensor_tensor(out=mixed[:, j], in0=weight[:, e], scalar=routing[:, j, e:e + 1],
                                                  in1=mixed[:, j], op0=ALU.mult, op1=ALU.add))
                e = EXPERTS - 1
                for h in range(HALVES):
                    q = slice(h * C, (h + 1) * C)
                    last = dve.scalar_tensor_tensor(out=kernel[q, j, :, q], in0=by_tap(weight[q, e]),
                                                    scalar=routing[q, j, e:e + 1], in1=by_tap(mixed[q, j]),
                                                    op0=ALU.mult, op1=ALU.add)
                last.then_inc(s.kernel, 1)
            for c in range(2 * IMAGES):
                dve.wait_ge(s.out_ps, c + 1)
                place = x[:, c * BANK:(c + 1) * BANK]
                dve.tensor_tensor(place, place, ps[:, c % RING, :], ALU.add).then_inc(s.added, 1)
    return turn + 1



def conv2(k, layer, turn):
    nc, x, xn, s = k.nc, k.x, k.xn, k.c2
    K, TAPS, A, ATAPS = 5, 25, 3, 9
    PAD = W + 4
    Q = HALVES * CM
    HALF = H // 2
    with ExitStack() as ctx:
        def sb(name, shape):
            return ctx.enter_context(nc.sbuf_tensor("c2_" + name, shape, F32))
        w, cols = sb("w", [P, Q]), sb("cols", [P, 4])
        row = sb("row", [P, 2 * TAPS + 2 * ATAPS + 4])
        fuse = sb("fuse", [P, 2, P])
        conv_b, adap_b, atrous_b, fuse_b = (cols[:, i:i + 1] for i in range(4))
        loads = layer_loads(k, [(w, "c2_w"), (cols, "c2_cols"), (fuse, "c2_fuse")], [(row, "c2_row")])
        layer_norm(k, turn, 1e-6, loads)
        total, g = sb("total", [P, IMAGES]), sb("g", [P, 1])
        taps, raw = sb("taps", [P, TAPS + ATAPS]), sb("raw", [P, TAPS + ATAPS])
        f = sb("f", [P, PAD, PAD])
        near, far, product = sb("near", [P, H, W]), sb("far", [P, H, W]), sb("product", [P, 2, H, W])
        f_ps = ctx.enter_context(nc.psum_tensor("c2_f_ps", [P, 2, BANK], F32))
        g_ps = ctx.enter_context(nc.psum_tensor("c2_g_ps", [P, BANK], F32))
        out_ps = ctx.enter_context(nc.psum_tensor("c2_out_ps", [P, 2, BANK], F32))
        block = ctx.enter_context(nc.Block())

        @block.tensor
        def _(pe):
            pe.wait_ge(k.fetched_sem, k.fetched)
            for c in range(2):
                for j in range(IMAGES):
                    last = pe.matmul(f_ps[j * Q:(j + 1) * Q, c, :], w[:],
                                     xn[:, j * PIX + c * BANK:j * PIX + (c + 1) * BANK], start=True, stop=True)
                last.then_inc(s.f_ps, 1)
            pe.wait_ge(s.total, 1)
            for j in range(IMAGES):
                last = pe.matmul(g_ps[j * Q:(j + 1) * Q, 0:1], w[:], total[:, j:j + 1], start=True, stop=True)
            last.then_inc(s.g_ps, 1)
            pe.wait_ge(s.near, TAPS)
            pe.wait_ge(s.far, ATAPS)
            for c in range(2 * IMAGES):
                j, y = c // 2, (c % 2) * HALF
                q = slice(j * Q, (j + 1) * Q)
                if c >= 2:
                    pe.wait_ge(s.added, c - 1)
                pe.matmul(out_ps[:, c % 2, :], fuse[q, 0, :], near[q, y:y + HALF, :], start=True, stop=False)
                pe.matmul(out_ps[:, c % 2, :], fuse[q, 1, :], far[q, y:y + HALF, :],
                          start=False, stop=True).then_inc(s.out_ps, 1)

        @block.scalar
        def _(act):
            act.wait_ge(k.fetched_sem, k.fetched)
            act.wait_ge(s.cleared, 1)
            for c in range(2):
                act.wait_ge(s.f_ps, c + 1)
                act.activation(f[:, 2 + c * HALF:2 + (c + 1) * HALF, 2:2 + W],
                               f_ps[:, c, :].rearrange("p (y x) -> p y x", x=W), ACT.Relu,
                               bias=conv_b).then_inc(s.f, 1)
            act.wait_ge(s.g_ps, 1)
            act.activation(g[:], g_ps[:, 0:1], ACT.Relu, bias=conv_b, scale=1.0 / PIX).then_inc(s.g, 1)
            act.wait_ge(s.taps, 1)
            act.wait_ge(s.f, 2)
            for t in range(ATAPS):
                dy, dx = 2 * (t // A), 2 * (t % A)
                view = f[:, dy:dy + H, dx:dx + W]
                if t == 0:
                    act.activation(far[:], view, ACT.Identity, bias=atrous_b,
                                   scale=taps[:, TAPS:TAPS + 1]).then_inc(s.product, 1)
                else:
                    if t >= 3:
                        act.wait_ge(s.far, t - 1)
                    act.activation(product[:, t % 2], view, ACT.Copy,
                                   scale=taps[:, TAPS + t:TAPS + t + 1]).then_inc(s.product, 1)

        @block.gpsimd
        def _(pool):
            pool.memset(f[:], 0.0).then_inc(s.cleared, 1)
            pool.wait_ge(s.product, 1)
            pool.engine_nop().then_inc(s.far, 1)
            for t in range(1, ATAPS):
                pool.wait_ge(s.product, t + 1)
                pool.wait_ge(s.far, t)
                pool.tensor_tensor(far[:], far[:], product[:, t % 2], ALU.add).then_inc(s.far, 1)

        @block.vector
        def _(dve):
            step = [0]

            def done(ins):
                step[0] += 1
                ins.then_inc(s.step, 1)
                dve.wait_ge(s.step, step[0])

            dve.tensor_reduce(total[:], xn[:].rearrange("p (j n) -> p j n", n=PIX), AX.X,
                              ALU.add).then_inc(s.total, 1)
            dve.wait_ge(k.fetched_sem, k.fetched)
            dve.wait_ge(s.g, 1)
            for o, n, b in ((0, TAPS, 0), (TAPS, ATAPS, 2 * TAPS)):
                scalars = 2 * (TAPS + ATAPS) + (0 if o == 0 else 2)
                done(dve.scalar_tensor_tensor(out=raw[:, o:o + n], in0=row[:, b:b + n], scalar=g[:],
                                              in1=row[:, b + n:b + 2 * n], op0=ALU.mult, op1=ALU.add))
                last = dve.tensor_scalar(taps[:, o:o + n], raw[:, o:o + n], row[:, scalars:scalars + 1],
                                         row[:, scalars + 1:scalars + 2], ALU.mult, ALU.add)
            last.then_inc(s.taps, 1)
            dve.wait_ge(s.taps, 1)
            dve.wait_ge(s.f, 2)
            for t in range(TAPS):
                view = f[:, t // K:t // K + H, t % K:t % K + W]
                if t == 0:
                    ins = dve.tensor_scalar(near[:], view, taps[:, 0:1], adap_b, ALU.mult, ALU.add)
                else:
                    dve.wait_ge(s.near, t)
                    ins = dve.scalar_tensor_tensor(out=near[:], in0=view, scalar=taps[:, t:t + 1], in1=near[:],
                                                   op0=ALU.mult, op1=ALU.add)
                ins.then_inc(s.near, 1)
            for c in range(2 * IMAGES):
                dve.wait_ge(s.out_ps, c + 1)
                place = x[:, c * BANK:(c + 1) * BANK]
                dve.scalar_tensor_tensor(out=place, in0=out_ps[:, c % 2, :], scalar=fuse_b, in1=place,
                                         op0=ALU.add, op1=ALU.add).then_inc(s.added, 1)
    return turn + 1



TAPS = 9
TILE_ROWS = P // W
QTILES = PIX // P
REACH = 2
XTILES = QTILES + 1
TAP_GROUP = 3


def conv3(k, layer, turn):
    nc, x, xn, s = k.nc, k.x, k.xn, k.c3
    GN = 2
    PAD = W + 2
    HALF = H // 2
    with ExitStack() as ctx:
        def sb(name, shape, dt=F32):
            return ctx.enter_context(nc.sbuf_tensor("c3_" + name, shape, dt))
        w_off, cols = sb("w_off", [P, TAPS, 4 * TAPS]), sb("cols", [P, 3])
        w_deform = sb("w_deform", [P, TAPS // TAP_GROUP, HALVES * TAP_GROUP * C])
        base, ints, pairs = sb("base", [P, 4 * TAPS]), sb("ints", [P, 2 * H + TILE_ROWS]), sb("pairs", [P, P])
        loads = layer_loads(k, [(w_off, "c3_w_off"), (cols, "c3_cols"), (w_deform, "c3_w_deform"), (base, "c3_base"),
                  (pairs, "pairs")], [(ints, "c3_ints")])
        off_b, gn_gamma, gn_beta = (cols[:, i:i + 1] for i in range(3))
        start_at_one(k, k.c3_near.all + k.c3_rest.all)
        layer_norm(k, turn, 1e-6, loads)
        coords = sb("coords", [P, TILES, 4 * TAPS])
        flag = sb("flag", [1, 2], mybir.dt.int32)
        offsets(k, PAD, HALF, w_off, off_b, coords, flag)
        sums = sb("sums", [P, TILES, HALVES, C])
        band = {ty: [(ty, ty + 1)] for ty in range(QTILES)}
        sample(k, "near", k.c3_near, band, w_deform, coords, base, ints, sums, None)
        rest = {}
        for ty in range(QTILES):
            q0, q1 = band[ty][0]
            rest[ty] = [(a, min(a + 2, end)) for start, end in ((0, q0 - 1), (q1 + 1, XTILES - 1))
                        for a in range(start, end + 1, 3)]
        sample(k, "rest", k.c3_rest, rest, w_deform, coords, base, ints, sums, flag)
        group_norm(k, sums, pairs, gn_gamma, gn_beta)
    return turn + 1


def start_at_one(k, semaphores):
    with ExitStack() as ctx:
        block = ctx.enter_context(k.nc.Block())

        @block.sync
        def _(sp):
            for semaphore in semaphores:
                sp.sem_inc(semaphore, 1)


def offsets(k, PAD, HALF, w_off, off_b, coords, flag):
    nc, xn, s = k.nc, k.xn, k.c3
    ROWS = 4 * TAPS
    LOW_ROW = 64
    PER_BANK = 8
    with ExitStack() as ctx:
        high, low = (ctx.enter_context(nc.sbuf_tensor(f"c3_padded_{n}", [P, IMAGES, PAD, PAD], F32R))
                     for n in ("high", "low"))
        w_parts = ctx.enter_context(nc.sbuf_tensor("c3_w_parts", [P, TAPS, LOW_ROW + ROWS], F32R))
        off = ctx.enter_context(nc.sbuf_tensor("c3_off", [ROWS, N], F32))
        reach = ctx.enter_context(nc.sbuf_tensor("c3_reach", [P, 4], F32))
        most = ctx.enter_context(nc.sbuf_tensor("c3_most", [1, 4], F32))
        ps = ctx.enter_context(nc.psum_tensor("c3_off_ps", [P, 2, BANK], F32))
        turned = ctx.enter_context(nc.psum_tensor("c3_turned", [P, 4, BANK], F32))
        block = ctx.enter_context(nc.Block())

        def image(j):
            return xn[:, j * PIX:(j + 1) * PIX].rearrange("p (y x) -> p y x", x=W)

        def inner(part, j):
            return part[:, j, 1:1 + H, 1:1 + W]

        @block.gpsimd
        def _(pool):
            pool.memset(w_parts[:, :, ROWS:LOW_ROW].bitcast(F32), 0.0).then_inc(s.filled, 1)
            for j in range(IMAGES):
                for part in (high, low):
                    pool.memset(part[:, j].bitcast(F32), 0.0).then_inc(s.cleared, 1)

        @block.scalar
        def _(act):
            act.wait_ge(k.fetched_sem, k.fetched)
            act.copy(w_parts[:, :, 0:ROWS], w_off[:]).then_inc(s.w_high, 1)
            for j in range(IMAGES):
                act.wait_ge(s.cleared, 2 * j + 2)
                act.copy(inner(high, j), image(j)).then_inc(s.high, 1)
            for c in range(N // BANK):
                act.wait_ge(s.off_ps, c + 1)
                act.activation(off[:, c * BANK:(c + 1) * BANK], ps[0:ROWS, c % 2, :], ACT.Identity,
                               bias=off_b[0:ROWS]).then_inc(s.off_high, 1)

        @block.tensor
        def _(pe):
            pe.wait_ge(s.w_low, 1)
            for c in range(2 * IMAGES):
                j, y = c // 2, (c % 2) * HALF
                pe.wait_ge(s.padded, j + 1)
                if c >= 2:
                    pe.wait_ge(s.off, c - 1)
                for t in range(TAPS):
                    for part in (high, low):
                        last = pe.matmul(ps[0:LOW_ROW + ROWS, c % 2, :], w_parts[:, t, :],
                                         part[:, j, y + t // 3:y + t // 3 + HALF, t % 3:t % 3 + W],
                                         start=(t == 0 and part is high), stop=(t == TAPS - 1 and part is low))
                last.then_inc(s.off_ps, 1)
            for t in range(TILES):
                pe.wait_ge(s.off, t * P // BANK + 1)
                last = pe.transpose(turned[:, t // PER_BANK, (t % PER_BANK) * ROWS:(t % PER_BANK + 1) * ROWS],
                                    off[:, t * P:(t + 1) * P], k.identity[0:ROWS, 0:ROWS])
                if t % PER_BANK == PER_BANK - 1:
                    last.then_inc(s.turned, 1)
            pe.wait_ge(s.reach, 1)
            pe.transpose(ps[0:1, 0, 0:P], reach[:, 2:3], k.identity[:]).then_inc(s.reach_ps, 1)

        @block.vector
        def _(dve):
            step = [0]

            def done(ins):
                step[0] += 1
                ins.then_inc(s.step, 1)
                dve.wait_ge(s.step, step[0])

            dve.wait_ge(s.filled, 1)
            dve.wait_ge(s.w_high, 1)
            dve.tensor_tensor(w_parts[:, :, LOW_ROW:LOW_ROW + ROWS], w_off[:], w_parts[:, :, 0:ROWS].bitcast(F32),
                              ALU.subtract).then_inc(s.w_low, 1)
            for j in range(IMAGES):
                dve.wait_ge(s.high, j + 1)
                dve.tensor_tensor(inner(low, j), image(j), inner(high, j).bitcast(F32),
                                  ALU.subtract).then_inc(s.padded, 1)
            for c in range(N // BANK):
                dve.wait_ge(s.off_high, c + 1)
                own = off[:, c * BANK:(c + 1) * BANK]
                dve.tensor_tensor(own, own, ps[LOW_ROW:LOW_ROW + ROWS, c % 2, :], ALU.add).then_inc(s.off, 1)
            dve.wait_ge(s.turned, TILES // PER_BANK)
            rows = coords[:].rearrange("p t (n c) -> p t n c", c=2)[:, :, :, 0]
            for b in range(TILES // PER_BANK):
                last = dve.tensor_copy(coords[:, b * PER_BANK:(b + 1) * PER_BANK, :],
                                       turned[:, b, 0:PER_BANK * ROWS].rearrange("p (t r) -> p t r", r=ROWS))
            done(last)
            dve.tensor_reduce(reach[:, 0:1], rows, AX.XY, ALU.max)
            done(dve.tensor_reduce(reach[:, 1:2], rows, AX.XY, ALU.min))
            dve.scalar_tensor_tensor(out=reach[:, 2:3], in0=reach[:, 1:2], scalar=-1.0, in1=reach[:, 0:1],
                                     op0=ALU.mult, op1=ALU.max).then_inc(s.reach, 1)
            dve.wait_ge(s.reach_ps, 1)
            done(dve.tensor_reduce(most[:, 0:1], ps[0:1, 0, 0:P], AX.X, ALU.max))
            done(dve.tensor_scalar(most[:, 1:2], most[:, 0:1], float(REACH), None, ALU.is_ge))
            dve.tensor_copy(flag[:, 0:1], most[:, 1:2])


def sample(k, name, s, blocks, w_deform, coords, base, ints, sums, flag):
    nc, xn = k.nc, k.xn
    items = [(ty, h, q0, q1) for ty in range(QTILES) for h in range(HALVES) for q0, q1 in blocks[ty]]
    first = [i == 0 or items[i - 1][:2] != it[:2] for i, it in enumerate(items)]
    last_of = [i + 1 == len(items) or items[i + 1][:2] != it[:2] for i, it in enumerate(items)]
    G = TAPS // TAP_GROUP
    ITEMS, STEPS, SUMS, VALUES = len(items), len(items) * G, HALVES * QTILES, XTILES * G
    VCOLS = TAP_GROUP * C
    RMAX = max(q1 - q0 + 1 for _, _, q0, q1 in items) * TILE_ROWS
    EDGE = REACH + 1
    assert ITEMS % 2 == 0 and STEPS % 2 == 0
    with ExitStack() as ctx:
        def sb(nm, shape, dt=F32):
            return ctx.enter_context(nc.sbuf_tensor(f"c3_{name}_{nm}", shape, dt))
        staged = sb("staged", [P, (EDGE + H + EDGE) * W])
        position = sb("position", [P, QTILES, 4 * TAPS])
        values = sb("values", [P, XTILES, G, HALVES * VCOLS])
        dist = sb("dist", [P, 2, TAPS, W + RMAX])
        hats = sb("hats", [P, 2, TAPS, W + RMAX])
        weights = sb("weights", [P, 2, TAP_GROUP, RMAX * W])
        matrix = sb("matrix", [P, 2, TAP_GROUP, RMAX * W])
        turned = ctx.enter_context(nc.psum_tensor(f"c3_{name}_turned", [P, 2, TAP_GROUP, BANK], F32))
        sum_ps = ctx.enter_context(nc.psum_tensor(f"c3_{name}_sum_ps", [P, 2, BANK], F32))
        block = ctx.enter_context(nc.Block())

        def run(eng, body):
            def loop():
                with eng.Fori(0, IMAGES, 1) as j:
                    body(j)
            if flag is None:
                loop()
            else:
                beyond = eng.value_load(flag[0:1, 0:1], min_val=0, max_val=1)
                with eng.If(beyond > 0):
                    loop()

        @block.tensor
        def _(pe):
            def values_of(j):
                pe.wait_ge(s.staged, 1 + j + 1)
                pe.wait_ge(s.summed, 1 + j * SUMS)
                for v in range(VALUES):
                    q, g = v // G, v % G
                    pe.wait_ge(s.values, 1 + j * VALUES + max(v - 1, 0))
                    pe.matmul(sum_ps[:, v % 2, 0:HALVES * VCOLS], staged[:, q * P + g * W:(q + 1) * P + g * W],
                              w_deform[:, g, :],
                              start=True, stop=True).then_inc(s.values_ps, 1)

            def turn(j, n):
                q0, q1 = items[n // G][2:]
                pe.wait_ge(s.weights, 1 + j * STEPS + n + 1)
                pe.wait_ge(s.matrix, 1 + j * STEPS + max(n - 1, 0))
                for t in range(TAP_GROUP):
                    for q in range(q1 - q0 + 1):
                        last = pe.transpose(turned[:, n % 2, t, q * P:(q + 1) * P],
                                            weights[:, n % 2, t, q * P:(q + 1) * P], k.identity[:])
                last.then_inc(s.turned, 1)

            def multiply(j, n):
                i, g = n // G, n % G
                ty, h, q0, q1 = items[i]
                pe.wait_ge(s.matrix, 1 + j * STEPS + n + 1)
                tile = ty * HALVES + h
                if g == 0 and first[i]:
                    pe.wait_ge(s.summed, 1 + j * SUMS + max(tile - 1, 0))
                for t in range(TAP_GROUP):
                    for q in range(q1 - q0 + 1):
                        last = pe.matmul(sum_ps[:, tile % 2, 0:C], matrix[:, n % 2, t, q * P:(q + 1) * P],
                                         values[:, q0 + q, g, h * VCOLS + t * C:h * VCOLS + (t + 1) * C],
                                         start=(g == 0 and first[i] and t == 0 and q == 0),
                                         stop=(g == G - 1 and last_of[i] and t == TAP_GROUP - 1 and q == q1 - q0))
                last.then_inc(s.used, 1)

            def body(j):
                values_of(j)
                pe.wait_ge(s.values, 1 + (j + 1) * VALUES)
                for n in range(STEPS):
                    turn(j, n)
                    if n > 0:
                        multiply(j, n - 1)
                multiply(j, STEPS - 1)
            run(pe, body)

        @block.scalar
        def _(act):
            def body(j):
                act.wait_ge(s.used, 1 + j * STEPS)
                for v in range(VALUES):
                    q, g = v // G, v % G
                    act.wait_ge(s.values_ps, 1 + j * VALUES + v + 1)
                    act.copy(values[:, q, g, :], sum_ps[:, v % 2, 0:HALVES * VCOLS]).then_inc(s.values, 1)
                for n in range(STEPS):
                    q0, q1 = items[n // G][2:]
                    width = (q1 - q0 + 1) * P
                    act.wait_ge(s.turned, 1 + j * STEPS + n + 1)
                    act.wait_ge(s.used, 1 + j * STEPS + max(n - 1, 0))
                    act.copy(matrix[:, n % 2, :, 0:width], turned[:, n % 2, :, 0:width]).then_inc(s.matrix, 1)
            run(act, body)

        @block.gpsimd
        def _(pool):
            def body(j):
                pool.wait_ge(s.position, 1 + j + 1)
                for i, (ty, h, q0, q1) in enumerate(items):
                    pool.wait_ge(s.hats, 1 + j * ITEMS + max(i - 1, 0))
                    own = position[:, ty, h * 2 * TAPS:(h + 1) * 2 * TAPS].rearrange("p (t c) -> p t c", c=2)
                    rows = (q1 - q0 + 1) * TILE_ROWS
                    start = H + (q0 - ty) * TILE_ROWS - REACH
                    pool.tensor_tensor(dist[:, i % 2, :, 0:W], spread(own[:, :, 1], 2, W),
                                       spread(ints[:, H:H + W], 1, TAPS), ALU.subtract)
                    pool.tensor_tensor(dist[:, i % 2, :, W:W + rows], spread(own[:, :, 0], 2, rows),
                                       spread(ints[:, start:start + rows], 1, TAPS),
                                       ALU.subtract).then_inc(s.dist, 1)
            run(pool, body)

        @block.vector
        def _(dve):
            def body(j):
                def used(i):
                    q0, q1 = items[i][2:]
                    return W + (q1 - q0 + 1) * TILE_ROWS

                def negate(i):
                    dve.wait_ge(s.dist, 1 + j * ITEMS + i + 1)
                    dve.wait_ge(s.weights, 1 + j * STEPS + G * max(i - 1, 0))
                    own = dist[:, i % 2, :, 0:used(i)]
                    dve.scalar_tensor_tensor(out=hats[:, i % 2, :, 0:used(i)], in0=own, scalar=-1.0, in1=own,
                                             op0=ALU.mult, op1=ALU.min).then_inc(s.hats, 1)

                def hat(i):
                    dve.wait_ge(s.hats, 1 + j * ITEMS + i + 1)
                    dve.tensor_scalar(hats[:, i % 2, :, 0:used(i)], hats[:, i % 2, :, 0:used(i)], 1.0, 0.0,
                                      ALU.add, ALU.max).then_inc(s.hatted, 1)

                def weigh(n):
                    i, g = n // G, n % G
                    rows = used(i) - W
                    own = hats[:, i % 2, g * TAP_GROUP:(g + 1) * TAP_GROUP, :]
                    dve.wait_ge(s.hatted, 1 + j * ITEMS + i + 1)
                    dve.wait_ge(s.turned, 1 + j * STEPS + max(n - 1, 0))
                    dve.tensor_tensor(
                        weights[:, n % 2, :, 0:rows * W].rearrange("p t (r c) -> p t r c", c=W),
                        spread(own[:, :, W:W + rows], 3, W), spread(own[:, :, 0:W], 2, rows),
                        ALU.mult).then_inc(s.weights, 1)

                def keep(i):
                    ty, h = items[i][:2]
                    dve.wait_ge(s.used, 1 + j * STEPS + (i + 1) * G)
                    place = sums[:, bass.ds(j * QTILES + ty, 1), h, :].rearrange("p o c -> p (o c)")
                    source = sum_ps[:, (ty * HALVES + h) % 2, 0:C]
                    if flag is None:
                        dve.tensor_scalar(place, source, 1.0, None, ALU.mult).then_inc(s.summed, 1)
                    else:
                        dve.tensor_tensor(place, place, source, ALU.add).then_inc(s.summed, 1)

                dve.wait_ge(s.values_ps, 1 + j * VALUES)
                dve.tensor_scalar(staged[:, EDGE * W:(EDGE + H) * W], xn[:, bass.ds(j * PIX, PIX)], 1.0, None,
                                  ALU.mult).then_inc(s.staged, 1)
                dve.wait_ge(s.dist, 1 + j * ITEMS)
                dve.tensor_tensor(position[:], coords[:, bass.ds(j * QTILES, QTILES), :],
                                  spread(base[:], 1, QTILES), ALU.add).then_inc(s.position, 1)
                negate(0)
                hat(0)
                for i in range(ITEMS):
                    if i + 1 < ITEMS:
                        negate(i + 1)
                    weigh(G * i)
                    if i + 1 < ITEMS:
                        hat(i + 1)
                    weigh(G * i + 1)
                    if i > 0 and last_of[i - 1]:
                        keep(i - 1)
                    weigh(G * i + 2)
                keep(ITEMS - 1)
            for edge in (slice(0, EDGE * W), slice((EDGE + H) * W, (EDGE + H + EDGE) * W)):
                dve.memset(staged[:, edge], 0.0)
            run(dve, body)


def group_norm(k, sums, pairs, gamma, beta):
    nc, x, s = k.nc, k.x, k.c3
    STATS = PIX // BANK
    with ExitStack() as ctx:
        def sb(name, shape):
            return ctx.enter_context(nc.sbuf_tensor("gn_" + name, shape, F32))
        y = sb("y", [P, N])
        stats, own = sb("stats", [P, IMAGES * STATS, 6]), sb("own", [P, IMAGES, 4])
        group = sb("group", [P, 7, IMAGES])
        ps = ctx.enter_context(nc.psum_tensor("gn_ps", [P, 2, BANK], F32))
        mean_ps = ctx.enter_context(nc.psum_tensor("gn_mean_ps", [P, IMAGES, 2], F32))
        block = ctx.enter_context(nc.Block())

        @block.tensor
        def _(pe):
            for g in range(N // BANK):
                if g >= 2:
                    pe.wait_ge(s.y, g - 1)
                for t in range(BANK // P):
                    last = pe.transpose(ps[:, g % 2, t * P:(t + 1) * P],
                                        sums[:, g * (BANK // P) + t].rearrange("p h c -> p (h c)"), k.identity[:])
                last.then_inc(s.y_ps, 1)
            pe.wait_ge(s.own, 1)
            pe.matmul(mean_ps[:], pairs[:], own[:, :, 0:2], start=True, stop=True).then_inc(s.group, 1)

        @block.scalar
        def _(act):
            for g in range(N // BANK):
                act.wait_ge(s.y_ps, g + 1)
                act.copy(y[:, g * BANK:(g + 1) * BANK], ps[:, g % 2, :]).then_inc(s.y, 1)
            act.wait_ge(s.neg_var, 1)
            act.activation(group[:, 3], group[:, 2], ACT.Sqrt, bias=k.eps[1e-5][:], scale=-1.0).then_inc(s.dev, 1)
            act.wait_ge(s.affine, 1)
            for j in range(IMAGES):
                act.activation(y[:, j * PIX:(j + 1) * PIX], y[:, j * PIX:(j + 1) * PIX], ACT.Relu,
                               bias=group[:, 6, j:j + 1], scale=group[:, 5, j:j + 1]).then_inc(s.relu, 1)

        @block.vector
        def _(dve):
            step = [k.c3_steps]

            def done(ins):
                step[0] += 1
                ins.then_inc(s.gn_step, 1)
                dve.wait_ge(s.gn_step, step[0])

            for g in range(N // BANK):
                dve.wait_ge(s.y, g + 1)
                last = dve.bn_stats(stats[:, g, :], y[:, g * BANK:(g + 1) * BANK])
            done(last)
            for j in range(IMAGES):
                last = dve.bn_aggr(own[:, j, 2:4], stats[:, j * STATS:(j + 1) * STATS, :])
            done(last)
            dve.tensor_copy(own[:, :, 0], own[:, :, 2])
            done(dve.tensor_tensor(own[:, :, 1], own[:, :, 2], own[:, :, 2], ALU.mult))
            dve.tensor_tensor(own[:, :, 1], own[:, :, 1], own[:, :, 3], ALU.add).then_inc(s.own, 1)
            dve.wait_ge(s.group, 1)
            done(dve.tensor_copy(group[:, 0:2], mean_ps[:].rearrange("p j c -> p c j")))
            done(dve.tensor_tensor(group[:, 3], group[:, 0], group[:, 0], ALU.mult))
            dve.tensor_tensor(group[:, 2], group[:, 3], group[:, 1], ALU.subtract).then_inc(s.neg_var, 1)
            dve.wait_ge(s.dev, 1)
            done(dve.reciprocal(group[:, 4], group[:, 3]))
            done(dve.tensor_scalar(group[:, 5], group[:, 4], gamma, None, ALU.mult))
            done(dve.tensor_tensor(group[:, 4], group[:, 0], group[:, 5], ALU.mult))
            dve.tensor_scalar(group[:, 6], group[:, 4], -1.0, beta, ALU.mult, ALU.add).then_inc(s.affine, 1)
            for j in range(IMAGES):
                dve.wait_ge(s.relu, j + 1)
                place = x[:, j * PIX:(j + 1) * PIX]
                dve.tensor_tensor(place, place, y[:, j * PIX:(j + 1) * PIX], ALU.add)



def load_image(k, sp, j):
    for h in range(HALVES):
        sp.dma_start(k.x[h * C:(h + 1) * C, j * PIX:(j + 1) * PIX],
                     k.ins["x"][h * IMAGES + j]).then_inc(k.image_loaded[j], 16)


def load_first(k):
    nc = k.nc
    with ExitStack() as ctx:
        block = ctx.enter_context(nc.Block())

        @block.sync
        def _(sp):
            sp.dma_start(k.centring[:], k.ins["centring"]).then_inc(k.constants, 16)
            load_image(k, sp, 0)
            for to, name in ((k.shifted, "shifted"), (k.rows, "rows")):
                sp.dma_start(to[:], k.ins[name]).then_inc(k.constants, 16)
            k.constants_all = 16 * 3

        @block.vector
        def _(dve):
            for eps, place in k.eps.items():
                dve.memset(place[:], eps)


def store_image(k, sp, j):
    for h in range(HALVES):
        sp.dma_start(k.out[h * IMAGES + j], k.x[h * C:(h + 1) * C, j * PIX:(j + 1) * PIX]).then_inc(k.stored, 16)


def layer_loads(k, copies, rows):
    k.fetched += 16 * (len(copies) + len(rows))
    loads = [(to[:], k.ins[name], k.fetched_sem) for to, name in copies]
    loads += [(to[:], k.ins[name].partition_broadcast(P), k.fetched_sem) for to, name in rows]
    return loads + pending_loads(k)


def pending_loads(k):
    loads, k.loads = k.loads, []
    return loads


def mixture_loads(k, layer):
    w, ins = k.w, k.ins
    swiglu = layer in (0, 3)
    m = SWIGLU if swiglu else GELU
    E = m.experts
    w.first = w.first_room[:, 0:2 * P * E]
    w.router = w.router_room[:, 0:HALVES * E]
    w.router_bias = w.router_bias_room[:, 0:E]
    copies = [(w.first[0:C], ins[f"f{layer}_first"]), (w.first[C:P], ins[f"f{layer}_first"]),
              (w.second[:], ins[f"f{layer}_second"]), (w.router, ins[f"f{layer}_router"]),
              (w.router_bias, ins[f"f{layer}_router_bias"].partition_broadcast(P))]
    if not swiglu:
        copies += [(w.bias1[:], ins[f"f{layer}_bias1"]),
                   (w.bias2[:], ins[f"f{layer}_bias2"])]
    w.all += 16 * len(copies)
    return [(to, source, w.loaded) for to, source in copies]


def ffn(k, layer, turn, last_layer):
    nc, w = k.nc, k.w
    swiglu = layer in (0, 3)
    m = SWIGLU if swiglu else GELU
    with ExitStack() as ctx:
        k.parts = ctx.enter_context(nc.sbuf_tensor(f"parts{layer}", [P, HALVES, N], F32R))
        w.high = ctx.enter_context(nc.sbuf_tensor(f"high{layer}", [P, 2 * P * m.experts], F32R))
        w.low = ctx.enter_context(nc.sbuf_tensor(f"low{layer}", [P, 2 * P * m.experts], F32R))
        tiles = m.experts * m.hidden // P
        w.second_parts = ctx.enter_context(nc.sbuf_tensor(f"second_parts{layer}", [P, tiles, 2 * C], F32R))
        w.bias2_parts = None if swiglu else ctx.enter_context(
            nc.sbuf_tensor(f"bias2_parts{layer}", [GATE_ROWS, 2 * C], F32R))
        top_two = TopTwo(k, ctx, m)
        layer_norm(k, turn, 1e-5, pending_loads(k), router=(top_two, w))
        mixture(k, k.mixtures, m, w, swiglu, top_two, last_layer)
        k.mixtures += 1


class Network:
    pass


class Weights:
    pass



class LayerNormSignals:
    def __init__(self, new):
        self.mean = new("ln_mean")
        self.centred = new("ln_centred")
        self.squared = new("ln_squared")
        self.var = new("ln_var")
        self.dev = new("ln_dev")
        self.scale = new("ln_scale")
        self.wide = new("ln_wide")
        self.normed = new("ln_normed")


class GateSignals:
    def __init__(self, new):
        self.logits = new("gt_logits")
        self.high = new("gt_high")
        self.first_high = new("gt_first_high")
        self.w_high = new("gt_w_high")
        self.gap = new("gt_gap")
        self.exp = new("gt_exp")
        self.step = new("gt_step")


class MixtureSignals:
    def __init__(self, new):
        self.cleared = new("mx_cleared")
        self.own_gates = new("mx_own_gates")
        self.gates_turned = new("mx_gates_turned")
        self.gate_high = new("mx_gate_high")
        self.gate_low = new("mx_gate_low")
        self.first = new("mx_first")
        self.spread = new("mx_spread")
        self.act = new("mx_act")
        self.gated = new("mx_gated")
        self.hidden = new("mx_hidden")
        self.high = new("mx_high")
        self.high_rest = new("mx_high_rest")
        self.low = new("mx_low")
        self.low_rest = new("mx_low_rest")
        self.second = new("mx_second")
        self.added_high = new("mx_added_high")
        self.added = new("mx_added")


class BatchNormSignals:
    def __init__(self, new):
        self.stats = new("bn_stats")
        self.own = new("bn_own")
        self.both = new("bn_both")
        self.neg_var = new("bn_neg_var")
        self.dev = new("bn_dev")
        self.step = new("bn_step")


class Conv0Signals:
    def __init__(self, new):
        self.key_ps = new("c0_key_ps")
        self.key = new("c0_key")
        self.key_max = new("c0_key_max")
        self.key_exp = new("c0_key_exp")
        self.qv_ps = new("c0_qv_ps")
        self.qv = new("c0_qv")
        self.q_max = new("c0_q_max")
        self.q_shift = new("c0_q_shift")
        self.q_exp = new("c0_q_exp")
        self.q_soft = new("c0_q_soft")
        self.turned_ps = new("c0_turned_ps")
        self.turned = new("c0_turned")
        self.small_ps = new("c0_small_ps")
        self.small = new("c0_small")
        self.sigmoid = new("c0_sigmoid")
        self.gate_exp = new("c0_gate_exp")
        self.out_ps = new("c0_out_ps")
        self.added = new("c0_added")
        self.step = new("c0_step")


class Conv1Signals:
    def __init__(self, new):
        self.cleared = new("c1_cleared")
        self.padded = new("c1_padded")
        self.small_ps = new("c1_small_ps")
        self.squeezed = new("c1_squeezed")
        self.logit = new("c1_logit")
        self.routing = new("c1_routing")
        self.total = new("c1_total")
        self.kernel = new("c1_kernel")
        self.out_ps = new("c1_out_ps")
        self.added = new("c1_added")
        self.step = new("c1_step")


class Conv2Signals:
    def __init__(self, new):
        self.cleared = new("c2_cleared")
        self.f_ps = new("c2_f_ps")
        self.f = new("c2_f")
        self.total = new("c2_total")
        self.g_ps = new("c2_g_ps")
        self.g = new("c2_g")
        self.taps = new("c2_taps")
        self.product = new("c2_product")
        self.far = new("c2_far")
        self.near = new("c2_near")
        self.out_ps = new("c2_out_ps")
        self.added = new("c2_added")
        self.step = new("c2_step")


class Conv3Signals:
    def __init__(self, new):
        self.cleared = new("c3_cleared")
        self.padded = new("c3_padded")
        self.filled = new("c3_filled")
        self.w_high = new("c3_w_high")
        self.w_low = new("c3_w_low")
        self.high = new("c3_high")
        self.off_high = new("c3_off_high")
        self.off_ps = new("c3_off_ps")
        self.off = new("c3_off")
        self.turned = new("c3_turned")
        self.reach = new("c3_reach")
        self.reach_ps = new("c3_reach_ps")
        self.step = new("c3_step")
        self.y_ps = new("c3_y_ps")
        self.y = new("c3_y")
        self.own = new("c3_own")
        self.group = new("c3_group")
        self.neg_var = new("c3_neg_var")
        self.dev = new("c3_dev")
        self.affine = new("c3_affine")
        self.relu = new("c3_relu")
        self.gn_step = new("c3_gn_step")


class SampleSignals:
    def __init__(self, new, name):
        self.staged = new(f"{name}_staged")
        self.position = new(f"{name}_position")
        self.values_ps = new(f"{name}_values_ps")
        self.values = new(f"{name}_values")
        self.dist = new(f"{name}_dist")
        self.hats = new(f"{name}_hats")
        self.hatted = new(f"{name}_hatted")
        self.weights = new(f"{name}_weights")
        self.turned = new(f"{name}_turned")
        self.matrix = new(f"{name}_matrix")
        self.used = new(f"{name}_used")
        self.summed = new(f"{name}_summed")
        self.all = [self.staged, self.position, self.values_ps, self.values, self.dist, self.hats, self.hatted,
                    self.weights, self.turned, self.matrix, self.used, self.summed]


def build(nc, ins, out, plan):
    with ExitStack() as ctx:
        def sb(name, shape, dt=F32):
            return ctx.enter_context(nc.sbuf_tensor(name, shape, dt))

        def new(name):
            return ctx.enter_context(nc.semaphore(name))

        k = Network()
        k.nc, k.ins, k.out = nc, ins, out
        k.x = sb("x", [P, N])
        k.xn = sb("xn", [P, N])
        k.gate = sb("gate", [P, (HALVES * TILES + SLOTS) * SWIGLU.experts])
        k.selection = sb("selection", [GATE_ROWS, SWIGLU.experts * P], F32R)
        k.centring = sb("centring", [P, P])
        k.identity = sb("identity", [P, P])
        k.shifted = sb("shifted", [P, 2 * HALVES * LN_TILES])
        k.rows = sb("rows", [HALVES * LN_TILES, LN_TILES * P])
        k.countdown = sb("countdown", [P, SWIGLU.experts])
        k.eps = {e: sb(f"eps{i}", [P, 1]) for i, e in enumerate((1e-5, 1e-6))}
        k.constants, k.more_constants = new("constants"), new("more_constants")
        k.image_loaded = [new(f"image{j}_loaded") for j in range(IMAGES)]
        k.stored = ctx.enter_context(nc.semaphore("stored"))
        k.ln = LayerNormSignals(new)
        k.gt = GateSignals(new)
        k.mx = MixtureSignals(new)
        k.mx_base = dict(expert=0, gelu=0, swiglu=0, tile=0, step=0, picked=0)
        k.w = Weights()
        k.w.first_room = sb("w_first", [P, 2 * P * SWIGLU.experts])
        k.w.second = sb("w_second", [P, C * SWIGLU.experts])
        k.w.router_room = sb("w_router", [P, HALVES * SWIGLU.experts])
        k.w.router_bias_room = sb("w_router_bias", [P, SWIGLU.experts])
        k.w.bias1 = sb("w_bias1", [P, 2 * GELU.experts])
        k.w.bias2 = sb("w_bias2", [GATE_ROWS, C])
        k.w.loaded = ctx.enter_context(nc.semaphore("w_loaded"))
        k.w.all = 0
        k.mixtures = 0
        k.fetched_sem = ctx.enter_context(nc.semaphore("fetched"))
        k.fetched = 0
        k.bn = BatchNormSignals(new)
        k.c0 = Conv0Signals(new)
        k.c1 = Conv1Signals(new)
        k.c2 = Conv2Signals(new)
        k.c3 = Conv3Signals(new)
        k.c3_steps = 0
        k.c3_near, k.c3_rest = SampleSignals(new, "near"), SampleSignals(new, "rest")
        load_first(k)
        k.loads = [(k.identity[:], ins["identity"], k.more_constants),
                   (k.countdown[:], ins["countdown"], k.more_constants)]
        turn = 0
        ready = None
        for place, (what, layer) in enumerate(plan):
            if layer != ready:
                k.loads += mixture_loads(k, layer)
                ready = layer
            if what == "ffn":
                ffn(k, layer, turn, last_layer=(place == len(plan) - 1))
                turn += 1
            else:
                turn = what(k, layer, turn)


def lay_out(inputs):
    f = lambda n: np.ascontiguousarray(inputs[n])
    stack = lambda a: np.concatenate([a, a], axis=0)

    def diagonal(a):
        z = np.zeros_like(a)
        return np.concatenate([np.concatenate([a, z], axis=1), np.concatenate([z, a], axis=1)])

    c = {
        "x": f("x").reshape(B, C, PIX),
        "average": diagonal(np.full((C, C), 1.0 / C, np.float32)),
        "centring": diagonal(np.eye(C, dtype=np.float32) - np.float32(1.0 / C)),
        "identity": np.eye(P, dtype=np.float32),
        "rows": np.repeat(np.eye(HALVES * LN_TILES, dtype=np.float32), C, axis=1),
        "shifted": np.concatenate([np.zeros((P, 2 * LN_TILES - 2)), diagonal(np.full((C, 1), 1.0 / C)),
                                   np.zeros((P, 2 * LN_TILES))], axis=1).astype(np.float32),
        "countdown": np.broadcast_to(np.arange(SWIGLU.experts, 0, -1, dtype=np.float32), (P, SWIGLU.experts)),
    }
    p = "L0_conv_"
    c["c0_wk"] = diagonal(f(p + "wk").T)
    c["c0_wqv"] = np.concatenate([diagonal(f(p + "wq").T), diagonal(f(p + "wv").T)], axis=1)
    c["c0_bqv"] = np.concatenate([f(p + "bq"), f(p + "bq"), f(p + "bv"), f(p + "bv")])
    c["c0_cols"] = np.stack([stack(f(p + n)) for n in ("bn_gamma", "bn_beta", "bk", "b_rep")]
                            + [np.broadcast_to(f(p + "b_se"), (P,))], axis=1)
    c["c0_wrep"] = f(p + "w_rep").T.reshape(HEADS, HK, C).transpose(1, 0, 2).reshape(HK, HEADS * C)
    c["c0_fc"] = np.concatenate([f(p + n).reshape(-1) for n in
                                 ("w_fc1", "b_fc1", "w_fc2", "b_fc2", "w_se")]).reshape(1, 14)
    c["halves"] = np.tile(np.eye(C, dtype=np.float32) / HALVES, (HALVES, HALVES))
    c["quads"] = np.repeat(np.eye(HALVES * HEADS, dtype=np.float32), HK, axis=0) / (HK * HK)
    c["heads"] = diagonal(np.tile(np.eye(HK, dtype=np.float32), (HEADS, HEADS)))
    p = "L1_conv_"
    c["c1_w1"] = diagonal(f(p + "w1").T)
    c["c1_w2"] = diagonal(f(p + "w2").T)
    c["c1_wexp"] = f(p + "w_exp").reshape(-1)
    weight = f(p + "weight")
    c["c1_weight"] = stack(weight.transpose(2, 0, 3, 4, 1).reshape(C, weight.shape[0], 9 * C))
    p = "L2_conv_conv_"
    c["c2_w"] = diagonal(f(p + "w").T)
    c["c2_row"] = np.concatenate([f(p + n).reshape(-1) for n in (
        "kernel_w", "kernel_b", "kernel2_w", "kernel2_b", "k_w", "k_b", "k2_w", "k2_b")])
    p = "L2_conv_"
    c["c2_cols"] = np.stack([np.tile(f(p + n), B) for n in ("conv_b", "adap_b", "atrous_b")]
                            + [np.tile(f(p + "fuse_b"), 2 * HALVES)], axis=1)
    fw = f(p + "fuse_w").T
    near, far = np.concatenate([fw, np.zeros_like(fw)], axis=1), np.concatenate([np.zeros_like(fw), fw], axis=1)
    c["c2_fuse"] = np.stack([np.tile(diagonal(a), (IMAGES, 1)) for a in (near, far)], axis=1)
    p = "L3_conv_"
    off_w = f(p + "offset_w").reshape(2 * TAPS, C, TAPS).transpose(2, 1, 0)
    c["c3_w_off"] = np.stack([diagonal(a) for a in off_w], axis=1)
    off_b = f(p + "offset_b")
    c["c3_cols"] = np.stack([np.concatenate([off_b, off_b, np.zeros(P - 4 * TAPS, np.float32)]),
                             stack(f(p + "gn_gamma")), stack(f(p + "gn_beta"))], axis=1)
    deform = f(p + "deform_w").reshape(C, C, TAPS // TAP_GROUP, TAP_GROUP).transpose(2, 1, 3, 0)
    c["c3_w_deform"] = np.stack([diagonal(a.reshape(C, TAP_GROUP * C)) for a in deform], axis=1)
    at = np.arange(P)
    tap = np.arange(TAPS)
    base = np.stack([(at // W)[:, None] + 0 * tap[None], (at % W)[:, None] - 1 + (tap % 3)[None]], axis=2)
    c["c3_base"] = np.tile(base.reshape(P, 2 * TAPS), (1, HALVES)).astype(np.float32)
    c["c3_ints"] = np.arange(-H, H + TILE_ROWS, dtype=np.float32)
    c["pairs"] = np.kron(np.eye(P // 2), np.full((2, 2), 0.5)).astype(np.float32)
    for layer in (0, 3):
        p = f"L{layer}_ffn_"
        E = SWIGLU.experts
        first = np.stack([f(p + "w1"), f(p + "w2")], axis=1)
        c[f"f{layer}_first"] = first.transpose(2, 0, 1, 3).reshape(C, E * 2 * P)
        c[f"f{layer}_second"] = f(p + "w3").transpose(1, 0, 2).reshape(P, E * C)
        c[f"f{layer}_router"] = diagonal(f(p + "gate_w"))
        c[f"f{layer}_router_bias"] = f(p + "gate_b")
    for layer in (1, 2):
        p = f"L{layer}_ffn_"
        E = GELU.experts
        c[f"f{layer}_first"] = f(p + "W1").transpose(1, 0, 2).reshape(C, E * 2 * P)
        c[f"f{layer}_second"] = f(p + "W2").reshape(E, 2, P, C).transpose(2, 0, 1, 3).reshape(P, E * 2 * C)
        c[f"f{layer}_router"] = diagonal(f(p + "Wg"))
        c[f"f{layer}_router_bias"] = f(p + "bg")
        c[f"f{layer}_bias1"] = f(p + "b1").reshape(E, 2, P).transpose(2, 0, 1).reshape(P, E * 2)
        bias2 = np.zeros((GATE_ROWS, C), np.float32)
        bias2[0:E] = bias2[LOW_GATES:LOW_GATES + E] = f(p + "b2")
        c[f"f{layer}_bias2"] = bias2
    return {n: np.ascontiguousarray(a) for n, a in c.items()}



PLAN = [(conv0, 0), ("ffn", 0), (conv1, 1), ("ffn", 1), (conv2, 2), ("ffn", 2), (conv3, 3), ("ffn", 3)]


def kernel(**inputs):
    import concourse.bacc as bacc
    from concourse.bass_utils import run_bass_kernel_spmd

    arrays = lay_out(inputs)
    nc = bacc.Bacc("TRN2", target_bir_lowering=False, num_devices=1)
    ins = {name: nc.dram_tensor(f"in_{name}", a.shape, mybir.dt.from_np(a.dtype), kind="ExternalInput").ap()
           for name, a in arrays.items()}
    out = nc.dram_tensor("out_x", (B, C, PIX), F32, kind="ExternalOutput").ap()
    build(nc, ins, out, PLAN)
    result = run_bass_kernel_spmd(nc, [{f"in_{name}": a for name, a in arrays.items()}], core_ids=[0])
    return result.results[0]["out_x"].reshape(B, C, H, W)
```
